# Optimizing a Trainium2 kernel written in Bass

```python
import numpy as np
import jax
import jax.numpy as jnp

def _softmax(x, axis=-1):
    return jax.nn.softmax(x, axis=axis)

def _gelu(x):
    return jax.nn.gelu(x, approximate=True)

def _silu(x):
    return jax.nn.silu(x)

def _sigmoid(x):
    return jax.nn.sigmoid(x)

def _layernorm(x, axis=-1, eps=1e-05):
    m = jnp.mean(x, axis=axis, keepdims=True)
    v = jnp.var(x, axis=axis, keepdims=True)
    return (x - m) / jnp.sqrt(v + eps)

def _scatter_add(tgt, idx, src, axis=0):
    return tgt.at[idx].add(src)

def _segment_sum(src, seg, n):
    return jax.ops.segment_sum(src, seg, n)
kernel_name = 'mk_hybrid_d1_jaxref_r4_287aab'

def setup_inputs(seed: int=0):
    np.random.seed(seed)
    _w = jnp.asarray

    def _L0_attn_a_setup():
        import jax, jax.numpy as jnp
        import numpy as np
        N_HEAD = 16
        key = jax.random.key(seed)
        ks = jax.random.split(key, 10)
        C = 256
        B, T = (4, 2048)
        s = 1.0 / np.sqrt(C)
        return {'x': jax.random.normal(ks[0], (B, T, C), dtype=jnp.float32), 'Wq': jax.random.normal(ks[1], (C, C), dtype=jnp.float32) * s, 'bq': jax.random.normal(ks[2], (C,), dtype=jnp.float32) * s, 'Wk': jax.random.normal(ks[3], (C, C), dtype=jnp.float32) * s, 'bk': jax.random.normal(ks[4], (C,), dtype=jnp.float32) * s, 'Wv': jax.random.normal(ks[5], (C, C), dtype=jnp.float32) * s, 'bv': jax.random.normal(ks[6], (C,), dtype=jnp.float32) * s, 'Wp': jax.random.normal(ks[7], (C, C), dtype=jnp.float32) * s, 'bp': jax.random.normal(ks[8], (C,), dtype=jnp.float32) * s}
    _L0_attn_a_in = _L0_attn_a_setup()

    def _L0_attn_b_setup():
        import math
        import jax, jax.numpy as jnp
        import numpy as np
        SEQ, BATCH, D_MODEL, NHEAD, FEAT = (512, 2, 256, 8, 128)

        def _sinusoid_pe(length, d_model, dtype):
            pos = jnp.arange(length, dtype=dtype)[:, None]
            div = jnp.exp(jnp.arange(0, d_model, 2, dtype=dtype) * (-math.log(10000.0) / d_model))
            ang = pos * div
            return jnp.stack([jnp.sin(ang), jnp.cos(ang)], axis=-1).reshape(length, d_model)

        def _left_shift(x):
            I, J, B, N = x.shape
            zero = jnp.zeros((I, 1, B, N), x.dtype)
            padded = jnp.concatenate([zero, x], axis=1)
            padded = padded.reshape(J + 1, I, B, N)[1:]
            x = padded.reshape(I, J, B, N)
            return jnp.tril(x)
        key = jax.random.key(seed)
        ks = jax.random.split(key, 8)
        s = 0.02
        return {'x': jax.random.normal(ks[0], (SEQ, BATCH, D_MODEL), dtype=jnp.float32), 'gamma': jnp.ones((D_MODEL,), jnp.float32), 'beta': jnp.zeros((D_MODEL,), jnp.float32), 'Wq': jax.random.normal(ks[1], (D_MODEL, NHEAD * FEAT), jnp.float32) * s, 'Wv': jax.random.normal(ks[2], (D_MODEL, NHEAD * FEAT), jnp.float32) * s, 'Wr': jax.random.normal(ks[3], (D_MODEL, NHEAD * FEAT), jnp.float32) * s, 'u_bias': jax.random.normal(ks[4], (NHEAD, FEAT), jnp.float32) * s, 'v_bias': jax.random.normal(ks[5], (NHEAD, FEAT), jnp.float32) * s, 'Wout': jax.random.normal(ks[6], (NHEAD * FEAT, D_MODEL), jnp.float32) * s, 'bout': jnp.zeros((D_MODEL,), jnp.float32)}
    _L0_attn_b_in = _L0_attn_b_setup()

    def _L0_ffn_setup():
        import jax, jax.numpy as jnp
        import numpy as np
        D = 256
        H = 16
        DH = D // H
        DC = D // 4
        HID = 512
        G = 2
        EPG = 4
        E = G * EPG
        TOPK = 2
        EPS = 1e-06
        B, T = (2, 512)

        def _rope_sincos(t, dh):
            inv_freq = 1.0 / 10000.0 ** (jnp.arange(0, dh, 2, dtype=jnp.float32) / dh)
            ang = jnp.arange(t, dtype=jnp.float32)[:, None] * inv_freq[None, :]
            return (jnp.sin(ang), jnp.cos(ang))

        def _apply_rope(x, sin, cos):
            x1 = x[..., ::2]
            x2 = x[..., 1::2]
            r = jnp.stack([x1 * cos - x2 * sin, x1 * sin + x2 * cos], axis=-1)
            return r.reshape(x.shape)

        def _swiglu(x):
            a, b = jnp.split(x, 2, axis=-1)
            return jax.nn.silu(a) * b

        def _rmsnorm(x, w):
            return x * jax.lax.rsqrt(jnp.mean(x * x, axis=-1, keepdims=True) + EPS) * w
        key = jax.random.key(seed)
        ks = jax.random.split(key, 14)
        s = 0.02
        return {'src': jax.random.normal(ks[0], (B, T, D), jnp.float32), 'Wq': jax.random.normal(ks[1], (D, D), jnp.float32) * s, 'Wk_c': jax.random.normal(ks[2], (D, DC), jnp.float32) * s, 'Wv_c': jax.random.normal(ks[3], (D, DC), jnp.float32) * s, 'Wk': jax.random.normal(ks[4], (DC, D), jnp.float32) * s, 'Wv': jax.random.normal(ks[5], (DC, D), jnp.float32) * s, 'Wo': jax.random.normal(ks[6], (D, D), jnp.float32) * s, 'W_shared_in': jax.random.normal(ks[7], (D, 2 * HID), jnp.float32) * s, 'W_shared_out': jax.random.normal(ks[8], (HID, D), jnp.float32) * s, 'W1_shared': jax.random.normal(ks[9], (D, 2 * HID), jnp.float32) * s, 'W2_experts': jax.random.normal(ks[10], (E, HID, D), jnp.float32) * s, 'Wg_gate': jax.random.normal(ks[11], (D, G), jnp.float32) * s, 'We_gate': jax.random.normal(ks[12], (D, E), jnp.float32) * s, 'group_bias': jnp.zeros((G,), jnp.float32), 'expert_bias': jnp.zeros((E,), jnp.float32), 'norm1_w': jnp.ones((D,), jnp.float32), 'norm2_w': jnp.ones((D,), jnp.float32)}
    _L0_ffn_in = _L0_ffn_setup()
    _d = {'L0_attn_a_x': _L0_attn_a_in['x'], 'L0_attn_a_Wq': _L0_attn_a_in['Wq'], 'L0_attn_a_bq': _L0_attn_a_in['bq'], 'L0_attn_a_Wk': _L0_attn_a_in['Wk'], 'L0_attn_a_bk': _L0_attn_a_in['bk'], 'L0_attn_a_Wv': _L0_attn_a_in['Wv'], 'L0_attn_a_bv': _L0_attn_a_in['bv'], 'L0_attn_a_Wp': _L0_attn_a_in['Wp'], 'L0_attn_a_bp': _L0_attn_a_in['bp'], 'L0_attn_b_gamma': _L0_attn_b_in['gamma'], 'L0_attn_b_beta': _L0_attn_b_in['beta'], 'L0_attn_b_Wq': _L0_attn_b_in['Wq'], 'L0_attn_b_Wv': _L0_attn_b_in['Wv'], 'L0_attn_b_Wr': _L0_attn_b_in['Wr'], 'L0_attn_b_u_bias': _L0_attn_b_in['u_bias'], 'L0_attn_b_v_bias': _L0_attn_b_in['v_bias'], 'L0_attn_b_Wout': _L0_attn_b_in['Wout'], 'L0_attn_b_bout': _L0_attn_b_in['bout'], 'L0_ffn_Wq': _L0_ffn_in['Wq'], 'L0_ffn_Wk_c': _L0_ffn_in['Wk_c'], 'L0_ffn_Wv_c': _L0_ffn_in['Wv_c'], 'L0_ffn_Wk': _L0_ffn_in['Wk'], 'L0_ffn_Wv': _L0_ffn_in['Wv'], 'L0_ffn_Wo': _L0_ffn_in['Wo'], 'L0_ffn_W_shared_in': _L0_ffn_in['W_shared_in'], 'L0_ffn_W_shared_out': _L0_ffn_in['W_shared_out'], 'L0_ffn_W1_shared': _L0_ffn_in['W1_shared'], 'L0_ffn_W2_experts': _L0_ffn_in['W2_experts'], 'L0_ffn_Wg_gate': _L0_ffn_in['Wg_gate'], 'L0_ffn_We_gate': _L0_ffn_in['We_gate'], 'L0_ffn_group_bias': _L0_ffn_in['group_bias'], 'L0_ffn_expert_bias': _L0_ffn_in['expert_bias'], 'L0_ffn_norm1_w': _L0_ffn_in['norm1_w'], 'L0_ffn_norm2_w': _L0_ffn_in['norm2_w']}
    _x0 = _d['L0_attn_a_x']
    _d['L0_attn_a_x'] = jax.random.normal(jax.random.fold_in(jax.random.key(seed), 1), (4, 1024, 256), dtype=_x0.dtype)
    del _x0
    return _d

def reference(L0_attn_a_x, L0_attn_a_Wq, L0_attn_a_bq, L0_attn_a_Wk, L0_attn_a_bk, L0_attn_a_Wv, L0_attn_a_bv, L0_attn_a_Wp, L0_attn_a_bp, L0_attn_b_gamma, L0_attn_b_beta, L0_attn_b_Wq, L0_attn_b_Wv, L0_attn_b_Wr, L0_attn_b_u_bias, L0_attn_b_v_bias, L0_attn_b_Wout, L0_attn_b_bout, L0_ffn_Wq, L0_ffn_Wk_c, L0_ffn_Wv_c, L0_ffn_Wk, L0_ffn_Wv, L0_ffn_Wo, L0_ffn_W_shared_in, L0_ffn_W_shared_out, L0_ffn_W1_shared, L0_ffn_W2_experts, L0_ffn_Wg_gate, L0_ffn_We_gate, L0_ffn_group_bias, L0_ffn_expert_bias, L0_ffn_norm1_w, L0_ffn_norm2_w):

    def _L0_attn_a_ref(x, Wq, bq, Wk, bk, Wv, bv, Wp, bp):
        import jax, jax.numpy as jnp
        import numpy as np
        N_HEAD = 16
        B, T, C = x.shape
        H = N_HEAD
        d = C // H

        def proj_heads(W, b):
            h = x @ W.T + b
            return h.reshape(B, T, H, d).transpose(0, 2, 1, 3)
        q = proj_heads(Wq, bq)
        k = proj_heads(Wk, bk)
        v = proj_heads(Wv, bv)
        q = jax.nn.softmax(q, axis=-1)
        k = jax.nn.softmax(k, axis=-1)
        k_sum = k.sum(axis=-2, keepdims=True)
        D_inv = 1.0 / (q * k_sum).sum(axis=-1, keepdims=True)
        context = jnp.einsum('bhnd,bhnv->bhdv', k, v)
        out = jnp.einsum('bhqd,bhdv->bhqv', q, context)
        out = out * D_inv + q
        out = out.transpose(0, 2, 1, 3).reshape(B, T, C)
        return out @ Wp.T + bp

    def _L0_attn_b_ref(x, gamma, beta, Wq, Wv, Wr, u_bias, v_bias, Wout, bout):
        import math
        import jax, jax.numpy as jnp
        import numpy as np
        SEQ, BATCH, D_MODEL, NHEAD, FEAT = (512, 2, 256, 8, 128)

        def _sinusoid_pe(length, d_model, dtype):
            pos = jnp.arange(length, dtype=dtype)[:, None]
            div = jnp.exp(jnp.arange(0, d_model, 2, dtype=dtype) * (-math.log(10000.0) / d_model))
            ang = pos * div
            return jnp.stack([jnp.sin(ang), jnp.cos(ang)], axis=-1).reshape(length, d_model)

        def _left_shift(x):
            I, J, B, N = x.shape
            zero = jnp.zeros((I, 1, B, N), x.dtype)
            padded = jnp.concatenate([zero, x], axis=1)
            padded = padded.reshape(J + 1, I, B, N)[1:]
            x = padded.reshape(I, J, B, N)
            return jnp.tril(x)
        I, B, D = x.shape
        H, F = u_bias.shape
        sqrt_d = jnp.asarray(math.sqrt(D), x.dtype)
        mu = jnp.mean(x, axis=-1, keepdims=True)
        var = jnp.mean((x - mu) ** 2, axis=-1, keepdims=True)
        h = (x - mu) * jax.lax.rsqrt(var + 1e-05) * gamma + beta
        pe = _sinusoid_pe(I, D, x.dtype)[::-1]
        q = (h @ Wq).reshape(I, B, H, F)
        k = (h @ Wq).reshape(I, B, H, F)
        v = (h @ Wv).reshape(I, B, H, F)
        r = (pe @ Wr).reshape(I, H, F)
        content = jnp.einsum('ibnf,jbnf->ijbn', q + u_bias, k)
        pos = jnp.einsum('ibnf,jnf->ijbn', q + v_bias, r)
        pos = _left_shift(pos)
        attn = jax.nn.softmax((content + pos) / sqrt_d, axis=1)
        o = jnp.einsum('ijbn,jbnf->ibnf', attn, v).reshape(I, B, H * F)
        return o @ Wout + bout

    def _L0_ffn_ref(src, Wq, Wk_c, Wv_c, Wk, Wv, Wo, W_shared_in, W_shared_out, W1_shared, W2_experts, Wg_gate, We_gate, group_bias, expert_bias, norm1_w, norm2_w):
        import jax, jax.numpy as jnp
        import numpy as np
        D = 256
        H = 16
        DH = D // H
        DC = D // 4
        HID = 512
        G = 2
        EPG = 4
        E = G * EPG
        TOPK = 2
        EPS = 1e-06
        B, T = (2, 512)

        def _rope_sincos(t, dh):
            inv_freq = 1.0 / 10000.0 ** (jnp.arange(0, dh, 2, dtype=jnp.float32) / dh)
            ang = jnp.arange(t, dtype=jnp.float32)[:, None] * inv_freq[None, :]
            return (jnp.sin(ang), jnp.cos(ang))

        def _apply_rope(x, sin, cos):
            x1 = x[..., ::2]
            x2 = x[..., 1::2]
            r = jnp.stack([x1 * cos - x2 * sin, x1 * sin + x2 * cos], axis=-1)
            return r.reshape(x.shape)

        def _swiglu(x):
            a, b = jnp.split(x, 2, axis=-1)
            return jax.nn.silu(a) * b

        def _rmsnorm(x, w):
            return x * jax.lax.rsqrt(jnp.mean(x * x, axis=-1, keepdims=True) + EPS) * w
        Bb, Tt, C = src.shape
        q = (src @ Wq).reshape(Bb, Tt, H, DH).transpose(0, 2, 1, 3)
        k = (src @ Wk_c @ Wk).reshape(Bb, Tt, H, DH).transpose(0, 2, 1, 3)
        v = (src @ Wv_c @ Wv).reshape(Bb, Tt, H, DH).transpose(0, 2, 1, 3)
        sin, cos = _rope_sincos(Tt, DH)
        q = _apply_rope(q, sin, cos)
        k = _apply_rope(k, sin, cos)
        attn = jnp.einsum('bhqd,bhkd->bhqk', q, k) / np.sqrt(DH).astype(np.float32)
        attn = jax.nn.softmax(attn, axis=-1)
        sa = jnp.einsum('bhqk,bhkd->bhqd', attn, v)
        sa = sa.transpose(0, 2, 1, 3).reshape(Bb, Tt, C) @ Wo
        x = _rmsnorm(src + sa, norm1_w)
        S = Bb * Tt
        flat = x.reshape(S, C)
        shared = _swiglu(flat @ W_shared_in) @ W_shared_out
        g_probs = jax.nn.softmax(flat @ Wg_gate + group_bias, -1)
        g_idx = jnp.argmax(g_probs, axis=-1)
        e_logits = flat @ We_gate + expert_bias
        e_group = jnp.arange(E) // EPG
        in_group = e_group[None, :] == g_idx[:, None]
        e_probs = jax.nn.softmax(jnp.where(in_group, e_logits, -jnp.inf), -1)
        g_prob = jnp.take_along_axis(g_probs, g_idx[:, None], axis=1)
        p_expert = e_probs * g_prob
        topv, topi = jax.lax.top_k(p_expert, TOPK)
        w = jnp.zeros((S, E), flat.dtype).at[jnp.arange(S)[:, None], topi].set(topv)
        h = _swiglu(flat @ W1_shared)
        routed = jnp.zeros_like(shared)
        for e in range(E):
            routed = routed + h @ W2_experts[e] * w[:, e:e + 1]
        out = x + (shared + routed).reshape(Bb, Tt, C)
        return _rmsnorm(out, norm2_w)
    x = L0_attn_a_x
    x = x + _L0_attn_a_ref(_layernorm(x, axis=-1), L0_attn_a_Wq, L0_attn_a_bq, L0_attn_a_Wk, L0_attn_a_bk, L0_attn_a_Wv, L0_attn_a_bv, L0_attn_a_Wp, L0_attn_a_bp)
    x = x + _L0_ffn_ref(_layernorm(x, axis=-1), L0_ffn_Wq, L0_ffn_Wk_c, L0_ffn_Wv_c, L0_ffn_Wk, L0_ffn_Wv, L0_ffn_Wo, L0_ffn_W_shared_in, L0_ffn_W_shared_out, L0_ffn_W1_shared, L0_ffn_W2_experts, L0_ffn_Wg_gate, L0_ffn_We_gate, L0_ffn_group_bias, L0_ffn_expert_bias, L0_ffn_norm1_w, L0_ffn_norm2_w)
    x = x + _L0_attn_b_ref(_layernorm(x, axis=-1), L0_attn_b_gamma, L0_attn_b_beta, L0_attn_b_Wq, L0_attn_b_Wv, L0_attn_b_Wr, L0_attn_b_u_bias, L0_attn_b_v_bias, L0_attn_b_Wout, L0_attn_b_bout)
    x = x + _L0_ffn_ref(_layernorm(x, axis=-1), L0_ffn_Wq, L0_ffn_Wk_c, L0_ffn_Wv_c, L0_ffn_Wk, L0_ffn_Wv, L0_ffn_Wo, L0_ffn_W_shared_in, L0_ffn_W_shared_out, L0_ffn_W1_shared, L0_ffn_W2_experts, L0_ffn_Wg_gate, L0_ffn_We_gate, L0_ffn_group_bias, L0_ffn_expert_bias, L0_ffn_norm1_w, L0_ffn_norm2_w)
    return x

_drawn_inputs = setup_inputs


def setup_inputs(seed=0):
    import zlib

    import numpy as np

    out = dict(_drawn_inputs(seed))
    spreads = {'L0_attn_b_gamma': (1.0, 0.6),
     'L0_attn_b_beta': (0.0, 0.788),
     'L0_attn_b_bout': (0.0, 0.1),
     'L0_ffn_group_bias': (0.0, 0.8),
     'L0_ffn_expert_bias': (0.0, 0.8),
     'L0_ffn_norm1_w': (1.0, 0.2),
     'L0_ffn_norm2_w': (1.0, 0.2)}
    factors = {'L0_attn_a_bq': 8.0,
     'L0_attn_a_Wk': 3.161,
     'L0_attn_a_bk': 8.0,
     'L0_attn_b_Wq': 64.0,
     'L0_attn_b_Wr': 64.0,
     'L0_attn_b_u_bias': 64.0,
     'L0_attn_b_v_bias': 64.0,
     'L0_ffn_Wq': 8.0,
     'L0_ffn_Wk_c': 8.0,
     'L0_ffn_Wv_c': 8.0,
     'L0_ffn_Wk': 8.0,
     'L0_ffn_Wv': 8.0,
     'L0_ffn_Wo': 8.0,
     'L0_ffn_W1_shared': 8.0,
     'L0_ffn_W2_experts': 8.0,
     'L0_ffn_Wg_gate': 8.0,
     'L0_ffn_We_gate': 8.0}
    for name, (base, spread) in spreads.items():
        noise = np.random.default_rng([zlib.crc32(name.encode()), seed]).standard_normal(out[name].shape)
        drawn = base * np.exp(spread * noise) if base else spread * noise
        out[name] = jnp.asarray(drawn.astype(out[name].dtype))
    for name, factor in factors.items():
        out[name] = (out[name] * factor).astype(out[name].dtype)
    return out
```

```python
import math
from contextlib import ExitStack

import numpy as np

import concourse.bass as bass
from concourse import mybir

ALU = mybir.AluOpType
ACT = mybir.ActivationFunctionType
AX = mybir.AxisListType
F32 = mybir.dt.float32
F32R = mybir.dt.float32r
P = 128
C = 256
B = 4
T = 1024
N = B * T
G = 512
K4 = G // P
NG = N // G
CH = C // P
DH = 16
LN_EPS = 1e-5
LN_LINKS = 3 * K4 + 1


class Phase:

    def __init__(self, nc, name):
        self.nc, self.name, self.ctx, self.sems = nc, name, ExitStack(), []

    def __enter__(self):
        return self

    def sb(self, name, shape, dt=F32):
        return self.ctx.enter_context(self.nc.sbuf_tensor(f"{self.name}_{name}", shape, dt))

    def ps(self, name, shape, dt=F32):
        return self.ctx.enter_context(self.nc.psum_tensor(f"{self.name}_{name}", shape, dt))

    def sem(self, name):
        s = self.nc.alloc_semaphore(name=f"{self.name}_{name}")
        self.sems.append(s)
        return s

    def __exit__(self, *err):
        if err[0] is None:
            self.ctx.close()
            self.nc.clear_and_free_semaphores(self.sems)
            self.nc.all_engine_barrier()


class Chain:

    def __init__(self, eng, sem, item, per):
        self.eng, self.sem, self.base, self.per, self.n = eng, sem, item * per, per, 0

    def done(self, ins):
        self.n += 1
        assert self.n <= self.per
        ins.then_inc(self.sem, 1)

    def wait(self):
        self.eng.wait_ge(self.sem, self.base + self.n)

    def __call__(self, ins):
        self.done(ins)
        self.wait()

    def close(self):
        assert self.n == self.per, (self.n, self.per)


def normalize_group(dve, nc, item, chain_sem, var_ready, rstd_ready, x4, stats, mv, var, rstd, out4):
    link = Chain(dve, chain_sem, item, LN_LINKS)
    for k in range(K4):
        link.done(nc.vector.bn_stats(stats[:, k, :], x4[:, k, :]))
    link.wait()
    link.done(nc.vector.memset(var[:, :], 0.0))
    for k in range(K4):
        link.done(nc.vector.bn_aggr(mv[:, k, :], stats[:, k, :]))
    link.wait()
    nc.vector.tensor_scalar(var[:, :], mv[:, :, 1], LN_EPS, None, ALU.add).then_inc(var_ready, 1)
    dve.wait_ge(rstd_ready, item + 1)
    for k in range(K4):
        link.done(nc.vector.tensor_scalar(out4[:, k, :], x4[:, k, :], mv[:, k, 0:1], rstd[:, k:k + 1],
                                          ALU.subtract, ALU.mult))
    link.wait()
    link.close()


def group_view(dram, g):
    return dram[bass.ds(g * G, G), :].rearrange("(k p) c -> p k c", p=P)


def linear_keys(nc, x_d, q_d, ctx_d, w):
    with Phase(nc, "lk") as ph:
        sb, ps, sem = ph.sb, ph.ps, ph.sem
        x4, xn = sb("x4", [P, 2, K4, C]), sb("xn", [P, 2, K4, C])
        stats, mv = sb("stats", [P, K4, 6]), sb("mv", [P, K4, 2])
        var, rstd, nhalf = sb("var", [P, K4]), sb("rstd", [P, K4]), sb("nhalf", [P, K4])
        ident, wt = sb("ident", [P, P]), sb("wt", [P, CH, 3 * C])
        bias, block_mask, head_mask = sb("bias", [P, 3 * C]), sb("block", [P, P]), sb("heads", [P, 8])
        xT = sb("xT", [P, 2, CH, G])
        qk = sb("qk", [P, 2, 2 * C])
        qkn = sb("qkn", [P, 2, 2 * C])
        v = sb("v", [P, 2, CH, P + 2])
        mx, sm = sb("mx", [P, 2, 32]), sb("sm", [P, 2, 32])
        ctx = sb("ctx", [P, CH, P + 8])
        tp = ps("tp", [P, CH, G])
        qk_ps = [ps(f"qk{i}", [P, 2 * C]) for i in range(2)]
        v_ps = [ps(f"v{i}", [P, C]) for i in range(2)]
        c_ps = [ps(f"c{i}", [P, P + 2]) for i in range(2)]
        weights_in, x_in, consts = sem("weights_in"), [sem("x_in0"), sem("x_in1")], sem("consts")
        ln_chain, var_ready, rstd_ready = sem("ln_chain"), sem("var_ready"), sem("rstd_ready")
        turned, xT_ready = sem("turned"), sem("xT_ready")
        qk_made, biased, exp_ready, soft_chain = sem("qk_made"), sem("biased"), sem("exp_ready"), sem("soft_chain")
        shifted, q_out = sem("shifted"), [sem("q_out0"), sem("q_out1")]
        summed, ctx_chain, ctx_out = sem("summed"), sem("ctx_chain"), sem("ctx_out")
        NWD = 7
        NT = T // P

        block = ph.ctx.enter_context(nc.Block())

        @block.sync
        def _(sp):
            for dst, a in ((ident, w["ident"]), (bias, w["qkv_bias"].broadcast_to([P, 3 * C])),
                           (block_mask, w["block_mask"]), (head_mask, w["head_mask"])):
                sp.dma_start(dst[:], a).then_inc(weights_in, 16)
            for j in range(3):
                sp.dma_start(wt[:, :, j * C:(j + 1) * C], w["qkv"][j].rearrange("(h p) f -> p h f", p=P)).then_inc(weights_in, 16)

            def load(b, half):
                sp.dma_start(x4[:, half], group_view(x_d, 2 * b + half)).then_inc(x_in[half], 16)

            load(0, 0)
            load(0, 1)

            def step(b, more):
                for half in range(2):
                    g = 2 * b + half
                    for k in range(K4):
                        t = g * K4 + k
                        sp.wait_ge(soft_chain, (t + 1) * 3)
                        sp.dma_start(q_d[bass.ds(t * P, P), :], qkn[:, k % 2, 0:C]).then_inc(q_out[k % 2], 16)
                    if more:
                        load(b + 1, half)
                sp.wait_ge(ctx_chain, (b + 1) * 4)
                sp.dma_start(ctx_d[:, bass.ds(b * CH, CH), :], ctx[:, :, :]).then_inc(ctx_out, 16)

            with sp.Fori(0, B - 1) as b:
                step(b, True)
            step(B - 1, False)
            for s in q_out:
                sp.wait_ge(s, B * NT // 2 * 16)
            sp.wait_ge(ctx_out, B * 16)

        @block.gpsimd
        def _(pool):
            nc.gpsimd.memset(nhalf[:, :], -0.5).then_inc(consts, 1)
            pool.wait_ge(consts, 1)
            nc.gpsimd.memset(v[:, :, :, P:P + 2], 1.0).then_inc(consts, 1)
            with pool.Fori(0, B) as b:
                for half in range(2):
                    pool.wait_ge(var_ready, 2 * b + half + 1)
                    nc.gpsimd.tensor_tensor(rstd[:, :], var[:, :], nhalf[:, :], ALU.pow).then_inc(rstd_ready, 1)

        @block.scalar
        def _(act):
            def turned_in(b, half, first):
                g = 2 * b + half
                act.wait_ge(turned, g + 1)
                if not first:
                    act.wait_ge(qk_made, (g - 1) * K4)
                nc.scalar.copy(xT[:, half], tp[:, :, :]).then_inc(xT_ready, 1)

            def step(b, first, more):
                for half in range(2):
                    for k in range(K4):
                        t = (2 * b + half) * K4 + k
                        act.wait_ge(shifted, t + 1)
                        nc.scalar.activation(qk[:, k % 2], qk[:, k % 2], ACT.Exp).then_inc(exp_ready, 1)
                        if k == 1 and (half == 0 or more):
                            turned_in(b + half, 1 - half, first and half == 0)

            turned_in(0, 0, True)
            step(0, True, True)
            with act.Fori(1, B - 1) as b:
                step(b, False, True)
            step(B - 1, False, False)

        @block.vector
        def _(dve):
            dve.wait_ge(weights_in, NWD * 16)
            dve.wait_ge(consts, 2)

            def norm(b, half, first):
                g = 2 * b + half
                dve.wait_ge(x_in[half], (b + 1) * 16)
                if not first:
                    dve.wait_ge(turned, g - 1)
                normalize_group(dve, nc, g, ln_chain, var_ready, rstd_ready, x4[:, half], stats, mv, var, rstd, xn[:, half])

            def heads(a):
                return a.rearrange("p (h d) -> p h d", d=DH)

            def spread(a):
                return a.rearrange("p (h o) -> p h o", o=1).broadcast_to([P, 32, DH])

            def shift(t, k, first):
                i = k % 2
                link = Chain(dve, biased, t, 3)
                dve.wait_ge(qk_made, t + 1)
                if not first:
                    dve.wait_ge(summed, t - 1)
                link.done(nc.vector.tensor_tensor(qk[:, i], qk_ps[i][:, :], bias[:, 0:2 * C], ALU.add))
                link(nc.vector.tensor_tensor(v[:, i, :, 0:P], v_ps[i][:, :].rearrange("p (h f) -> p h f", h=CH),
                                             bias[:, 2 * C:3 * C].rearrange("p (h f) -> p h f", h=CH), ALU.add))
                link(nc.vector.tensor_reduce(mx[:, i], heads(qk[:, i]), AX.X, ALU.max))
                nc.vector.tensor_tensor(heads(qk[:, i]), heads(qk[:, i]), spread(mx[:, i]), ALU.subtract).then_inc(shifted, 1)

            def soften(t, k, first):
                i = k % 2
                link = Chain(dve, soft_chain, t, 3)
                dve.wait_ge(exp_ready, t + 1)
                link(nc.vector.tensor_reduce(sm[:, i], heads(qk[:, i]), AX.X, ALU.add))
                link(nc.vector.reciprocal(sm[:, i], sm[:, i]))
                if not first:
                    dve.wait_ge(summed, t - 1)
                    dve.wait_ge(q_out[i], first_store(t, k))
                link(nc.vector.tensor_tensor(heads(qkn[:, i]), heads(qk[:, i]), spread(sm[:, i]), ALU.mult))

            def first_store(t, k):
                return stores[0] + (k // 2) * 16

            stores = [0]

            def keys_of(b, first):
                link = Chain(dve, ctx_chain, b, 4)
                dve.wait_ge(summed, (b + 1) * NT)
                if not first:
                    dve.wait_ge(ctx_out, b * 16)
                for h in range(CH):
                    link.done(nc.vector.tensor_tensor(ctx[:, h, 0:P], c_ps[h][:, 0:P], block_mask[:, :], ALU.mult))
                    link.done(nc.vector.tensor_tensor(ctx[:, h, P:P + 8], c_ps[h][:, P:P + 1].broadcast_to([P, 8]),
                                                      head_mask[:, :], ALU.mult))
                link.close()

            def step(b, first, more):
                for half in range(2):
                    for k in range(K4):
                        t = (2 * b + half) * K4 + k
                        early = first and half == 0 and k < 2
                        shift(t, k, early)
                        if k == 0 and (half == 0 or more) and not (first and half == 0):
                            norm(b + half, 1 - half, first and half == 0)
                        stores[0] = (2 * b + half) * 32
                        soften(t, k, early)
                keys_of(b, first)

            norm(0, 0, True)
            norm(0, 1, True)
            step(0, True, True)
            with dve.Fori(1, B - 1) as b:
                step(b, False, True)
            step(B - 1, False, False)

        @block.tensor
        def _(pe):
            pe.wait_ge(weights_in, NWD * 16)

            def turn(b, half, first):
                g = 2 * b + half
                pe.wait_ge(ln_chain, (g + 1) * LN_LINKS)
                if not first:
                    pe.wait_ge(xT_ready, g)
                for k in range(K4):
                    for h in range(CH):
                        last = nc.tensor.transpose(tp[:, h, k * P:(k + 1) * P], xn[:, half, k, h * P:(h + 1) * P], ident[:, :])
                last.then_inc(turned, 1)

            def project(b, half, k, early):
                t = (2 * b + half) * K4 + k
                if k == 0:
                    pe.wait_ge(xT_ready, 2 * b + half + 1)
                if not early:
                    pe.wait_ge(biased, (t - 1) * 3)
                cols = slice(k * P, (k + 1) * P)
                for out, f in ((v_ps[k % 2], slice(2 * C, 3 * C)), (qk_ps[k % 2], slice(0, 2 * C))):
                    for h in range(CH):
                        mm = nc.tensor.matmul(out[:, :], xT[:, half, h, cols], wt[:, h, f], start=h == 0, stop=h == CH - 1)
                mm.then_inc(qk_made, 1)

            def sum_keys(b, half, k, first):
                t = (2 * b + half) * K4 + k
                pe.wait_ge(soft_chain, (t + 1) * 3)
                if half == 0 and k == 0 and not first:
                    pe.wait_ge(ctx_chain, b * 4)
                for h in range(CH):
                    mm = nc.tensor.matmul(c_ps[h][:, :], qkn[:, k % 2, C + h * P:C + (h + 1) * P], v[:, k % 2, h, :],
                                          start=half == 0 and k == 0, stop=half == 1 and k == K4 - 1)
                mm.then_inc(summed, 1)

            def step(b, first, more):
                for half in range(2):
                    for k in range(K4):
                        project(b, half, k, first and half == 0 and k < 2)
                        if k > 0:
                            sum_keys(b, half, k - 1, first)
                        elif half:
                            sum_keys(b, 0, K4 - 1, first)
                        elif not first:
                            sum_keys(b - 1, 1, K4 - 1, False)
                        if k == 1 and (half == 0 or more):
                            turn(b + half, 1 - half, False)

            turn(0, 0, True)
            step(0, True, True)
            with pe.Fori(1, B - 1) as b:
                step(b, False, True)
            step(B - 1, False, False)
            sum_keys(B - 1, 1, K4 - 1, False)


def linear_mix(nc, x_d, q_d, ctx_d, out_d, w):
    W = P + 8
    with Phase(nc, "lm") as ph:
        sb, ps, sem = ph.sb, ph.ps, ph.sem
        q4, x4 = sb("q4", [P, 2, K4, C]), sb("x4", [P, 2, K4, C])
        ctx = sb("ctx", [P, 2, CH, W])
        ident, wp, bp = sb("ident", [P, P]), sb("wp", [P, CH, C]), sb("bp", [P, C])
        qT, aT = sb("qT", [P, CH, G]), sb("aT", [P, CH, G])
        inv, a4 = sb("inv", [P, 2, 16]), sb("a4", [P, K4, C])
        tp, tq = ps("tp", [P, CH, G]), ps("tq", [P, CH, G])
        mix = [ps(f"mix{i}", [P, CH, W]) for i in range(2)]
        o_ps = [ps(f"o{i}", [P, C]) for i in range(2)]
        weights_in, loads = sem("weights_in"), [sem("loads0"), sem("loads1")]
        q_turned, qT_ready, mixed, mix_chain = sem("q_turned"), sem("qT_ready"), sem("mixed"), sem("mix_chain")
        a_turned, aT_ready, projected, out_chain = sem("a_turned"), sem("aT_ready"), sem("projected"), sem("out_chain")
        xb_ready = sem("xb_ready")
        stored = [sem("stored0"), sem("stored1")]
        NL = 3
        block = ph.ctx.enter_context(nc.Block())

        def batches(eng, group):
            group(0, 0, True)
            group(0, 1, False)
            with eng.Fori(1, B) as b:
                for half in range(2):
                    group(b, half, False)

        @block.sync
        def _(sp):
            for dst, a in ((ident, w["ident"]), (wp, w["wpt"].rearrange("(h p) f -> p h f", p=P)),
                           (bp, w["bp"].broadcast_to([P, C]))):
                sp.dma_start(dst[:], a).then_inc(weights_in, 16)

            def load(b, half, fresh):
                g = 2 * b + half
                if not fresh:
                    sp.wait_ge(stored[half], b * 16)
                    sp.wait_ge(mix_chain, b * 2 * K4 * 3 + (half - 1) * K4 * 3)
                sp.dma_start(q4[:, half], group_view(q_d, g)).then_inc(loads[half], 16)
                sp.dma_start(x4[:, half], group_view(x_d, g)).then_inc(loads[half], 16)
                sp.dma_start(ctx[:, half], ctx_d[:, bass.ds(b * CH, CH), :]).then_inc(loads[half], 16)

            def store(b, half):
                g = 2 * b + half
                sp.wait_ge(out_chain, (g + 1) * K4)
                sp.dma_start(group_view(out_d, g), x4[:, half]).then_inc(stored[half], 16)

            load(0, 0, True)
            load(0, 1, True)
            with sp.Fori(0, B - 1) as b:
                for half in range(2):
                    store(b, half)
                    load(b + 1, half, False)
            for half in range(2):
                store(B - 1, half)
            for s in stored:
                sp.wait_ge(s, B * 16)

        @block.gpsimd
        def _(pool):
            pool.wait_ge(weights_in, NL * 16)
            with pool.Fori(0, B) as b:
                for half in range(2):
                    pool.wait_ge(loads[half], (b + 1) * NL * 16)
                    nc.gpsimd.tensor_tensor(x4[:, half], x4[:, half],
                                            bp[:, :].rearrange("p (o c) -> p o c", o=1).broadcast_to([P, K4, C]),
                                            ALU.add).then_inc(xb_ready, 1)

        @block.scalar
        def _(act):
            def group(b, half, first):
                g = 2 * b + half
                act.wait_ge(q_turned, g + 1)
                if not first:
                    act.wait_ge(mixed, g * K4)
                nc.scalar.copy(qT[:, :, :], tq[:, :, :]).then_inc(qT_ready, 1)
                act.wait_ge(a_turned, g + 1)
                if not first:
                    act.wait_ge(projected, g * K4)
                nc.scalar.copy(aT[:, :, :], tp[:, :, :]).then_inc(aT_ready, 1)

            batches(act, group)

        @block.vector
        def _(dve):
            def finish(g, half):
                dve.wait_ge(xb_ready, g + 1)
                for k in range(K4):
                    dve.wait_ge(projected, g * K4 + k + 1)
                    nc.vector.tensor_tensor(x4[:, half, k], x4[:, half, k], o_ps[k % 2][:, :], ALU.add).then_inc(out_chain, 1)

            def group(b, half, first):
                g = 2 * b + half
                dve.wait_ge(loads[half], (b + 1) * NL * 16)
                for k in range(K4):
                    t = g * K4 + k
                    link = Chain(dve, mix_chain, t, 3)
                    dve.wait_ge(mixed, t + 1)
                    if k == 0 and not first:
                        dve.wait_ge(a_turned, g)
                    m = mix[k % 2]
                    link(nc.vector.reciprocal(inv[:, k % 2].rearrange("p (h d) -> p h d", h=CH), m[:, :, P:W]))
                    link(nc.vector.tensor_tensor(
                        a4[:, k].rearrange("p (h n d) -> p h n d", h=CH, d=DH),
                        m[:, :, 0:P].rearrange("p h (n d) -> p h n d", d=DH),
                        inv[:, k % 2].rearrange("p (h n o) -> p h n o", h=CH, o=1).broadcast_to([P, CH, 8, DH]), ALU.mult))
                    link(nc.vector.tensor_tensor(a4[:, k], a4[:, k], q4[:, half, k], ALU.add))
                finish(g, half)

            batches(dve, group)

        @block.tensor
        def _(pe):
            pe.wait_ge(weights_in, NL * 16)

            def turn_q(b, half, first):
                g = 2 * b + half
                pe.wait_ge(loads[half], (b + 1) * NL * 16)
                if not first:
                    pe.wait_ge(qT_ready, g)
                for k in range(K4):
                    for h in range(CH):
                        mm = nc.tensor.transpose(tq[:, h, k * P:(k + 1) * P], q4[:, half, k, h * P:(h + 1) * P], ident[:, :])
                mm.then_inc(q_turned, 1)

            def group(b, half, first, more=True):
                g = 2 * b + half
                pe.wait_ge(qT_ready, g + 1)
                for k in range(K4):
                    t = g * K4 + k
                    if not (first and k < 2):
                        pe.wait_ge(mix_chain, (t - 1) * 3)
                    for h in range(CH):
                        mm = nc.tensor.matmul(mix[k % 2][:, h], qT[:, h, k * P:(k + 1) * P], ctx[:, half, h], start=True, stop=True)
                    mm.then_inc(mixed, 1)
                if more:
                    turn_q(b + half, 1 - half, False)
                pe.wait_ge(mix_chain, (g + 1) * K4 * 3)
                if not first:
                    pe.wait_ge(aT_ready, g)
                for k in range(K4):
                    for h in range(CH):
                        mm = nc.tensor.transpose(tp[:, h, k * P:(k + 1) * P], a4[:, k, h * P:(h + 1) * P], ident[:, :])
                mm.then_inc(a_turned, 1)
                pe.wait_ge(aT_ready, g + 1)
                for k in range(K4):
                    t = g * K4 + k
                    if not (first and k < 2):
                        pe.wait_ge(out_chain, t - 1)
                    for h in range(CH):
                        mm = nc.tensor.matmul(o_ps[k % 2][:, :], aT[:, h, k * P:(k + 1) * P], wp[:, h, :],
                                              start=h == 0, stop=h == CH - 1)
                    mm.then_inc(projected, 1)

            turn_q(0, 0, True)
            group(0, 0, True)
            group(0, 1, False)
            with pe.Fori(1, B - 1) as b:
                for half in range(2):
                    group(b, half, False)
            group(B - 1, 0, False)
            group(B - 1, 1, False, False)


def ffn_project(nc, tag, x_d, src_d, qk_d, V, w):
    with Phase(nc, tag + "_fp") as ph:
        sb, ps, sem = ph.sb, ph.ps, ph.sem
        x4 = sb("x4", [P, 2, K4, C])
        src = sb("src", [P, 2, K4, C])
        stats, mv = sb("stats", [P, K4, 6]), sb("mv", [P, K4, 2])
        var, rstd, nhalf = sb("var", [P, K4]), sb("rstd", [P, K4]), sb("nhalf", [P, K4])
        ident = sb("ident", [P, P])
        wq, wqs = sb("wq", [P, CH, C]), sb("wqs", [P, CH, C])
        wc = sb("wc", [P, CH, P])
        wk, wks, wv = sb("wk", [64, C]), sb("wks", [64, C]), sb("wv", [P, C])
        cos, sin = sb("cos", [P, T]), sb("sin", [P, T])
        srcT = sb("srcT", [P, 2, CH, G])
        kcvc = sb("kcvc", [P, G])
        ta, tb = sb("ta", [P, 2, G]), sb("tb", [P, 2, G])
        rot = sb("rot", [P, 2, G])
        hi, lo = sb("hi", [P, 2, G], F32R), sb("lo", [P, 2, G], F32R)
        tp = ps("tp", [P, CH, G])
        pair = [[ps(f"pair{i}{j}", [P, G]) for j in range(2)] for i in range(2)]
        kv_ps, v_ps = ps("kv", [P, G]), ps("v", [P, 2, C])

        weights_in, x_in = sem("weights_in"), [sem("x_in0"), sem("x_in1")]
        src_out = [sem("src_out0"), sem("src_out1")]
        consts = sem("consts")
        ln_chain, var_ready, rstd_ready = sem("ln_chain"), sem("var_ready"), sem("rstd_ready")
        turned, srcT_ready = sem("turned"), sem("srcT_ready")
        kv_made, kv_ready = sem("kv_made"), sem("kv_ready")
        v_made, v_ready = sem("v_made"), sem("v_ready")
        pair_made, pair_read, rot_chain, rot_ready = sem("pair_made"), sem("pair_read"), sem("rot_chain"), sem("rot_ready")
        hi_ready, lo_ready, parts_out = sem("hi_ready"), sem("lo_ready"), [sem("parts_out0"), sem("parts_out1")]
        NW = 10

        block = ph.ctx.enter_context(nc.Block())

        def groups(eng, body):
            with eng.Fori(0, B) as b:
                for half in range(2):
                    body(b, half)

        @block.sync
        def _(sp):
            for dst, a in ((ident, w["ident"]), (wq, w["wq"].rearrange("(h p) f -> p h f", p=P)),
                           (wqs, w["wqs"].rearrange("(h p) f -> p h f", p=P)), (wk, w["wk"]), (wks, w["wks"]),
                           (cos, w["cos"]), (sin, w["sin"])):
                sp.dma_start(dst[:], a).then_inc(weights_in, 16)
            sp.dma_start(wv[64:128, :], w["wv"]).then_inc(weights_in, 16)
            sp.dma_start(wc[:, :, 0:64], w["wkc"].rearrange("(h p) f -> p h f", p=P)).then_inc(weights_in, 16)
            sp.dma_start(wc[:, :, 64:128], w["wvc"].rearrange("(h p) f -> p h f", p=P)).then_inc(weights_in, 16)

            def load_x(b, half):
                sp.dma_start(x4[:, half], group_view(x_d, 2 * b + half)).then_inc(x_in[half], 16)

            load_x(0, 0)
            load_x(0, 1)

            def step(b, half, more):
                g = 2 * b + half
                sp.wait_ge(ln_chain, (g + 1) * LN_LINKS)
                sp.dma_start(group_view(src_d, g), src[:, half]).then_inc(src_out[half], 16)
                if more:
                    load_x(b + 1, half)
                for n in range(4):
                    rows = qk_d[:, bass.ds(b * C + (n % 2) * P, P), half * G:(half + 1) * G]
                    sp.wait_ge(hi_ready, g * 4 + n + 1)
                    sp.dma_start(rows[2 * (n // 2)], hi[:, n % 2].bitcast(F32)).then_inc(parts_out[n % 2], 16)
                    sp.wait_ge(lo_ready, g * 4 + n + 1)
                    sp.dma_start(rows[2 * (n // 2) + 1], lo[:, n % 2].bitcast(F32)).then_inc(parts_out[n % 2], 16)

            with sp.Fori(0, B - 1) as b:
                for half in range(2):
                    step(b, half, True)
            for half in range(2):
                step(B - 1, half, False)
            for s in src_out:
                sp.wait_ge(s, B * 16)
            for s in parts_out:
                sp.wait_ge(s, NG * 4 * 16)

        @block.gpsimd
        def _(pool):
            nc.gpsimd.memset(nhalf[:, :], -0.5).then_inc(consts, 1)
            pool.wait_ge(consts, 1)

            def step(b, half):
                g = 2 * b + half
                pool.wait_ge(var_ready, g + 1)
                nc.gpsimd.tensor_tensor(rstd[:, :], var[:, :], nhalf[:, :], ALU.pow).then_inc(rstd_ready, 1)

            groups(pool, step)

        @block.vector
        def _(dve):
            dve.wait_ge(weights_in, NW * 16)

            def norm(b, half, first):
                g = 2 * b + half
                dve.wait_ge(x_in[half], (b + 1) * 16)
                if not first:
                    dve.wait_ge(turned, g - 1)
                    dve.wait_ge(src_out[half], b * 16)
                normalize_group(dve, nc, g, ln_chain, var_ready, rstd_ready, x4[:, half], stats, mv, var, rstd,
                                src[:, half])

            def rotate(b, half, first):
                g = 2 * b + half
                link = Chain(dve, rot_chain, g, 12)
                for n in range(4):
                    i = n % 2
                    t = slice(half * G, (half + 1) * G)
                    dve.wait_ge(pair_made, g * 4 + n + 1)
                    link.done(nc.vector.tensor_tensor(ta[:, i], pair[i][0][:, :], cos[:, t], ALU.mult))
                    link.done(nc.vector.tensor_tensor(tb[:, i], pair[i][1][:, :], sin[:, t], ALU.mult))
                    link.wait()
                    if not (first and n < 2):
                        dve.wait_ge(hi_ready, g * 4 + n - 1)
                    link(nc.vector.tensor_tensor(rot[:, i], ta[:, i], tb[:, i], ALU.add))
                    dve.wait_ge(hi_ready, g * 4 + n + 1)
                    if not (first and n < 2):
                        dve.wait_ge(parts_out[i], g * 64 + (n // 2) * 32)
                    nc.vector.tensor_tensor(lo[:, i], rot[:, i], hi[:, i].bitcast(F32), ALU.subtract).then_inc(lo_ready, 1)
                link.close()

            norm(0, 0, True)
            norm(0, 1, True)
            rotate(0, 0, True)
            with dve.Fori(1, B) as b:
                norm(b, 0, False)
                rotate(b - 1, 1, False)
                norm(b, 1, False)
                rotate(b, 0, False)
            rotate(B - 1, 1, False)

        @block.scalar
        def _(act):
            def turned_in(b, half, first):
                g = 2 * b + half
                act.wait_ge(turned, g + 1)
                if not first:
                    act.wait_ge(v_made, 2 * (g - 1))
                nc.scalar.copy(srcT[:, half], tp[:, :, :]).then_inc(srcT_ready, 1)

            def halves(b, half, n, first):
                g = 2 * b + half
                act.wait_ge(rot_chain, g * 12 + 3 * n + 3)
                if not (first and n < 2):
                    act.wait_ge(parts_out[n % 2], g * 64 + (n // 2) * 32)
                nc.scalar.copy(hi[:, n % 2], rot[:, n % 2]).then_inc(hi_ready, 1)

            def step(b, half, first, more):
                g = 2 * b + half
                act.wait_ge(kv_made, g + 1)
                if not (first and half == 0):
                    act.wait_ge(pair_made, 4 * g)
                nc.scalar.copy(kcvc[:, :], kv_ps[:, :]).then_inc(kv_ready, 1)
                halves(b, half, 0, first and half == 0)
                halves(b, half, 1, first and half == 0)
                for r in range(2):
                    act.wait_ge(v_made, 2 * g + r + 1)
                    kt = half * K4 + 2 * r
                    nc.scalar.copy(V[:, bass.ds(b * 8, 8), kt:kt + 2, :].rearrange("p u k c -> p k u c"),
                                   v_ps[:, :, :].rearrange("p k (u c) -> p k u c", u=8)).then_inc(v_ready, 1)
                if more:
                    turned_in(b + half, 1 - half, first and half == 0)
                halves(b, half, 2, False)
                halves(b, half, 3, False)

            turned_in(0, 0, True)
            step(0, 0, True, True)
            step(0, 1, False, True)
            with act.Fori(1, B - 1) as b:
                for half in range(2):
                    step(b, half, False, True)
            step(B - 1, 0, False, True)
            step(B - 1, 1, False, False)

        @block.tensor
        def _(pe):
            pe.wait_ge(weights_in, NW * 16)

            def turn(b, half, first):
                g = 2 * b + half
                pe.wait_ge(ln_chain, (g + 1) * LN_LINKS)
                if not first:
                    pe.wait_ge(srcT_ready, g)
                for k in range(K4):
                    for h in range(CH):
                        last = nc.tensor.transpose(tp[:, h, k * P:(k + 1) * P], src[:, half, k, h * P:(h + 1) * P], ident[:, :])
                last.then_inc(turned, 1)

            def project(b, half, first, more):
                g = 2 * b + half
                pe.wait_ge(srcT_ready, g + 1)
                if not first:
                    pe.wait_ge(kv_ready, g)
                for h in range(CH):
                    mm = nc.tensor.matmul(kv_ps[:, :], wc[:, h, :], srcT[:, half, h, :], start=h == 0, stop=h == CH - 1)
                mm.then_inc(kv_made, 1)
                for n in range(4):
                    if not (first and n < 2):
                        pe.wait_ge(rot_chain, g * 12 + 3 * (n - 2) + 2)
                    f = slice((n % 2) * P, (n % 2 + 1) * P)
                    if n == 2:
                        pe.wait_ge(kv_ready, g + 1)
                    for j in range(2):
                        if n < 2:
                            a = (wq, wqs)[j]
                            for h in range(CH):
                                mm = nc.tensor.matmul(pair[n % 2][j][:, :], a[:, h, f], srcT[:, half, h, :],
                                                      start=h == 0, stop=h == CH - 1)
                        else:
                            mm = nc.tensor.matmul(pair[n % 2][j][:, :], (wk, wks)[j][:, f], kcvc[0:64, :],
                                                  start=True, stop=True)
                    mm.then_inc(pair_made, 1)
                    if n == 1:
                        pe.wait_ge(kv_ready, g + 1)
                        for r in range(2):
                            if not (first and r == 0):
                                pe.wait_ge(v_ready, 2 * g + r)
                            for k in range(2):
                                mm = nc.tensor.matmul(v_ps[:, k, :], kcvc[64:128, (2 * r + k) * P:(2 * r + k + 1) * P],
                                                      wv[64:128, :], start=True, stop=True)
                            mm.then_inc(v_made, 1)
                        if more:
                            turn(b + half, 1 - half, False)

            turn(0, 0, True)
            project(0, 0, True, True)
            project(0, 1, False, True)
            with pe.Fori(1, B - 1) as b:
                for half in range(2):
                    project(b, half, False, True)
            project(B - 1, 0, False, True)
            project(B - 1, 1, False, False)


def ffn_attend(nc, tag, qk_d, V, heads_d, w):
    U = 32
    KT = T // P
    NB = 3
    LEAD = 3
    R = 4 * DH
    SCALE = 0.25
    with Phase(nc, tag + "_fa") as ph:
        sb, ps, sem = ph.sb, ph.ps, ph.sem
        qs = [sb(f"qs{i}", [R + 2, 2, T], F32R) for i in range(NB)]
        ks = [sb(f"ks{i}", [R + 2, 2, T], F32R) for i in range(NB)]
        va = [sb(f"va{i}", [P, KT, 2, 32]) for i in range(NB)]
        probs = [sb(f"probs{i}", [P, T]) for i in range(4)]
        pm = sb("pm", [P, 2, KT, 2])
        mx = sb("mx", [P, 2 * KT])
        nhi, nlo = sb("nhi", [2 * KT, P], F32R), sb("nlo", [2 * KT, P], F32R)
        osb, ident = sb("osb", [P, G]), sb("ident", [P, P])
        rsum = sb("rsum", [P, K4 * 4])
        heads = [sb(f"heads{i}", [P, KT, 2 * DH]) for i in range(NB)]
        ring = [ps(f"ring{i}", [P, G]) for i in range(3)]
        score = [ps(f"score{i}", [P, T]) for i in range(2)]
        acc = ps("acc", [P, G])

        ident_in, ones_set, va_set = sem("ident_in"), sem("ones_set"), sem("va_set")
        loaded = [sem(f"loaded{i}") for i in range(NB)]
        rows_in = [sem(f"rows_in{i}") for i in range(NB)]
        va_ready = sem("va_ready")
        ring_made, ring_read = sem("ring_made"), sem("ring_read")
        mx_ready, nhi_ready = sem("mx_ready"), sem("nhi_ready")
        score_made, exp_done, pv_done = sem("score_made"), sem("exp_done"), sem("pv_done")
        heads_out = [sem(f"heads_out{i}") for i in range(NB)]
        osb_ready, out_chain = sem("osb_ready"), sem("out_chain")

        block = ph.ctx.enter_context(nc.Block())

        def steady(eng, step, first=0):
            for u in range(3 * first + 1):
                step(0, u)
            with eng.Fori(first, 9) as i:
                for c in (1, 2, 3):
                    step(i, c, True)
            for u in range(28, U + 1):
                step(0, u)

        def items(u):
            out = []
            if u == U:
                return ["out"]
            for k in range(KT):
                if u is None or u + (1 if k + LEAD < KT else 2) < U:
                    out += [("one", k, x) for x in range(4)]
                if k == 2 and u != 0:
                    out.append("out")
                if k == KT - LEAD and (u is None or u + 1 < U):
                    out.append("max")
            return out

        PER_UNIT = len(items(None))
        BEFORE = 4 * KT + 1 + 4 * LEAD
        assert PER_UNIT % 3 == 1

        def place(i, c, inner, what):
            if inner:
                n = BEFORE + len(items(0)) + (c - 1) * PER_UNIT + items(None).index(what)
                return 3 * i * PER_UNIT + n, ring[n % 3]
            n = BEFORE + sum(len(items(v)) for v in range(c)) + items(c).index(what)
            return n, ring[n % 3]

        def ready_out(i, c, inner=False):
            return place(i, c + 1, inner, "out")[0] + 1

        def ready_max(i, c, inner=False):
            return 4 * KT + 1 if not inner and c == 0 else place(i, c - 1, inner, "max")[0] + 1

        @block.sync
        def _(sp):
            sp.dma_start(ident[:, :], w["ident"]).then_inc(ident_in, 16)

            def load(i, c):
                u = 3 * i + c
                for stack, parts in ((qs, (0, 0, 1, 1)), (ks, (2, 3, 2, 3))):
                    for r, part in enumerate(parts):
                        sp.dma_start(stack[c % NB][r * DH:(r + 1) * DH].bitcast(F32),
                                     qk_d[part, bass.ds(u * 32, 32), :].rearrange("(h d) t -> d h t", h=2)
                                     ).then_inc(loaded[c % NB], 16)

            def max_rows(i, c, inner=False):
                u = 3 * i + c
                sp.wait_ge(nhi_ready, u + 1)
                sp.dma_start(qs[c % NB][R:R + 1].bitcast(F32), nhi[:, :].bitcast(F32)).then_inc(rows_in[c % NB], 16)
                sp.wait_ge(ring_read, ready_max(i, c, inner))
                sp.dma_start(qs[c % NB][R + 1:R + 2].bitcast(F32), nlo[:, :].bitcast(F32)).then_inc(rows_in[c % NB], 16)

            for u in range(NB):
                load(0, u)
            max_rows(0, 0)

            def step(i, c, inner=False):
                u = 3 * i + c
                if inner or u + 1 < U:
                    max_rows(i, c + 1, inner)
                if inner or u >= 1:
                    sp.wait_ge(ring_read, ready_out(i, c - 1, inner))
                    sp.dma_start(heads_d[:, bass.ds(u - 1, 1), :, :].rearrange("p u k c -> p (u k c)"),
                                 heads[(c - 1) % NB][:, :, :].rearrange("p k c -> p (k c)")
                                 ).then_inc(heads_out[(c - 1) % NB], 16)
                if inner or u + NB < U:
                    sp.wait_ge(score_made, (u + 1) * 2 * KT)
                    load(i, c + NB)

            steady(sp, step)
            for s in heads_out:
                sp.wait_ge(s, (U // NB) * 16)
            sp.wait_ge(heads_out[0], (U // NB + 1) * 16)
            sp.wait_ge(heads_out[1], (U // NB + 1) * 16)

        @block.gpsimd
        def _(pool):
            for i in range(NB):
                nc.gpsimd.memset(va[i][:, :, :, :], 0.0).then_inc(va_set, 1)
            pool.wait_ge(va_set, NB)
            for i in range(NB):
                nc.gpsimd.memset(va[i][:, :, :, DH:DH + 1], 1.0).then_inc(va_set, 1)
            pool.wait_ge(va_set, 2 * NB)
            for i in range(NB):
                if i:
                    pool.wait_ge(ones_set, i)
                nc.gpsimd.memset(ks[i][R:R + 2].bitcast(F32), 1.0).then_inc(ones_set, 1)
            pool.wait_ge(ones_set, NB)

            def values(i, c):
                u = 3 * i + c
                nc.gpsimd.tensor_copy(va[c % NB][:, :, :, 0:DH],
                                      V[:, bass.ds(u, 1), :, :].rearrange("p u k (h d) -> p (u k) h d", h=2)
                                      ).then_inc(va_ready, 1)

            for u in range(NB):
                values(0, u)

            def step(i, c, inner=False):
                u = 3 * i + c
                if inner or u + NB < U:
                    pool.wait_ge(pv_done, (u + 1) * KT)
                    values(i, c + NB)

            steady(pool, step)

        @block.scalar
        def _(act):
            def exps(i, c, k, first_ones):
                u = 3 * i + c
                for h in range(2):
                    act.wait_ge(score_made, u * 2 * KT + 2 * k + h + 1)
                    if not first_ones:
                        act.wait_ge(pv_done, u * KT + k - 1)
                    nc.scalar.activation(probs[(2 * k + h) % 4][:, :], score[h][:, :], ACT.Exp,
                                         scale=SCALE).then_inc(exp_done, 1)

            def take_out(i, c, first_one, inner=False):
                u = 3 * i + c
                act.wait_ge(pv_done, (u + 1) * KT)
                if not first_one:
                    act.wait_ge(ring_made, ready_out(i, c - 1, inner))
                nc.scalar.copy(osb[:, :], acc[:, :]).then_inc(osb_ready, 1)

            def step(i, c, inner=False):
                u = 3 * i + c
                if not inner and u == U:
                    take_out(i, c - 1, False)
                    return
                zero = not inner and u == 0
                for k in range(KT):
                    exps(i, c, k, zero and k < 2)
                    if k == 0 and not zero:
                        take_out(i, c - 1, not inner and u == 1, inner)
            step(0, 0)
            step(0, 1)
            with act.Fori(0, 8) as i:
                for c in (2, 3, 4):
                    step(i, c, True)
            for u in range(26, U + 1):
                step(0, u)

        @block.vector
        def _(dve):
            def reduce_first(at, p):
                for x in range(4):
                    n, bank = at(x)
                    dve.wait_ge(ring_made, n + 1)
                    nc.vector.tensor_reduce(pm[:, x // 2, p, x % 2:x % 2 + 1], bank[:, :], AX.X,
                                            ALU.max).then_inc(ring_read, 1)

            def largest(i, c, n):
                u = 3 * i + c
                dve.wait_ge(ring_read, n)
                nc.vector.tensor_reduce(mx[:, :].rearrange("p (h q) -> p h q", h=2), pm[:, :, :, :], AX.X,
                                        ALU.max).then_inc(mx_ready, 1)
                dve.wait_ge(mx_ready, u + 1)

            def negatives(i, c, where, first_one):
                u = 3 * i + c
                n, bank = where
                dve.wait_ge(ring_made, n + 1)
                if not first_one:
                    dve.wait_ge(rows_in[(c - 1) % NB], (i + (c - 1) // NB + 1) * 32)
                nc.vector.tensor_scalar(nhi[:, :], bank[0:2 * KT, 0:P], -1.0, None, ALU.mult).then_inc(nhi_ready, 1)
                dve.wait_ge(nhi_ready, u + 1)
                nc.vector.scalar_tensor_tensor(out=nlo[:, :], in0=bank[0:2 * KT, 0:P], scalar=-1.0,
                                               in1=nhi[:, :].bitcast(F32), op0=ALU.mult,
                                               op1=ALU.subtract).then_inc(ring_read, 1)

            def divide(i, c, where, first_ones=False):
                u = 3 * i + c
                n, bank = where
                link = Chain(dve, out_chain, u, 2)
                dve.wait_ge(ring_made, n + 1)
                if not first_ones:
                    dve.wait_ge(ring_read, n)
                out = bank[:, :].rearrange("p (j s c) -> p j s c", j=K4, s=4)
                link(nc.vector.reciprocal(rsum[:, :].rearrange("p (j s) -> p j s", s=4), out[:, :, :, DH]))
                inv = rsum[:, :].rearrange("p (j h q) -> p j h q", j=K4, h=2)
                if not first_ones:
                    dve.wait_ge(heads_out[c % NB], (i + c // NB) * 16)
                for q in range(2):
                    dst = heads[c % NB][:, q * K4:(q + 1) * K4, :].rearrange("p k (h d) -> p k h d", h=2)
                    ins = nc.vector.tensor_tensor(dst, out[:, :, q::2, 0:DH],
                                                  inv[:, :, :, q:q + 1].broadcast_to([P, K4, 2, DH]), ALU.mult)
                    if q == 0:
                        link(ins)
                    else:
                        ins.then_inc(ring_read, 1)
                link.close()

            def step(i, c, inner=False):
                u = 3 * i + c
                for k in range(KT):
                    p = k + LEAD
                    n = 1 if p < KT else 2
                    if inner or u + n < U:
                        reduce_first(lambda x, k=k: place(i, c, inner, ("one", k, x)), p % KT)
                    if p == KT - 1 and (inner or u + 1 < U):
                        largest(i, c + 1, place(i, c, inner, ("one", k, 3))[0] + 1)
                    if p == KT and (inner or u + 1 < U):
                        negatives(i, c + 1, place(i, c, inner, "max"), False)
                    if k == 2 and (inner or u >= 1):
                        divide(i, c - 1, place(i, c, inner, "out"), not inner and u <= NB)

            for p in range(KT):
                reduce_first(lambda x, p=p: (4 * p + x, ring[(4 * p + x) % 3]), p)
            largest(0, 0, 4 * KT)
            negatives(0, 0, (4 * KT, ring[4 * KT % 3]), True)
            for p in range(LEAD):
                reduce_first(lambda x, p=p: (4 * (KT + p) + 1 + x, ring[(4 * (KT + p) + 1 + x) % 3]), p)
            steady(dve, step, 1)

        @block.tensor
        def _(pe):
            pe.wait_ge(ident_in, 16)
            pe.wait_ge(ones_set, NB)

            def free(n):
                pe.wait_ge(ring_read, n - 2)

            def first_pass(i, c, p, x, where, fresh=False):
                n, bank = where
                if p == 0 and x == 0:
                    pe.wait_ge(loaded[c % NB], (i + c // NB + 1) * 8 * 16)
                if not fresh:
                    free(n)
                h, kh = x // 2, x % 2
                nc.tensor.matmul(bank[:, :], qs[c % NB][0:R, h, p * P:(p + 1) * P],
                                 ks[c % NB][0:R, h, kh * G:(kh + 1) * G], start=True, stop=True).then_inc(ring_made, 1)

            def turn_max(i, c, where):
                n, bank = where
                pe.wait_ge(mx_ready, 3 * i + c + 1)
                free(n)
                nc.tensor.transpose(bank[0:2 * KT, 0:P], mx[:, :], ident[:, :]).then_inc(ring_made, 1)

            def second_pass(i, c, k, h, first_ones):
                u = 3 * i + c
                if k == 0 and h == 0:
                    pe.wait_ge(rows_in[c % NB], (i + c // NB + 1) * 32)
                if not first_ones:
                    pe.wait_ge(exp_done, u * 2 * KT + 2 * (k - 1) + h + 1)
                for q in range(2):
                    mm = nc.tensor.matmul(score[h][:, q * G:(q + 1) * G], ks[c % NB][:, h, k * P:(k + 1) * P],
                                          qs[c % NB][:, h, q * G:(q + 1) * G], start=True, stop=True)
                mm.then_inc(score_made, 1)

            def products(i, c, k, first_unit):
                u = 3 * i + c
                pe.wait_ge(exp_done, u * 2 * KT + 2 * k + 2)
                if k == 0:
                    pe.wait_ge(va_ready, u + 1)
                    if not first_unit:
                        pe.wait_ge(osb_ready, u)
                for s in range(4):
                    h, q = s // 2, s % 2
                    mm = nc.tensor.matmul(acc[32 * s:32 * s + 32, :], va[c % NB][:, k, h, :],
                                          probs[(2 * k + h) % 4][:, q * G:(q + 1) * G],
                                          start=k == 0, stop=k == KT - 1)
                mm.then_inc(pv_done, 1)

            def turn_out(i, c, where):
                n, bank = where
                pe.wait_ge(osb_ready, 3 * i + c + 1)
                free(n)
                for j in range(K4):
                    mm = nc.tensor.transpose(bank[:, j * P:(j + 1) * P], osb[:, j * P:(j + 1) * P], ident[:, :])
                mm.then_inc(ring_made, 1)

            def step(i, c, inner=False):
                u = 3 * i + c
                zero = not inner and u == 0
                if not inner and u == U:
                    products(i, c - 1, KT - 1, False)
                    turn_out(i, c - 1, place(i, c, False, "out"))
                    return
                for k in range(KT):
                    p = k + LEAD
                    n = 1 if p < KT else 2
                    ahead = inner or u + n < U

                    def one(x):
                        if ahead:
                            first_pass(i, c + n, p % KT, x, place(i, c, inner, ("one", k, x)))
                    one(0)
                    second_pass(i, c, k, 0, zero and k == 0)
                    one(1)
                    second_pass(i, c, k, 1, zero and k == 0)
                    one(2)
                    if k > 0:
                        products(i, c, k - 1, zero)
                    elif not zero:
                        products(i, c - 1, KT - 1, False)
                    one(3)
                    if k == 2 and not zero:
                        turn_out(i, c - 1, place(i, c, inner, "out"))
                    if p == KT and (inner or u + 1 < U):
                        turn_max(i, c + 1, place(i, c, inner, "max"))

            for p in range(KT):
                for x in range(4):
                    first_pass(0, 0, p, x, (4 * p + x, ring[(4 * p + x) % 3]), 4 * p + x < 3)
            turn_max(0, 0, (4 * KT, ring[4 * KT % 3]))
            for p in range(LEAD):
                for x in range(4):
                    n = 4 * (KT + p) + 1 + x
                    first_pass(0, 1, p, x, (n, ring[n % 3]))
            steady(pe, step)


E_, HID = 8, 512
RMS_EPS = 1e-6


def split_weights(nc, tag, w, res):
    with Phase(nc, tag + "_sw") as ph:
        raw = [ph.sb(f"raw{i}", [P, 2048]) for i in range(2)]
        pieces = [(w["w2"][:, kc], [r[:, kc] for r in res["w2"]], 2048) for kc in range(HID // P)]
        pieces += [(w["w1"], res["w1"], 2048), (w["wso"], res["wso"], 1024)]
        came, hi_ready, lo_ready = [ph.sem("came0"), ph.sem("came1")], ph.sem("hi_ready"), ph.sem("lo_ready")
        block = ph.ctx.enter_context(nc.Block())

        def flat(a):
            return a.rearrange("p a b -> p (a b)") if len(a.shape) == 3 else a

        @block.sync
        def _(sp):
            for n, (src, _, width) in enumerate(pieces):
                if n >= 2:
                    sp.wait_ge(lo_ready, n - 1)
                sp.dma_start(raw[n % 2][:, 0:width], flat(src)).then_inc(came[n % 2], 16)

        @block.scalar
        def _(act):
            for n, (_, (hi, _), width) in enumerate(pieces):
                act.wait_ge(came[n % 2], 16 * (n // 2 + 1))
                nc.scalar.copy(flat(hi), raw[n % 2][:, 0:width]).then_inc(hi_ready, 1)

        @block.vector
        def _(dve):
            for n, (_, (hi, lo), width) in enumerate(pieces):
                dve.wait_ge(hi_ready, n + 1)
                nc.vector.tensor_tensor(flat(lo), raw[n % 2][:, 0:width], flat(hi).bitcast(F32),
                                        ALU.subtract).then_inc(lo_ready, 1)


def ffn_experts(nc, tag, x_d, src_d, heads_d, out_d, w, res):
    NP = 2 * HID // P
    IT = 1 + E_ // 2
    with Phase(nc, tag + "_fx") as ph:
        sb, ps, sem = ph.sb, ph.ps, ph.sem
        (w2h, w2l), (w1h, w1l), (wsoh, wsol) = res["w2"], res["w1"], res["wso"]
        wsh, wsl = sb("wsh", [P, CH, 2 * HID], F32R), sb("wsl", [P, CH, 2 * HID], F32R)
        gwh, gwl = sb("gwh", [P, CH, 10], F32R), sb("gwl", [P, CH, 10], F32R)
        graw = sb("graw", [P, CH, 10])
        wo, ident = sb("wo", [P, CH, C]), sb("ident", [P, P])
        n1w, n2w = sb("n1w", [P, C]), sb("n2w", [P, C])
        gbias, lower = sb("gbias", [P, 10]), sb("lower", [P, 64])
        hh, hl = sb("hh", [P, NP, G], F32R), sb("hl", [P, NP, G], F32R)
        xh, xl = sb("xh", [P, CH, G], F32R), sb("xl", [P, CH, G], F32R)
        sa = sb("sa", [P, K4, C])
        saT, src4 = sb("saT", [P, CH, G]), sb("src4", [P, K4, C])
        y4, x1, acc = sb("y4", [P, K4, C]), sb("x1", [P, K4, C]), sb("acc", [P, K4, C])
        x4 = sb("x4", [P, K4, C])
        th, tt, v = sb("th", [P, 2, G]), sb("tt", [P, G]), sb("v", [P, 2, G])
        sq = sb("sq", [P, C])
        ss1, ms1, r1 = sb("ss1", [P, K4]), sb("ms1", [P, K4]), sb("r1", [P, K4])
        ss2, ms2, r2 = sb("ss2", [P, K4]), sb("ms2", [P, K4]), sb("r2", [P, K4])
        nhalf = sb("nhalf", [P, K4])
        lg = sb("lg", [P, K4, 10])
        g1 = sb("g1", [P, K4])
        gd, eg, mask, pen = sb("gd", [P, K4, 2]), sb("eg", [P, K4, 2]), sb("mask", [P, K4, 2]), sb("pen", [P, K4, 2])
        gprob = sb("gprob", [P, K4])
        el, pe_ = sb("el", [P, K4, E_]), sb("pe", [P, K4, E_])
        beat, tie = sb("beat", [P, K4, 64]), sb("tie", [P, K4, 64])
        wt = sb("wt", [P, K4, E_])
        tp = ps("tp", [P, CH, G])
        hp = [ps(f"hp{i}", [P, 2, G]) for i in range(2)]
        ex = [ps(f"ex{i}", [P, G]) for i in range(2)]

        weights_in, raw_in, consts = sem("weights_in"), sem("raw_in"), sem("consts")
        ws_hi, ws_lo = sem("ws_hi"), sem("ws_lo")
        sa_in, src_in, x_in, out_done = sem("sa_in"), sem("src_in"), sem("x_in"), sem("out_done")
        sa_turned, saT_ready, wo_made, y_ready = sem("sa_turned"), sem("saT_ready"), sem("wo_made"), sem("y_ready")
        ss1_ready, ms1_ready, r1_ready, x1_ready = sem("ss1_ready"), sem("ms1_ready"), sem("r1_ready"), sem("x1_ready")
        x1_turned, xh_ready, xl_ready = sem("x1_turned"), sem("xh_ready"), sem("xl_ready")
        gate_made, gate_chain, gexp = sem("gate_made"), sem("gate_chain"), sem("gexp")
        pair_made, tanh_ready, pair_chain = sem("pair_made"), sem("tanh_ready"), sem("pair_chain")
        hh_ready, hl_ready = sem("hh_ready"), sem("hl_ready")
        acc_set, ex_made, ex_chain = sem("acc_set"), sem("ex_made"), sem("ex_chain")
        ss2_ready, ms2_ready, r2_ready, out_chain = sem("ss2_ready"), sem("ms2_ready"), sem("r2_ready"), sem("out_chain")
        NWD = 7
        GATE = 24
        EXC = K4 * (1 + E_)
        OUTC = K4 + 1

        block = ph.ctx.enter_context(nc.Block())

        def steps(eng, step):
            step(0, True, False)
            with eng.Fori(1, NG) as s:
                step(s, False, False)
            step(NG, False, True)

        @block.sync
        def _(sp):
            sp.dma_start(x4[:, :, :].rearrange("p a b -> p (a b)"),
                         w["wsi"][:, 0:1, :].rearrange("p a b -> p (a b)")).then_inc(raw_in, 16)
            sp.dma_start(y4[:, :, :].rearrange("p a b -> p (a b)"),
                         w["wsi"][:, 1:2, :].rearrange("p a b -> p (a b)")).then_inc(raw_in, 16)
            sp.dma_start(graw[:, :, :], w["wgate"]).then_inc(raw_in, 16)
            for dst, a in ((ident, w["ident"]), (wo, w["wo"].rearrange("(h p) f -> p h f", p=P)),
                           (n1w, w["n1w"].broadcast_to([P, C])), (n2w, w["n2w"].broadcast_to([P, C])),
                           (gbias[:, 0:2], w["gbias"].broadcast_to([P, 2])),
                           (gbias[:, 2:10], w["ebias"].broadcast_to([P, 8])),
                           (lower, w["lower"].broadcast_to([P, 64]))):
                sp.dma_start(dst[:], a).then_inc(weights_in, 16)

            def load_front(b, half, first):
                g = 2 * b + half
                if not first:
                    sp.wait_ge(sa_turned, g)
                for k in range(K4):
                    sp.dma_start(sa[:, k].rearrange("p (u c) -> p u c", u=8),
                                 heads_d[:, bass.ds(b * 8, 8), half * K4 + k, :]).then_inc(sa_in, 16)
                if not first:
                    sp.wait_ge(y_ready, 2 * g)
                sp.dma_start(src4[:, :, :], group_view(src_d, g)).then_inc(src_in, 16)

            def load_x(g, first):
                if first:
                    sp.wait_ge(ws_lo, CH)
                else:
                    sp.wait_ge(out_done, g * 16)
                sp.dma_start(x4[:, :, :], group_view(x_d, g)).then_inc(x_in, 16)

            def store(g):
                sp.wait_ge(out_chain, (g + 1) * OUTC)
                sp.dma_start(group_view(out_d, g), x4[:, :, :]).then_inc(out_done, 16)

            load_front(0, 0, True)
            load_x(0, True)
            load_front(0, 1, False)
            store(0)
            load_x(1, False)
            with sp.Fori(1, B) as b:
                load_front(b, 0, False)
                store(2 * b - 1)
                load_x(2 * b, False)
                load_front(b, 1, False)
                store(2 * b)
                load_x(2 * b + 1, False)
            store(NG - 1)
            sp.wait_ge(out_done, NG * 16)

        @block.gpsimd
        def _(pool):
            nc.gpsimd.memset(nhalf[:, :], -0.5).then_inc(consts, 1)
            pool.wait_ge(consts, 1)

            def step(s, first, last):
                if not last:
                    pool.wait_ge(ms1_ready, s + 1)
                    nc.gpsimd.tensor_tensor(r1[:, :], ms1[:, :], nhalf[:, :], ALU.pow).then_inc(r1_ready, 1)
                if not first:
                    pool.wait_ge(ms2_ready, s)
                    nc.gpsimd.tensor_tensor(r2[:, :], ms2[:, :], nhalf[:, :], ALU.pow).then_inc(r2_ready, 1)

            steps(pool, step)

        @block.scalar
        def _(act):
            act.wait_ge(raw_in, 48)
            nc.scalar.copy(wsh[:, 0], x4[:, :, :].rearrange("p a b -> p (a b)")).then_inc(ws_hi, 1)
            nc.scalar.copy(wsh[:, 1], y4[:, :, :].rearrange("p a b -> p (a b)")).then_inc(ws_hi, 1)
            nc.scalar.copy(gwh[:, :, :], graw[:, :, :]).then_inc(ws_hi, 1)

            def pair(s, n):
                act.wait_ge(pair_made, NP * s + n + 1)
                nc.scalar.activation(th[:, n % 2], hp[(n + 1) % 2][:, 0], ACT.Tanh, scale=0.5).then_inc(tanh_ready, 1)

            def hidden_hi(s, n, first):
                act.wait_ge(pair_chain, (s * NP + n + 1) * 2)
                if n == 0 and not first:
                    act.wait_ge(ex_made, s * K4 * IT)
                nc.scalar.copy(hh[:, n], v[:, n % 2]).then_inc(hh_ready, 1)

            def squares(src, ss, ready, wait):
                for k in range(K4):
                    wait(k)
                    if k:
                        act.wait_ge(ready[0], ready[1] + k)
                    nc.scalar.activation(sq[:, :], src[:, k], ACT.Square, accum_out=ss[:, k:k + 1]).then_inc(ready[0], 1)

            def step(s, first, last):
                if not last:
                    act.wait_ge(sa_turned, s + 1)
                    if not first:
                        act.wait_ge(wo_made, s)
                    nc.scalar.copy(saT[:, :, :], tp[:, :, :]).then_inc(saT_ready, 1)
                    squares(y4, ss1, (ss1_ready, s * K4), lambda k: act.wait_ge(y_ready, 2 * s + k // 2 + 1))
                    act.wait_ge(ss1_ready, (s + 1) * K4)
                if not first:
                    squares(acc, ss2, (ss2_ready, (s - 1) * K4),
                            lambda k: act.wait_ge(ex_chain, (s - 1) * EXC + (k + 1) * (1 + E_)))
                    act.wait_ge(ss2_ready, s * K4)
                if last:
                    return
                act.wait_ge(x1_turned, s + 1)
                if not first:
                    act.wait_ge(pair_made, NP * s)
                nc.scalar.copy(xh[:, :, :], tp[:, :, :]).then_inc(xh_ready, 1)
                for n in range(NP):
                    pair(s, n)
                    if n:
                        hidden_hi(s, n - 1, first)
                    if n == 1:
                        act.wait_ge(gate_chain, s * GATE + 3)
                        nc.scalar.activation(eg[:, :, :], gd[:, :, :], ACT.Exp).then_inc(gexp, 1)
                    if n == 3:
                        act.wait_ge(gate_chain, s * GATE + 14)
                        nc.scalar.activation(pe_[:, :, :], el[:, :, :], ACT.Exp).then_inc(gexp, 1)
                hidden_hi(s, NP - 1, first)

            steps(act, step)

        @block.vector
        def _(dve):
            for i, (hi, lo, raw) in enumerate(((wsh[:, 0], wsl[:, 0], x4), (wsh[:, 1], wsl[:, 1], y4))):
                dve.wait_ge(ws_hi, i + 1)
                nc.vector.tensor_tensor(lo, raw[:, :, :].rearrange("p a b -> p (a b)"), hi.bitcast(F32),
                                        ALU.subtract).then_inc(ws_lo, 1)
            dve.wait_ge(ws_hi, 3)
            nc.vector.tensor_tensor(gwl[:, :, :], graw[:, :, :], gwh[:, :, :].bitcast(F32), ALU.subtract).then_inc(ws_lo, 1)
            dve.wait_ge(ws_lo, 3)
            dve.wait_ge(weights_in, NWD * 16)

            def accumulate(link, k, g, items):
                for i in items:
                    n = k * IT + i
                    dve.wait_ge(ex_made, g * K4 * IT + n + 1)
                    bank = ex[n % 2]
                    if i == 0:
                        if k == 0:
                            dve.wait_ge(acc_set, g + 1)
                        link(nc.vector.tensor_tensor(acc[:, k], bank[:, 0:C], acc[:, k], ALU.add))
                    else:
                        for j in range(2):
                            e = 2 * (i - 1) + j
                            link(nc.vector.scalar_tensor_tensor(
                                out=acc[:, k], in0=bank[:, j * C:(j + 1) * C], scalar=wt[:, k, e:e + 1],
                                in1=acc[:, k], op0=ALU.mult, op1=ALU.add))

            def mean_square(ss, ms, ready):
                nc.vector.tensor_scalar(ms[:, :], ss[:, :], 1.0 / C, RMS_EPS, ALU.mult, ALU.add).then_inc(ready, 1)

            def bcast(a, n):
                return a.rearrange("p (k o) -> p k o", o=1).broadcast_to([P, K4, n])

            def gate(s):
                link = Chain(dve, gate_chain, s, GATE)
                dve.wait_ge(gate_made, s + 1)
                link(nc.vector.tensor_tensor(lg[:, :, :], tp[:, 0, 0:40].rearrange("p (k n) -> p k n", k=K4),
                                             gbias[:, :].rearrange("p (o n) -> p o n", o=1).broadcast_to([P, K4, 10]), ALU.add))
                link(nc.vector.tensor_reduce(g1[:, :], lg[:, :, 0:2], AX.X, ALU.max))
                link(nc.vector.tensor_tensor(gd[:, :, :], lg[:, :, 0:2], bcast(g1[:, :], 2), ALU.subtract))
                yield
                dve.wait_ge(gexp, 2 * s + 1)
                link(nc.vector.tensor_reduce(g1[:, :], eg[:, :, :], AX.X, ALU.add))
                link(nc.vector.reciprocal(g1[:, :], g1[:, :]))
                link(nc.vector.tensor_tensor(eg[:, :, :], eg[:, :, :], bcast(g1[:, :], 2), ALU.mult))
                link(nc.vector.tensor_reduce(gprob[:, :], eg[:, :, :], AX.X, ALU.max))
                link(nc.vector.tensor_tensor(mask[:, :, 0], eg[:, :, 0], eg[:, :, 1], ALU.is_ge))
                link(nc.vector.tensor_scalar(mask[:, :, 1], mask[:, :, 0], -1.0, 1.0, ALU.mult, ALU.add))
                link(nc.vector.tensor_scalar(pen[:, :, :], mask[:, :, :], -1.0, 1e30, ALU.add, ALU.mult))
                el4 = el[:, :, :].rearrange("p k (g e) -> p k g e", g=2)
                wide = [P, K4, 2, E_ // 2]
                m4, p4 = (a[:, :, :].rearrange("p k (g o) -> p k g o", o=1).broadcast_to(wide) for a in (mask, pen))
                link(nc.vector.tensor_tensor(el4, lg[:, :, 2:10].rearrange("p k (g e) -> p k g e", g=2), m4, ALU.mult))
                link(nc.vector.tensor_tensor(el4, el4, p4, ALU.add))
                link(nc.vector.tensor_reduce(g1[:, :], el[:, :, :], AX.X, ALU.max))
                link(nc.vector.tensor_tensor(el[:, :, :], el[:, :, :], bcast(g1[:, :], E_), ALU.subtract))
                yield
                dve.wait_ge(gexp, 2 * s + 2)
                link(nc.vector.tensor_reduce(g1[:, :], pe_[:, :, :], AX.X, ALU.add))
                link(nc.vector.reciprocal(g1[:, :], g1[:, :]))
                link(nc.vector.tensor_tensor(g1[:, :], g1[:, :], gprob[:, :], ALU.mult))
                link(nc.vector.tensor_tensor(pe_[:, :, :], pe_[:, :, :], bcast(g1[:, :], E_), ALU.mult))
                mine = pe_[:, :, :].rearrange("p k (e o) -> p k e o", o=1).broadcast_to([P, K4, E_, E_])
                other = pe_[:, :, :].rearrange("p k (o e) -> p k o e", o=1).broadcast_to([P, K4, E_, E_])
                b4, t4 = (a[:, :, :].rearrange("p k (e f) -> p k e f", e=E_) for a in (beat, tie))
                link.done(nc.vector.tensor_tensor(b4, other, mine, ALU.is_gt))
                link(nc.vector.tensor_tensor(t4, other, mine, ALU.is_equal))
                link(nc.vector.tensor_tensor(tie[:, :, :], tie[:, :, :],
                                             lower[:, :].rearrange("p (o n) -> p o n", o=1).broadcast_to([P, K4, 64]), ALU.mult))
                link(nc.vector.tensor_tensor(beat[:, :, :], beat[:, :, :], tie[:, :, :], ALU.add))
                link(nc.vector.tensor_reduce(wt[:, :, :], b4, AX.X, ALU.add))
                link(nc.vector.scalar_tensor_tensor(out=wt[:, :, :], in0=wt[:, :, :], scalar=2.0, in1=pe_[:, :, :],
                                                    op0=ALU.is_lt, op1=ALU.mult))
                link.close()
                yield

            def pair(s, n):
                link = Chain(dve, pair_chain, s * NP + n, 2)
                bank = hp[(n + 1) % 2]
                dve.wait_ge(tanh_ready, s * NP + n + 1)
                link(nc.vector.scalar_tensor_tensor(out=tt[:, :], in0=th[:, n % 2], scalar=1.0, in1=bank[:, 0],
                                                    op0=ALU.add, op1=ALU.mult))
                link(nc.vector.scalar_tensor_tensor(out=v[:, n % 2], in0=tt[:, :], scalar=0.5, in1=bank[:, 1],
                                                    op0=ALU.mult, op1=ALU.mult))

            def hidden_lo(s, n):
                dve.wait_ge(hh_ready, s * NP + n + 1)
                nc.vector.tensor_tensor(hl[:, n], v[:, n % 2], hh[:, n].bitcast(F32), ALU.subtract).then_inc(hl_ready, 1)

            def output(g):
                link = Chain(dve, out_chain, g, OUTC)
                dve.wait_ge(r2_ready, g + 1)
                for k in range(K4):
                    link.done(nc.vector.scalar_tensor_tensor(out=acc[:, k], in0=acc[:, k], scalar=r2[:, k:k + 1],
                                                             in1=n2w[:, :], op0=ALU.mult, op1=ALU.mult))
                link.wait()
                dve.wait_ge(x_in, (g + 1) * 16)
                link(nc.vector.tensor_tensor(x4[:, :, :], x4[:, :, :], acc[:, :, :], ALU.add))
                link.close()

            def step(s, first, last):
                ex_link = None if first else Chain(dve, ex_chain, s - 1, EXC)
                everything = range(IT)

                def experts(k, items=everything):
                    if not first:
                        accumulate(ex_link, k, s - 1, items)

                experts(0)
                experts(1)
                if not last:
                    dve.wait_ge(wo_made, s + 1)
                    dve.wait_ge(src_in, (s + 1) * 16)
                    for j in range(2):
                        nc.vector.tensor_tensor(y4[:, 2 * j:2 * j + 2].rearrange("p k c -> p (k c)"), hp[0][:, j],
                                                src4[:, 2 * j:2 * j + 2].rearrange("p k c -> p (k c)"), ALU.add
                                                ).then_inc(y_ready, 1)
                experts(2)
                if not last:
                    dve.wait_ge(ss1_ready, (s + 1) * K4)
                    mean_square(ss1, ms1, ms1_ready)
                experts(3, range(0, 3))
                if not last:
                    dve.wait_ge(r1_ready, s + 1)
                    for k in range(K4):
                        nc.vector.scalar_tensor_tensor(out=x1[:, k], in0=y4[:, k], scalar=r1[:, k:k + 1],
                                                       in1=n1w[:, :], op0=ALU.mult, op1=ALU.mult).then_inc(x1_ready, 1)
                experts(3, range(3, IT))
                if last:
                    dve.wait_ge(ss2_ready, s * K4)
                    mean_square(ss2, ms2, ms2_ready)
                    output(s - 1)
                    return
                dve.wait_ge(xh_ready, s + 1)
                nc.vector.tensor_tensor(xl[:, :, :], tp[:, :, :], xh[:, :, :].bitcast(F32), ALU.subtract).then_inc(xl_ready, 1)
                if not first:
                    dve.wait_ge(ss2_ready, s * K4)
                    mean_square(ss2, ms2, ms2_ready)
                parts = gate(s)
                pair(s, 0)
                next(parts)
                pair(s, 1)
                hidden_lo(s, 0)
                next(parts)
                pair(s, 2)
                hidden_lo(s, 1)
                pair(s, 3)
                hidden_lo(s, 2)
                next(parts)
                for n in range(4, NP):
                    pair(s, n)
                    hidden_lo(s, n - 1)
                    if n == 4:
                        if not first:
                            output(s - 1)
                        nc.vector.tensor_copy(acc[:, :, :], x1[:, :, :]).then_inc(acc_set, 1)
                hidden_lo(s, NP - 1)

            steps(dve, step)

        @block.tensor
        def _(pe):
            pe.wait_ge(weights_in, NWD * 16)
            pe.wait_ge(ws_lo, 3)

            def experts(g, k):
                t = slice(k * P, (k + 1) * P)
                for i in range(IT):
                    n = k * IT + i
                    if n >= 2:
                        m = n - 2
                        pe.wait_ge(ex_chain, g * EXC + (m // IT) * (1 + E_) + 1 + 2 * (m % IT))
                    out = ex[n % 2][:, 0:C] if i == 0 else ex[n % 2][:, :]
                    for kc in range(HID // P):
                        if i == 0:
                            c, wh, wl = kc + HID // P, wsoh[:, kc], wsol[:, kc]
                        else:
                            c, wh, wl = kc, w2h[:, kc, (i - 1) * G:i * G], w2l[:, kc, (i - 1) * G:i * G]
                        for j, (a, r) in enumerate(((hh, wh), (hh, wl), (hl, wh))):
                            mm = nc.tensor.matmul(out, a[:, c, t], r, start=kc == 0 and j == 0,
                                                  stop=kc == HID // P - 1 and j == 2)
                    mm.then_inc(ex_made, 1)

            def turn_sa(s, first):
                pe.wait_ge(sa_in, (s + 1) * K4 * 16)
                if not first:
                    pe.wait_ge(gate_chain, (s - 1) * GATE + 1)
                for k in range(K4):
                    for h in range(CH):
                        mm = nc.tensor.transpose(tp[:, h, k * P:(k + 1) * P],
                                                 sa[:, k, h * P:(h + 1) * P], ident[:, :])
                mm.then_inc(sa_turned, 1)

            def project(s, first):
                pe.wait_ge(saT_ready, s + 1)
                if not first:
                    pe.wait_ge(pair_chain, s * NP * 2)
                for k in range(K4):
                    for h in range(CH):
                        mm = nc.tensor.matmul(hp[0][:, k // 2, (k % 2) * C:(k % 2 + 1) * C], saT[:, h, k * P:(k + 1) * P],
                                              wo[:, h, :], start=h == 0, stop=h == CH - 1)
                mm.then_inc(wo_made, 1)

            def turn_x1(s):
                pe.wait_ge(x1_ready, (s + 1) * K4)
                for k in range(K4):
                    for h in range(CH):
                        mm = nc.tensor.transpose(tp[:, h, k * P:(k + 1) * P], x1[:, k, h * P:(h + 1) * P], ident[:, :])
                mm.then_inc(x1_turned, 1)

            def gate(s):
                pe.wait_ge(xl_ready, s + 1)
                for k in range(K4):
                    t = slice(k * P, (k + 1) * P)
                    for h in range(CH):
                        for j, (a, r) in enumerate(((xh, gwh), (xh, gwl), (xl, gwh), (xl, gwl))):
                            mm = nc.tensor.matmul(tp[:, 0, k * 10:(k + 1) * 10], a[:, h, t], r[:, h, :],
                                                  start=h == 0 and j == 0, stop=h == CH - 1 and j == 3)
                mm.then_inc(gate_made, 1)

            def pair(s, n, first):
                if n == 0:
                    if not first:
                        pe.wait_ge(pair_chain, (s * NP - 1) * 2)
                elif n == 1:
                    pe.wait_ge(y_ready, 2 * (s + 1))
                else:
                    pe.wait_ge(pair_chain, (s * NP + n - 1) * 2)
                wh, wl = (w1h, w1l) if n < NP // 2 else (wsh, wsl)
                m = n % (NP // 2)
                for j in range(2):
                    f = slice(j * HID + m * P, j * HID + (m + 1) * P)
                    for h in range(CH):
                        for i, (a, x) in enumerate(((wh, xh), (wh, xl), (wl, xh))):
                            mm = nc.tensor.matmul(hp[(n + 1) % 2][:, j], a[:, h, f], x[:, h], start=h == 0 and i == 0,
                                                  stop=h == CH - 1 and i == 2)
                mm.then_inc(pair_made, 1)

            def step(s, first, last):
                if not first:
                    pe.wait_ge(hl_ready, s * NP)
                    experts(s - 1, 0)
                if not last:
                    turn_sa(s, first)
                if not first:
                    experts(s - 1, 1)
                if not last:
                    project(s, first)
                if not first:
                    experts(s - 1, 2)
                    experts(s - 1, 3)
                if last:
                    return
                turn_x1(s)
                gate(s)
                for n in range(NP):
                    pair(s, n, first)

            steps(pe, step)


def relative_attention(nc, x_d, out_d, w):
    H, FE = 8, 128
    NJ = T // P
    FW = H * FE
    PAIRS = [(i, k) for k in range(B) for i in range(k + 1)]
    NPROD = 5
    SCALE = 1.0 / C ** 0.5
    with Phase(nc, "ra") as ph:
        sb, ps, sem = ph.sb, ph.ps, ph.sem
        x4, xf = sb("x4", [P, B, C]), sb("xf", [P, B, C])
        stats, mv = sb("stats", [P, K4, 6]), sb("mv", [P, K4, 2])
        var, rstd, nhalf = sb("var", [P, K4]), sb("rstd", [P, K4]), sb("nhalf", [P, K4])
        h0, h1, h = sb("h0", [P, B, C]), sb("h1", [P, B, C]), sb("h", [P, B, C])
        ident, gamma, beta, bout = sb("ident", [P, P]), sb("gamma", [P, C]), sb("beta", [P, C]), sb("bout", [P, C])
        wqh, wql = sb("wqh", [P, CH, FW], F32R), sb("wql", [P, CH, FW], F32R)
        wvh, wvl = sb("wvh", [P, CH, FW], F32R), sb("wvl", [P, CH, FW], F32R)
        woh, wol = sb("woh", [P, H, C], F32R), sb("wol", [P, H, C], F32R)
        w5, w5h, w5l = sb("w5", [P, CH, H * 5]), sb("w5h", [P, CH, H * 5], F32R), sb("w5l", [P, CH, H * 5], F32R)
        pe_t, r5, ub, vb = sb("pe_t", [P, CH, B]), sb("r5", [P, H, 5]), sb("ub", [P, H]), sb("vb", [P, H])
        vr, ones, vrow = sb("vr", [P, H, B]), sb("ones", [P, P]), sb("vrow", [P, H, 5])
        tril = sb("tril", [P, NJ, H])
        hTh, hTl = sb("hTh", [P, CH, G], F32R), sb("hTl", [P, CH, G], F32R)
        q, o = sb("q", [P, B, FW]), sb("o", [P, B, FW])
        v = [sb(f"v{i}", [P, B, FW]) for i in range(2)]
        prod = [sb(f"prod{i}", [P, FW]) for i in range(NPROD)]
        posq = sb("posq", [P, B, H, 5])
        pad = sb("pad", [P, 5 * B, H])
        dots, sc = sb("dots", [P, B * B, H]), sb("sc", [P, B * B, H])
        mx = sb("mx", [P, B, H])
        oTh = [sb(f"oTh{i}", [P, H, P], F32R) for i in range(2)]
        oTl = [sb(f"oTl{i}", [P, H, P], F32R) for i in range(2)]
        tp = ps("tp", [P, 1024])
        ring = [ps(f"ring{i}", [P, FW]) for i in range(2)]
        pos_ps, out_ps = ps("pos", [P, B, H * 5]), ps("out", [P, C])

        weights_in, consts = sem("weights_in"), sem("consts")
        raw_in, split_hi, split_lo = sem("raw_in"), sem("split_hi"), sem("split_lo")
        prep_pe, prep = sem("prep_pe"), sem("prep")
        x_in, xf_in, stored = sem("x_in"), sem("xf_in"), sem("stored")
        ln1_chain, ln2_chain, var_ready, rstd_ready = sem("ln1_chain"), sem("ln2_chain"), sem("var_ready"), sem("rstd_ready")
        var2_ready, rstd2_ready = sem("var2_ready"), sem("rstd2_ready")
        h_ready, turned, hTh_ready, hTl_ready = sem("h_ready"), sem("turned"), sem("hTh_ready"), sem("hTl_ready")
        q_made, q_ready, v_made, v_ready, pos_made = sem("q_made"), sem("q_ready"), sem("v_made"), sem("v_ready"), sem("pos_made")
        prod_ready, dot_ready, soft_chain, exp_ready = sem("prod_ready"), sem("dot_ready"), sem("soft_chain"), sem("exp_ready")
        o_begun = sem("o_begun")
        o_chain, o_turned, oTh_ready, oTl_ready = sem("o_chain"), sem("o_turned"), sem("oTh_ready"), sem("oTl_ready")
        out_made, final_chain = sem("out_made"), sem("final_chain")
        ND = len(PAIRS)
        SOFT = 15
        AT_EXP = 12
        OC = (B - 1) * H

        block = ph.ctx.enter_context(nc.Block())

        def rows(dram, j):
            return dram.rearrange("(b t) c -> t b c", b=B)[bass.ds(j * P, P)]

        def flat(a):
            return a.rearrange("p a b -> p (a b)")

        def steps(eng, step):
            step(0, 0, True, True, True)
            step(1, 1, False, True, True)
            with eng.Fori(1, NJ // 2 - 1) as half:
                for i in range(2):
                    step(2 * half + i, i, False, True, True)
            step(NJ - 2, 0, False, True, False)
            step(NJ - 1, 1, False, False, False)

        raws = [(w["b_wq"], wqh, wql, q), (w["b_wv"], wvh, wvl, v[0]), (w["b_wout"], woh, wol, o)]

        @block.sync
        def _(sp):
            for src, _, _, stage in raws:
                sp.dma_start(flat(stage[:, 0:2, :]), flat(src)).then_inc(raw_in, 16)
            sp.dma_start(flat(q[:, 2:4, :]), flat(w["b_wr"])).then_inc(raw_in, 16)
            sp.dma_start(flat(v[0][:, 2:4, :]), flat(w["b_wqt"])).then_inc(raw_in, 16)
            for dst, a in ((ident, w["ident"]), (gamma, w["gamma"].broadcast_to([P, C])),
                           (beta, w["beta"].broadcast_to([P, C])), (bout, w["bout"].broadcast_to([P, C])),
                           (pe_t, w["pe_t"]), (ub, w["u_t"]), (vb, w["v_t"]), (tril, w["tril"])):
                sp.dma_start(dst[:], a).then_inc(weights_in, 16)

            def load(j):
                sp.dma_start(x4[:, :, :], rows(x_d, j)).then_inc(x_in, 16)

            load(0)
            sp.wait_ge(ln1_chain, LN_LINKS)
            load(1)

            def step(j, par, first, more, more2):
                if not first:
                    sp.wait_ge(stored, j * 16)
                sp.dma_start(xf[:, :, :], rows(x_d, j)).then_inc(xf_in, 16)
                if more2:
                    sp.wait_ge(ln1_chain, (j + 2) * LN_LINKS)
                    load(j + 2)
                sp.wait_ge(final_chain, (j + 1) * (B + 1))
                sp.dma_start(rows(out_d, j), xf[:, :, :]).then_inc(stored, 16)

            steps(sp, step)
            sp.wait_ge(stored, NJ * 16)

        @block.gpsimd
        def _(pool):
            nc.gpsimd.memset(nhalf[:, :], -0.5).then_inc(consts, 1)
            nc.gpsimd.memset(ones[:, :], 1.0).then_inc(consts, 1)
            pool.wait_ge(consts, 2)
            nc.gpsimd.memset(pad[:, :, :], 0.0).then_inc(consts, 1)
            pool.wait_ge(weights_in, 8 * 16)

            def norms(j, first):
                pool.wait_ge(var_ready, j + 1)
                nc.gpsimd.tensor_tensor(rstd[:, :], var[:, :], nhalf[:, :], ALU.pow).then_inc(rstd_ready, 1)
                pool.wait_ge(var2_ready, j + 1)
                nc.gpsimd.tensor_tensor(rstd[:, :], var[:, :], nhalf[:, :], ALU.pow).then_inc(rstd2_ready, 1)
                pool.wait_ge(ln2_chain, (j + 1) * LN_LINKS)
                if not first:
                    pool.wait_ge(turned, j)
                for n, (par, op) in enumerate(((gamma, ALU.mult), (beta, ALU.add))):
                    nc.gpsimd.tensor_tensor(h[:, :, :], h1[:, :, :] if n == 0 else h[:, :, :],
                                            par[:, :].rearrange("p (o c) -> p o c", o=1).broadcast_to([P, B, C]),
                                            op).then_inc(h_ready, 1)
                    pool.wait_ge(h_ready, 2 * j + n + 1)

            def products(j, first, items=range(ND)):
                for n in items:
                    i, k = PAIRS[n]
                    if i == 0:
                        pool.wait_ge(q_ready, j * B + k + 1)
                    if not (first and n < NPROD):
                        pool.wait_ge(dot_ready, j * ND + n - NPROD + 1)
                    nc.gpsimd.tensor_tensor(prod[n % NPROD][:, :], q[:, i], q[:, k], ALU.mult).then_inc(prod_ready, 1)

            norms(0, True)
            norms(1, False)
            products(0, True)

            def step(j, par, first, more, more2):
                if more:
                    products(j + 1, False, range(0, NPROD))
                if more2:
                    norms(j + 2, False)
                if more:
                    products(j + 1, False, range(NPROD, ND))

            steps(pool, step)

        @block.scalar
        def _(act):
            for n, (_, hi, _, stage) in enumerate(raws):
                act.wait_ge(raw_in, 5 * 16)
                nc.scalar.copy(flat(hi[:, :, :]), flat(stage[:, 0:2, :])).then_inc(split_hi, 1)
            act.wait_ge(prep, 6)
            nc.scalar.copy(flat(w5h[:, :, :]), flat(w5[:, :, :])).then_inc(split_hi, 1)

            def turned_in(j, first):
                act.wait_ge(turned, j + 1)
                if not first:
                    act.wait_ge(v_made, j * B)
                nc.scalar.copy(flat(hTh[:, :, :]), tp[:, :]).then_inc(hTh_ready, 1)

            def take(j, made, ready, dst, free, batches=range(B)):
                for b in batches:
                    act.wait_ge(made, j * B + b + 1)
                    if b == 0 and free:
                        act.wait_ge(*free)
                    nc.scalar.copy(dst[:, b], ring[b % 2][:, :]).then_inc(ready, 1)

            def begin(j, par, i, first):
                if i == 0:
                    act.wait_ge(soft_chain, (j + 1) * SOFT)
                    act.wait_ge(v_ready, (j + 1) * B)
                if not first:
                    act.wait_ge(o_turned, (j - 1) * B + i + 1)
                for n in range(H):
                    f = slice(n * FE, (n + 1) * FE)
                    ins = nc.scalar.activation(o[:, i, f], v[par][:, 0, f], ACT.Copy, scale=sc[:, i * B, n:n + 1])
                ins.then_inc(o_begun, 1)

            turned_in(0, True)
            act.wait_ge(split_lo, 4)
            act.wait_ge(prep, 6)
            take(0, q_made, q_ready, q, None)
            take(0, v_made, v_ready, v[0], None)

            def step(j, par, first, more, more2):
                if more:
                    turned_in(j + 1, False)
                act.wait_ge(soft_chain, j * SOFT + AT_EXP)
                nc.scalar.activation(sc[:, :, :], sc[:, :, :], ACT.Exp, scale=SCALE).then_inc(exp_ready, 1)
                for i in range(B):
                    begin(j, par, i, first)
                    if more:
                        take(j + 1, q_made, q_ready, q, (prod_ready, (j + 1) * ND), (i,))
                for b in range(B):
                    act.wait_ge(o_turned, j * B + b + 1)
                    if not (first and b < 2):
                        act.wait_ge(out_made, j * B + b - 1)
                    nc.scalar.copy(flat(oTh[b % 2][:, :, :]), tp[:, :]).then_inc(oTh_ready, 1)
                    if more:
                        take(j + 1, v_made, v_ready, v[1 - par], None if first else (o_chain, j * B * OC), (b,))

            steps(act, step)

        @block.vector
        def _(dve):
            dve.wait_ge(weights_in, 8 * 16)
            link = Chain(dve, prep, 0, 8)
            for n, (_, hi, lo, stage) in enumerate(raws):
                dve.wait_ge(split_hi, n + 1)
                nc.vector.tensor_tensor(flat(lo[:, :, :]), flat(stage[:, 0:2, :]), flat(hi[:, :, :]).bitcast(F32),
                                        ALU.subtract).then_inc(split_lo, 1)
            dve.wait_ge(prep_pe, 1)
            link.done(nc.vector.tensor_copy(r5[:, :, 0:4], pos_ps[:, 0, 0:32].rearrange("p (h j) -> p h j", h=H)))
            link(nc.vector.tensor_copy(r5[:, :, 4], ub[:, :]))
            link(nc.vector.tensor_tensor(vr[:, :, :], r5[:, :, 0:4],
                                         vb[:, :].rearrange("p (h o) -> p h o", o=1).broadcast_to([P, H, B]), ALU.mult))
            link(nc.vector.memset(vrow[:, :, :], 0.0))
            dve.wait_ge(prep_pe, 2)
            link(nc.vector.tensor_copy(vrow[:, :, 0:4], out_ps[:, 0:32].rearrange("p (h j) -> p h j", h=H)))
            dve.wait_ge(prep_pe, 3)
            link(nc.vector.tensor_copy(flat(w5[:, :, :]), flat(pos_ps[:, 0:CH, :])))
            dve.wait_ge(split_hi, 4)
            nc.vector.tensor_tensor(flat(w5l[:, :, :]), flat(w5[:, :, :]), flat(w5h[:, :, :]).bitcast(F32),
                                    ALU.subtract).then_inc(split_lo, 1)
            dve.wait_ge(consts, 3)

            def norms(j, first):
                dve.wait_ge(x_in, (j + 1) * 16)
                normalize_group(dve, nc, j, ln1_chain, var_ready, rstd_ready, x4, stats, mv, var, rstd, h0)
                if not first:
                    dve.wait_ge(h_ready, 2 * j)
                normalize_group(dve, nc, j, ln2_chain, var2_ready, rstd2_ready, h0, stats, mv, var, rstd, h1)

            def turned_lo(j):
                dve.wait_ge(hTh_ready, j + 1)
                nc.vector.tensor_tensor(flat(hTl[:, :, :]), tp[:, :], flat(hTh[:, :, :]).bitcast(F32),
                                        ALU.subtract).then_inc(hTl_ready, 1)

            def dot(j, items):
                for n in items:
                    i, k = PAIRS[n]
                    dve.wait_ge(prod_ready, j * ND + n + 1)
                    nc.vector.tensor_reduce(dots[:, i * B + k], prod[n % NPROD][:, :].rearrange("p (h f) -> p h f", h=H),
                                            AX.X, ALU.add).then_inc(dot_ready, 1)

            def scores(j):
                link = Chain(dve, soft_chain, j, SOFT)
                dve.wait_ge(dot_ready, (j + 1) * ND)
                for dst, src in ((slice(4, 13, 4), slice(1, 4)), (slice(9, 14, 4), slice(6, 8)), (slice(14, 15), slice(11, 12))):
                    link.done(nc.vector.tensor_copy(dots[:, dst], dots[:, src]))
                dve.wait_ge(pos_made, j + 1)
                link(nc.vector.tensor_tensor(posq[:, :, :, :].rearrange("p b h e -> p b (h e)"), pos_ps[:, :, :],
                                             vrow[:, :, :].rearrange("p (o h) e -> p o (h e)", o=1).broadcast_to([P, B, H * 5]), ALU.add))
                pad4 = pad[:, :, :].rearrange("p (i j) h -> p i j h", i=B)
                mask = tril[:, bass.ds(j, 1), :].broadcast_to([P, B, H])
                for i in range(B):
                    ins = nc.vector.tensor_tensor(pad4[:, i, 1:5], posq[:, i, :, 0:4].rearrange("p h e -> p e h"), mask, ALU.mult)
                    link.done(ins) if i < B - 1 else link(ins)
                link(nc.vector.tensor_tensor(sc[:, :, :], dots[:, :, :], pad[:, 4:20, :], ALU.add))
                return link

            def step(j, par, first, more, more2):
                link = scores(j)
                sc4 = sc[:, :, :].rearrange("p (i k) h -> p i k h", i=B)
                over_k = sc[:, :, :].rearrange("p (i k) h -> p i h k", i=B)
                uq = posq[:, :, :, 4].rearrange("p (o k) h -> p o k h", o=1).broadcast_to([P, B, B, H])
                mxb = mx[:, :, :].rearrange("p i (o h) -> p i o h", o=1).broadcast_to([P, B, B, H])
                link(nc.vector.tensor_tensor(sc4, sc4, uq, ALU.add))
                link(nc.vector.tensor_reduce(mx[:, :, :], over_k, AX.X, ALU.max))
                link(nc.vector.tensor_tensor(sc4, sc4, mxb, ALU.subtract))
                if more:
                    turned_lo(j + 1)
                dve.wait_ge(exp_ready, j + 1)
                link(nc.vector.tensor_reduce(mx[:, :, :], over_k, AX.X, ALU.add))
                link(nc.vector.reciprocal(mx[:, :, :], mx[:, :, :]))
                link(nc.vector.tensor_tensor(sc4, sc4, mxb, ALU.mult))
                link.close()
                dve.wait_ge(v_ready, (j + 1) * B)
                dve.wait_ge(xf_in, (j + 1) * 16)
                fin = Chain(dve, final_chain, j, B + 1)
                fin(nc.vector.tensor_tensor(xf[:, :, :], xf[:, :, :],
                                            bout[:, :].rearrange("p (o c) -> p o c", o=1).broadcast_to([P, B, C]), ALU.add))
                for i in range(B):
                    ol = Chain(dve, o_chain, j * B + i, OC)
                    dve.wait_ge(o_begun, j * B + i + 1)
                    for k in range(1, B):
                        for n in range(H):
                            f = slice(n * FE, (n + 1) * FE)
                            p1 = sc[:, i * B + k, n:n + 1]
                            ol.done(nc.vector.scalar_tensor_tensor(out=o[:, i, f], in0=v[par][:, k, f], scalar=p1,
                                                                   in1=o[:, i, f], op0=ALU.mult, op1=ALU.add))
                        ol.wait()
                        if more:
                            at = (i - 1) * 3 + k - 1
                            if at in (0, 2, 4, 5, 7):
                                dot(j + 1, [(0, 2, 4, 5, 7).index(at)])
                    ol.close()
                    if i >= 1:
                        lo_part(j, i - 1, first)
                    if i >= 2:
                        final(j, i - 2, fin)
                    if i == 1 and more2:
                        norms(j + 2, False)
                if more:
                    dot(j + 1, range(5, 7))
                lo_part(j, 3, first)
                final(j, 2, fin)
                if more:
                    dot(j + 1, range(7, ND))
                final(j, 3, fin)

            def lo_part(j, i, first):
                dve.wait_ge(oTh_ready, j * B + i + 1)
                nc.vector.tensor_tensor(flat(oTl[i % 2][:, :, :]), tp[:, :], flat(oTh[i % 2][:, :, :]).bitcast(F32),
                                        ALU.subtract).then_inc(oTl_ready, 1)

            def final(j, i, fin):
                dve.wait_ge(out_made, j * B + i + 1)
                fin(nc.vector.tensor_tensor(xf[:, i], xf[:, i], out_ps[:, :], ALU.add))

            norms(0, True)
            turned_lo(0)
            norms(1, False)
            dot(0, range(ND))
            steps(dve, step)

        @block.tensor
        def _(pe):
            pe.wait_ge(raw_in, 5 * 16)
            pe.wait_ge(weights_in, 8 * 16)
            wr, wqt = q[:, 2:4, :], v[0][:, 2:4, :].rearrange("p a (n c) -> p (a n) c", c=C)
            for n in range(H):
                for hf in range(CH):
                    mm = nc.tensor.matmul(pos_ps[:, 0, n * 4:(n + 1) * 4], wr[:, hf, n * FE:(n + 1) * FE], pe_t[:, hf, :],
                                          start=hf == 0, stop=hf == CH - 1)
            mm.then_inc(prep_pe, 1)
            pe.wait_ge(consts, 2)
            pe.wait_ge(prep, 3)
            nc.tensor.matmul(out_ps[:, 0:32], ones[:, :], vr[:, :, :].rearrange("p h j -> p (h j)"), start=True,
                             stop=True).then_inc(prep_pe, 1)
            for hf in range(CH):
                for n in range(H):
                    mm = nc.tensor.matmul(pos_ps[:, hf, n * 5:(n + 1) * 5], wqt[:, n, hf * P:(hf + 1) * P], r5[:, n, :],
                                          start=True, stop=True)
            mm.then_inc(prep_pe, 1)
            pe.wait_ge(split_lo, 4)
            pe.wait_ge(prep, 6)

            def turn(j, free):
                pe.wait_ge(h_ready, 2 * (j + 1))
                if free:
                    pe.wait_ge(*free)
                for k in range(B):
                    for hf in range(CH):
                        mm = nc.tensor.transpose(tp[:, hf * G + k * P:hf * G + (k + 1) * P], h[:, k, hf * P:(hf + 1) * P], ident[:, :])
                mm.then_inc(turned, 1)

            def three(out, lhs, rhs, first, last):
                (lh, ll), (rh, rl) = lhs, rhs
                for n, (a, r) in enumerate(((lh, rh), (lh, rl), (ll, rh))):
                    mm = nc.tensor.matmul(out, a, r, start=first and n == 0, stop=last and n == 2)
                return mm

            def project(j, wh, wl, made, free, batches=range(B)):
                for b in batches:
                    t = slice(b * P, (b + 1) * P)
                    free(b)
                    for cc in range(2):
                        f = slice(cc * G, (cc + 1) * G)
                        for hf in range(CH):
                            mm = three(ring[b % 2][:, f], (hTh[:, hf, t], hTl[:, hf, t]), (wh[:, hf, f], wl[:, hf, f]),
                                       hf == 0, hf == CH - 1)
                    mm.then_inc(made, 1)

            def queries(j, first):
                pe.wait_ge(hTl_ready, j + 1)

                def free(b):
                    if b >= 2:
                        pe.wait_ge(q_ready, j * B + b - 1)
                    elif not first:
                        pe.wait_ge(v_ready, (j - 1) * B + b + 3)
                project(j, wqh, wql, q_made, free)
                if not first:
                    pe.wait_ge(soft_chain, (j - 1) * SOFT + 4)
                for b in range(B):
                    t = slice(b * P, (b + 1) * P)
                    for hf in range(CH):
                        for n, (a, r) in enumerate(((hTh, w5h), (hTh, w5l), (hTl, w5h), (hTl, w5l))):
                            mm = nc.tensor.matmul(pos_ps[:, b, :], a[:, hf, t], r[:, hf, :], start=hf == 0 and n == 0,
                                                  stop=hf == CH - 1 and n == 3)
                mm.then_inc(pos_made, 1)

            def values(j, batches=range(B)):
                def free(b):
                    if b >= 2:
                        pe.wait_ge(v_ready, j * B + b - 1)
                    else:
                        pe.wait_ge(q_ready, j * B + b + 3)
                project(j, wvh, wvl, v_made, free, batches)

            def output(j, first, more):
                for i in range(B):
                    pe.wait_ge(o_chain, (j * B + i + 1) * OC)
                    if i == 0:
                        if more:
                            pe.wait_ge(hTl_ready, j + 2)
                        elif not first:
                            pe.wait_ge(oTl_ready, j * B)
                    else:
                        pe.wait_ge(oTl_ready, j * B + i)
                    for n in range(H):
                        mm = nc.tensor.transpose(tp[:, n * P:(n + 1) * P], o[:, i, n * FE:(n + 1) * FE], ident[:, :])
                    mm.then_inc(o_turned, 1)
                    if more:
                        values(j + 1, (i,))
                    if i > 0:
                        product(j, i - 1, first)
                product(j, B - 1, first)

            def product(j, i, first):
                pe.wait_ge(oTl_ready, j * B + i + 1)
                if not (first and i == 0):
                    pe.wait_ge(final_chain, j * (B + 1) + i + (0 if i == 0 else 1))
                for n in range(H):
                    mm = three(out_ps[:, :], (oTh[i % 2][:, n], oTl[i % 2][:, n]), (woh[:, n], wol[:, n]), n == 0, n == H - 1)
                mm.then_inc(out_made, 1)

            turn(0, None)
            queries(0, True)
            values(0)

            def step(j, par, first, more, more2):
                if more:
                    turn(j + 1, (hTl_ready, 1) if first else (oTl_ready, j * B))
                    queries(j + 1, False)
                output(j, first, more)

            steps(pe, step)


def transformer(nc, x_d, out_d, w):
    def scratch(name, shape):
        return nc.dram_tensor(name, shape, F32, kind="Internal").ap()

    q_d, ctx_d = scratch("lin_q", [N, C]), scratch("lin_sums", [P, B * CH, P + 8])
    src_d, qk_d, heads_d = scratch("ffn_src", [N, C]), scratch("ffn_qk", [4, N // (T // C), T]), scratch("ffn_heads", [P, 32, 8, 32])
    xa_d, xb_d, xc_d = (scratch(n, [N, C]) for n in ("after_linear", "after_ffn", "after_relative"))

    linear_keys(nc, x_d, q_d, ctx_d, w)
    linear_mix(nc, x_d, q_d, ctx_d, xa_d, w)
    feed_forward(nc, "f1", xa_d, xb_d, src_d, qk_d, heads_d, w)
    relative_attention(nc, xb_d, xc_d, w)
    feed_forward(nc, "f2", xc_d, out_d, src_d, qk_d, heads_d, w)


def feed_forward(nc, tag, x_d, out_d, src_d, qk_d, heads_d, w):
    with nc.sbuf_tensor(f"{tag}_values", [P, 32, 8, 32], F32) as V:
        ffn_project(nc, tag, x_d, src_d, qk_d, V, w)
        ffn_attend(nc, tag, qk_d, V, heads_d, w)
    with ExitStack() as ctx:
        parts = {name: [ctx.enter_context(nc.sbuf_tensor(f"{tag}_{name}_{half}", shape, F32R))[:, :, :] for half in ("hi", "lo")]
                 for name, shape in (("w2", [P, 4, 8 * C]), ("w1", [P, CH, 1024]), ("wso", [P, 4, C]))}
        split_weights(nc, tag, w, parts)
        ffn_experts(nc, tag, x_d, src_d, heads_d, out_d, w, parts)


def lay_out(inputs):
    a = {name[3:]: np.asarray(v) for name, v in inputs.items()}

    def rows(m):
        return m.reshape(-1, P, m.shape[-1]).transpose(1, 0, 2)

    head = np.arange(P) // DH
    inv_freq = (1.0 / 10000.0 ** (np.arange(0, DH, 2, dtype=np.float32) / np.float32(DH))).astype(np.float32)
    angle = (np.arange(T, dtype=np.float32)[:, None] * inv_freq[None]).T[(np.arange(P) % DH) // 2]
    sign = np.where(np.arange(P) % 2 == 0, -1, 1)[:, None]
    partner = np.arange(C) ^ 1
    pos = np.arange(B, dtype=np.float32)[::-1, None]
    div = np.exp(np.arange(0, C, 2, dtype=np.float32) * np.float32(-math.log(10000.0) / C))
    pe = np.stack([np.sin(pos * div), np.cos(pos * div)], -1).reshape(B, C)
    token = np.arange(T).reshape(T // P, P).T
    f, g, h = "ffn_", "attn_b_", "attn_a_"
    out = dict(
        x=a["attn_a_x"].reshape(N, C), ident=np.eye(P),
        qkv=np.stack([a[h + n].T for n in ("Wq", "Wk", "Wv")]),
        qkv_bias=np.concatenate([a[h + n] for n in ("bq", "bk", "bv")])[None],
        block_mask=head[:, None] == head[None], head_mask=head[:, None] == np.arange(8)[None],
        wpt=a[h + "Wp"].T, bp=a[h + "bp"][None],
        cos=np.cos(angle), sin=np.sin(angle) * sign,
        wq=a[f + "Wq"], wqs=a[f + "Wq"][:, partner], wkc=a[f + "Wk_c"], wvc=a[f + "Wv_c"],
        wk=a[f + "Wk"], wks=a[f + "Wk"][:, partner], wv=a[f + "Wv"], wo=a[f + "Wo"],
        w2=rows(a[f + "W2_experts"].transpose(1, 0, 2).reshape(4 * P, 8 * C)),
        w1=rows(a[f + "W1_shared"]), wso=rows(a[f + "W_shared_out"]), wsi=rows(a[f + "W_shared_in"]),
        wgate=rows(np.concatenate([a[f + "Wg_gate"], a[f + "We_gate"]], 1)),
        n1w=a[f + "norm1_w"][None], n2w=a[f + "norm2_w"][None],
        gbias=a[f + "group_bias"][None], ebias=a[f + "expert_bias"][None],
        lower=np.tril(np.ones((8, 8)), -1).reshape(1, 64),
        b_wq=rows(a[g + "Wq"]), b_wv=rows(a[g + "Wv"]), b_wr=rows(a[g + "Wr"]), b_wout=rows(a[g + "Wout"]),
        b_wqt=rows(a[g + "Wq"].T), gamma=a[g + "gamma"][None], beta=a[g + "beta"][None], bout=a[g + "bout"][None],
        u_t=a[g + "u_bias"].T, v_t=a[g + "v_bias"].T, pe_t=rows(pe.T),
        tril=np.arange(8)[None, None] <= token[:, :, None],
    )
    constants = ("ident", "block_mask", "head_mask", "cos", "sin", "lower", "pe_t", "tril")
    return {n: np.ascontiguousarray(v.astype(np.float32) if n in constants else v) for n, v in out.items()}


def kernel(**inputs):
    import concourse.bacc as bacc
    from concourse.bass_utils import run_bass_kernel_spmd

    nc = bacc.Bacc("TRN2", target_bir_lowering=False, num_devices=1)
    arrays = lay_out(inputs)
    aps = {n: nc.dram_tensor(n, v.shape, mybir.dt.from_np(v.dtype), kind="ExternalInput").ap() for n, v in arrays.items()}
    out = nc.dram_tensor("out", [N, C], F32, kind="ExternalOutput").ap()
    transformer(nc, aps.pop("x"), out, aps)
    r = run_bass_kernel_spmd(nc, [arrays], core_ids=[0])
    return r.results[0]["out"].reshape(B, T, C)
```

```python
import math
from contextlib import ExitStack

import numpy as np

import concourse.bass as bass
from concourse import mybir

ALU = mybir.AluOpType
ACT = mybir.ActivationFunctionType
AX = mybir.AxisListType
F32 = mybir.dt.float32
F32R = mybir.dt.float32r
P = 128
C = 256
B = 4
T = 1024
N = B * T
G = 512
K4 = G // P
NG = N // G
CH = C // P
DH = 16
LN_EPS = 1e-5
LN_LINKS = 3 * K4 + 1


class Phase:

    def __init__(self, nc, name):
        self.nc, self.name, self.ctx, self.sems = nc, name, ExitStack(), []

    def __enter__(self):
        return self

    def sb(self, name, shape, dt=F32):
        return self.ctx.enter_context(self.nc.sbuf_tensor(f"{self.name}_{name}", shape, dt))

    def ps(self, name, shape, dt=F32):
        return self.ctx.enter_context(self.nc.psum_tensor(f"{self.name}_{name}", shape, dt))

    def sem(self, name):
        s = self.nc.alloc_semaphore(name=f"{self.name}_{name}")
        self.sems.append(s)
        return s

    def __exit__(self, *err):
        if err[0] is None:
            self.ctx.close()
            self.nc.clear_and_free_semaphores(self.sems)
            self.nc.all_engine_barrier()


class Chain:

    def __init__(self, eng, sem, item, per):
        self.eng, self.sem, self.base, self.per, self.n = eng, sem, item * per, per, 0

    def done(self, ins):
        self.n += 1
        assert self.n <= self.per
        ins.then_inc(self.sem, 1)

    def wait(self):
        self.eng.wait_ge(self.sem, self.base + self.n)

    def __call__(self, ins):
        self.done(ins)
        self.wait()

    def close(self):
        assert self.n == self.per, (self.n, self.per)


def normalize_group(dve, nc, item, chain_sem, var_ready, rstd_ready, x4, stats, mv, var, rstd, out4):
    link = Chain(dve, chain_sem, item, LN_LINKS)
    for k in range(K4):
        link.done(nc.vector.bn_stats(stats[:, k, :], x4[:, k, :]))
    link.wait()
    link.done(nc.vector.memset(var[:, :], 0.0))
    for k in range(K4):
        link.done(nc.vector.bn_aggr(mv[:, k, :], stats[:, k, :]))
    link.wait()
    nc.vector.tensor_scalar(var[:, :], mv[:, :, 1], LN_EPS, None, ALU.add).then_inc(var_ready, 1)
    dve.wait_ge(rstd_ready, item + 1)
    for k in range(K4):
        link.done(nc.vector.tensor_scalar(out4[:, k, :], x4[:, k, :], mv[:, k, 0:1], rstd[:, k:k + 1],
                                          ALU.subtract, ALU.mult))
    link.wait()
    link.close()


def group_view(dram, g):
    return dram[bass.ds(g * G, G), :].rearrange("(k p) c -> p k c", p=P)


def linear_keys(nc, x_d, q_d, ctx_d, w):
    with Phase(nc, "lk") as ph:
        sb, ps, sem = ph.sb, ph.ps, ph.sem
        x4, xn = sb("x4", [P, 2, K4, C]), sb("xn", [P, 2, K4, C])
        stats, mv = sb("stats", [P, K4, 6]), sb("mv", [P, K4, 2])
        var, rstd, nhalf = sb("var", [P, K4]), sb("rstd", [P, K4]), sb("nhalf", [P, K4])
        ident, wt = sb("ident", [P, P]), sb("wt", [P, CH, 3 * C])
        bias, block_mask, head_mask = sb("bias", [P, 3 * C]), sb("block", [P, P]), sb("heads", [P, 8])
        xT = sb("xT", [P, 2, CH, G])
        qk = sb("qk", [P, K4, 2 * C])
        qkn = sb("qkn", [P, 2, K4, 2 * C])
        v = sb("v", [P, K4, CH, P + 2])
        mx, sm = sb("mx", [P, K4, 32]), sb("sm", [P, K4, 32])
        ctx = sb("ctx", [P, CH, P + 8])
        tp = ps("tp", [P, CH, G])
        qk_ps = [ps(f"qk{i}", [P, 2 * C]) for i in range(2)]
        v_ps = [ps(f"v{i}", [P, C]) for i in range(2)]
        c_ps = [ps(f"c{i}", [P, P + 2]) for i in range(2)]
        weights_in, x_in, consts = sem("weights_in"), [sem("x_in0"), sem("x_in1")], sem("consts")
        ln_chain, var_ready, rstd_ready = sem("ln_chain"), sem("var_ready"), sem("rstd_ready")
        turned, xT_ready = sem("turned"), sem("xT_ready")
        qk_made, biased, exp_ready, soft_chain = sem("qk_made"), sem("biased"), sem("exp_ready"), sem("soft_chain")
        qkn_ready = sem("qkn_ready")
        shifted, q_out = sem("shifted"), [sem("q_out0"), sem("q_out1")]
        summed, ctx_chain, ctx_out = sem("summed"), sem("ctx_chain"), sem("ctx_out")
        NWD = 7
        NT = T // P

        def heads(a):
            return a.rearrange("p (h d) -> p h d", d=DH)

        def spread(a):
            return a.rearrange("p (h o) -> p h o", o=1).broadcast_to([P, 32, DH])

        block = ph.ctx.enter_context(nc.Block())

        @block.sync
        def _(sp):
            for dst, a in ((ident, w["ident"]), (bias, w["qkv_bias"].broadcast_to([P, 3 * C])),
                           (block_mask, w["block_mask"]), (head_mask, w["head_mask"])):
                sp.dma_start(dst[:], a).then_inc(weights_in, 16)
            for j in range(3):
                sp.dma_start(wt[:, :, j * C:(j + 1) * C], w["qkv"][j].rearrange("(h p) f -> p h f", p=P)).then_inc(weights_in, 16)

            def load(b, half):
                sp.dma_start(x4[:, half], group_view(x_d, 2 * b + half)).then_inc(x_in[half], 16)

            load(0, 0)
            load(0, 1)

            def step(b, more):
                for half in range(2):
                    g = 2 * b + half
                    if more:
                        sp.wait_ge(ln_chain, (g + 1) * LN_LINKS)
                        load(b + 1, half)
                    sp.wait_ge(qkn_ready, (g + 1) * K4)
                    sp.dma_start(group_view(q_d, g), qkn[:, half, :, 0:C]).then_inc(q_out[half], 16)
                sp.wait_ge(ctx_chain, (b + 1) * 4)
                sp.dma_start(ctx_d[:, bass.ds(b * CH, CH), :], ctx[:, :, :]).then_inc(ctx_out, 16)

            with sp.Fori(0, B - 1) as b:
                step(b, True)
            step(B - 1, False)
            for s in q_out:
                sp.wait_ge(s, B * 16)
            sp.wait_ge(ctx_out, B * 16)

        @block.gpsimd
        def _(pool):
            nc.gpsimd.memset(nhalf[:, :], -0.5).then_inc(consts, 1)
            pool.wait_ge(consts, 1)
            nc.gpsimd.memset(v[:, :, :, P:P + 2], 1.0).then_inc(consts, 1)

            def power(g):
                pool.wait_ge(var_ready, g + 1)
                nc.gpsimd.tensor_tensor(rstd[:, :], var[:, :], nhalf[:, :], ALU.pow).then_inc(rstd_ready, 1)

            def subtract(t, k):
                pool.wait_ge(biased, (t + 1) * 3)
                nc.gpsimd.tensor_tensor(heads(qk[:, k]), heads(qk[:, k]), spread(mx[:, k]), ALU.subtract).then_inc(shifted, 1)

            def divide(b, half, k, first):
                g = 2 * b + half
                pool.wait_ge(soft_chain, (g * K4 + k + 1) * 2)
                if k == 0 and not first:
                    pool.wait_ge(summed, (g - 1) * K4)
                    pool.wait_ge(q_out[half], b * 16)
                nc.gpsimd.tensor_tensor(heads(qkn[:, half, k]), heads(qk[:, k]), spread(sm[:, k]), ALU.mult).then_inc(qkn_ready, 1)

            def step(b, first, more):
                for half in range(2):
                    for k in range(K4):
                        t = (2 * b + half) * K4 + k
                        if more or not (half and k == K4 - 1):
                            subtract(t + 1, (k + 1) % K4)
                        if k == 2 and more:
                            power(2 * b + half + 2)
                        divide(b, half, k, first)

            power(0)
            power(1)
            subtract(0, 0)
            step(0, True, True)
            with pool.Fori(1, B - 1) as b:
                step(b, False, True)
            step(B - 1, False, False)

        @block.scalar
        def _(act):
            def turned_in(b, half, first):
                g = 2 * b + half
                act.wait_ge(turned, g + 1)
                if not first:
                    act.wait_ge(qk_made, (g - 1) * K4)
                nc.scalar.copy(xT[:, half], tp[:, :, :]).then_inc(xT_ready, 1)

            def step(b, first, more):
                for half in range(2):
                    for k in range(K4):
                        t = (2 * b + half) * K4 + k
                        act.wait_ge(shifted, t + 1)
                        nc.scalar.activation(qk[:, k], qk[:, k], ACT.Exp).then_inc(exp_ready, 1)
                        if k == 1 and (half == 0 or more):
                            turned_in(b + half, 1 - half, first and half == 0)

            turned_in(0, 0, True)
            step(0, True, True)
            with act.Fori(1, B - 1) as b:
                step(b, False, True)
            step(B - 1, False, False)

        @block.vector
        def _(dve):
            dve.wait_ge(weights_in, NWD * 16)
            dve.wait_ge(consts, 2)

            def norm(b, half, first):
                g = 2 * b + half
                dve.wait_ge(x_in[half], (b + 1) * 16)
                if not first:
                    dve.wait_ge(turned, g - 1)
                normalize_group(dve, nc, g, ln_chain, var_ready, rstd_ready, x4[:, half], stats, mv, var, rstd, xn[:, half])

            def shift(t, k, first):
                link = Chain(dve, biased, t, 3)
                dve.wait_ge(qk_made, t + 1)
                if not first:
                    dve.wait_ge(summed, t - K4 + 1)
                    dve.wait_ge(qkn_ready, t - K4 + 1)
                link.done(nc.vector.tensor_tensor(qk[:, k], qk_ps[k % 2][:, :], bias[:, 0:2 * C], ALU.add))
                link(nc.vector.tensor_tensor(v[:, k, :, 0:P], v_ps[k % 2][:, :].rearrange("p (h f) -> p h f", h=CH),
                                             bias[:, 2 * C:3 * C].rearrange("p (h f) -> p h f", h=CH), ALU.add))
                link.done(nc.vector.tensor_reduce(mx[:, k], heads(qk[:, k]), AX.X, ALU.max))
                link.close()

            def soften(t, k, first):
                link = Chain(dve, soft_chain, t, 2)
                dve.wait_ge(exp_ready, t + 1)
                if not first:
                    dve.wait_ge(qkn_ready, t - K4 + 1)
                link(nc.vector.tensor_reduce(sm[:, k], heads(qk[:, k]), AX.X, ALU.add))
                link.done(nc.vector.reciprocal(sm[:, k], sm[:, k]))
                link.close()

            def keys_of(b, first):
                link = Chain(dve, ctx_chain, b, 4)
                dve.wait_ge(summed, (b + 1) * NT)
                if not first:
                    dve.wait_ge(ctx_out, b * 16)
                for h in range(CH):
                    link.done(nc.vector.tensor_tensor(ctx[:, h, 0:P], c_ps[h][:, 0:P], block_mask[:, :], ALU.mult))
                    link.done(nc.vector.tensor_tensor(ctx[:, h, P:P + 8], c_ps[h][:, P:P + 1].broadcast_to([P, 8]),
                                                      head_mask[:, :], ALU.mult))
                link.close()

            def step(b, first, more, second=False):
                for half in range(2):
                    for k in range(K4):
                        t = (2 * b + half) * K4 + k
                        if more or not (half and k == K4 - 1):
                            shift(t + 1, (k + 1) % K4, first and half == 0 and k < K4 - 1)
                        if k == 2 and more:
                            norm(b + 1, half, False)
                        if half == 0 and k == 1 and not first:
                            keys_of(b - 1, second)
                        soften(t, k, first and half == 0)

            norm(0, 0, True)
            norm(0, 1, True)
            shift(0, 0, True)
            step(0, True, True)
            step(1, False, True, second=True)
            with dve.Fori(2, B - 1) as b:
                step(b, False, True)
            step(B - 1, False, False)
            keys_of(B - 1, False)

        @block.tensor
        def _(pe):
            pe.wait_ge(weights_in, NWD * 16)

            def turn(b, half, first):
                g = 2 * b + half
                pe.wait_ge(ln_chain, (g + 1) * LN_LINKS)
                if not first:
                    pe.wait_ge(xT_ready, g)
                for k in range(K4):
                    for h in range(CH):
                        last = nc.tensor.transpose(tp[:, h, k * P:(k + 1) * P], xn[:, half, k, h * P:(h + 1) * P], ident[:, :])
                last.then_inc(turned, 1)

            def project(b, half, k, early):
                t = (2 * b + half) * K4 + k
                if k == 0:
                    pe.wait_ge(xT_ready, 2 * b + half + 1)
                if not early:
                    pe.wait_ge(biased, (t - 1) * 3)
                cols = slice(k * P, (k + 1) * P)
                for out, f in ((v_ps[k % 2], slice(2 * C, 3 * C)), (qk_ps[k % 2], slice(0, 2 * C))):
                    for h in range(CH):
                        mm = nc.tensor.matmul(out[:, :], xT[:, half, h, cols], wt[:, h, f], start=h == 0, stop=h == CH - 1)
                mm.then_inc(qk_made, 1)

            def sum_keys(b, half, k, first):
                t = (2 * b + half) * K4 + k
                pe.wait_ge(qkn_ready, t + 1)
                if half == 0 and k == 0 and not first:
                    pe.wait_ge(ctx_chain, b * 4)
                for h in range(CH):
                    mm = nc.tensor.matmul(c_ps[h][:, :], qkn[:, half, k, C + h * P:C + (h + 1) * P], v[:, k, h, :],
                                          start=half == 0 and k == 0, stop=half == 1 and k == K4 - 1)
                mm.then_inc(summed, 1)

            def step(b, first, more):
                for half in range(2):
                    for k in range(K4):
                        if k == K4 - 1 and (half == 0 or more):
                            turn(b + half, 1 - half, False)
                        project(b, half, k, first and half == 0 and k < 2)
                        if k >= 2:
                            sum_keys(b, half, k - 2, first)
                        elif half:
                            sum_keys(b, 0, K4 + k - 2, first)
                        elif not first:
                            sum_keys(b - 1, 1, K4 + k - 2, False)

            turn(0, 0, True)
            step(0, True, True)
            with pe.Fori(1, B - 1) as b:
                step(b, False, True)
            step(B - 1, False, False)
            sum_keys(B - 1, 1, K4 - 2, False)
            sum_keys(B - 1, 1, K4 - 1, False)


def linear_mix(nc, x_d, q_d, ctx_d, out_d, w):
    W = P + 8
    with Phase(nc, "lm") as ph:
        sb, ps, sem = ph.sb, ph.ps, ph.sem
        q4, x4 = sb("q4", [P, 2, K4, C]), sb("x4", [P, 2, K4, C])
        ctx = sb("ctx", [P, 2, CH, W])
        ident, wp, bp = sb("ident", [P, P]), sb("wp", [P, CH, C]), sb("bp", [P, C])
        qT, aT = sb("qT", [P, CH, G]), sb("aT", [P, CH, G])
        inv, a4 = sb("inv", [P, 2, 16]), sb("a4", [P, K4, C])
        tp, tq = ps("tp", [P, CH, G]), ps("tq", [P, CH, G])
        mix = [ps(f"mix{i}", [P, CH, W]) for i in range(2)]
        o_ps = [ps(f"o{i}", [P, C]) for i in range(2)]
        weights_in, loads, x_in = sem("weights_in"), [sem("loads0"), sem("loads1")], [sem("x_in0"), sem("x_in1")]
        q_turned, qT_ready, mixed, mix_chain = sem("q_turned"), sem("qT_ready"), sem("mixed"), sem("mix_chain")
        a_turned, aT_ready, projected, out_chain = sem("a_turned"), sem("aT_ready"), sem("projected"), sem("out_chain")
        xb_ready = sem("xb_ready")
        stored = [sem("stored0"), sem("stored1")]
        NL = 2
        block = ph.ctx.enter_context(nc.Block())

        def batches(eng, group):
            group(0, 0, True)
            group(0, 1, False)
            with eng.Fori(1, B) as b:
                for half in range(2):
                    group(b, half, False)

        @block.sync
        def _(sp):
            for dst, a in ((ident, w["ident"]), (wp, w["wpt"].rearrange("(h p) f -> p h f", p=P)),
                           (bp, w["bp"].broadcast_to([P, C]))):
                sp.dma_start(dst[:], a).then_inc(weights_in, 16)

            def load_q(b, half, fresh):
                g = 2 * b + half
                if not fresh:
                    sp.wait_ge(mix_chain, (g - 1) * K4 * 3)
                sp.dma_start(q4[:, half], group_view(q_d, g)).then_inc(loads[half], 16)
                sp.dma_start(ctx[:, half], ctx_d[:, bass.ds(b * CH, CH), :]).then_inc(loads[half], 16)

            def load_x(b, half, fresh):
                if not fresh:
                    sp.wait_ge(stored[half], b * 16)
                sp.dma_start(x4[:, half], group_view(x_d, 2 * b + half)).then_inc(x_in[half], 16)

            def store(b, half):
                g = 2 * b + half
                sp.wait_ge(out_chain, (g + 1) * K4)
                sp.dma_start(group_view(out_d, g), x4[:, half]).then_inc(stored[half], 16)

            for half in range(2):
                load_q(0, half, True)
                load_x(0, half, True)
            with sp.Fori(0, B - 1) as b:
                for half in range(2):
                    load_q(b + 1, half, False)
                    store(b, half)
                    load_x(b + 1, half, False)
            for half in range(2):
                store(B - 1, half)
            for s in stored:
                sp.wait_ge(s, B * 16)

        @block.gpsimd
        def _(pool):
            pool.wait_ge(weights_in, 3 * 16)
            with pool.Fori(0, B) as b:
                for half in range(2):
                    pool.wait_ge(x_in[half], (b + 1) * 16)
                    nc.gpsimd.tensor_tensor(x4[:, half], x4[:, half],
                                            bp[:, :].rearrange("p (o c) -> p o c", o=1).broadcast_to([P, K4, C]),
                                            ALU.add).then_inc(xb_ready, 1)

        @block.scalar
        def _(act):
            def queries(g, first):
                act.wait_ge(q_turned, g + 1)
                if not first:
                    act.wait_ge(mixed, g * K4)
                nc.scalar.copy(qT[:, :, :], tq[:, :, :]).then_inc(qT_ready, 1)

            def group(g, first):
                act.wait_ge(a_turned, g + 1)
                if not first:
                    act.wait_ge(projected, g * K4)
                nc.scalar.copy(aT[:, :, :], tp[:, :, :]).then_inc(aT_ready, 1)

            queries(0, True)
            queries(1, False)
            group(0, True)
            with act.Fori(1, NG - 1) as g:
                queries(g + 1, False)
                group(g, False)
            group(NG - 1, False)

        @block.vector
        def _(dve):
            def finish(g, half):
                dve.wait_ge(xb_ready, g + 1)
                for k in range(K4):
                    dve.wait_ge(projected, g * K4 + k + 1)
                    nc.vector.tensor_tensor(x4[:, half, k], x4[:, half, k], o_ps[k % 2][:, :], ALU.add).then_inc(out_chain, 1)

            def group(b, half, first):
                g = 2 * b + half
                dve.wait_ge(loads[half], (b + 1) * NL * 16)
                for k in range(K4):
                    t = g * K4 + k
                    link = Chain(dve, mix_chain, t, 3)
                    dve.wait_ge(mixed, t + 1)
                    if k == 0 and not first:
                        dve.wait_ge(a_turned, g)
                    m = mix[k % 2]
                    link(nc.vector.reciprocal(inv[:, k % 2].rearrange("p (h d) -> p h d", h=CH), m[:, :, P:W]))
                    link(nc.vector.tensor_tensor(
                        a4[:, k].rearrange("p (h n d) -> p h n d", h=CH, d=DH),
                        m[:, :, 0:P].rearrange("p h (n d) -> p h n d", d=DH),
                        inv[:, k % 2].rearrange("p (h n o) -> p h n o", h=CH, o=1).broadcast_to([P, CH, 8, DH]), ALU.mult))
                    link(nc.vector.tensor_tensor(a4[:, k], a4[:, k], q4[:, half, k], ALU.add))
                if not first:
                    finish(g - 1, 1 - half)

            batches(dve, group)
            finish(NG - 1, 1)

        @block.tensor
        def _(pe):
            pe.wait_ge(weights_in, 3 * 16)

            def turn_q(b, half, first):
                g = 2 * b + half
                pe.wait_ge(loads[half], (b + 1) * NL * 16)
                if not first:
                    pe.wait_ge(qT_ready, g)
                for k in range(K4):
                    for h in range(CH):
                        mm = nc.tensor.transpose(tq[:, h, k * P:(k + 1) * P], q4[:, half, k, h * P:(h + 1) * P], ident[:, :])
                mm.then_inc(q_turned, 1)

            def group(b, half, first, more=True, second=False):
                g = 2 * b + half
                pe.wait_ge(qT_ready, g + 1)
                for k in range(K4):
                    t = g * K4 + k
                    if not (first and k < 2):
                        pe.wait_ge(mix_chain, (t - 1) * 3)
                    for h in range(CH):
                        mm = nc.tensor.matmul(mix[k % 2][:, h], qT[:, h, k * P:(k + 1) * P], ctx[:, half, h], start=True, stop=True)
                    mm.then_inc(mixed, 1)
                if not first:
                    project(g - 1, first_one=second)
                if more:
                    turn_q(b + half, 1 - half, False)
                pe.wait_ge(mix_chain, (g + 1) * K4 * 3)
                if not first:
                    pe.wait_ge(aT_ready, g)
                for k in range(K4):
                    for h in range(CH):
                        mm = nc.tensor.transpose(tp[:, h, k * P:(k + 1) * P], a4[:, k, h * P:(h + 1) * P], ident[:, :])
                mm.then_inc(a_turned, 1)

            def project(g, first_one=False):
                pe.wait_ge(aT_ready, g + 1)
                for k in range(K4):
                    if not (first_one and k < 2):
                        pe.wait_ge(out_chain, g * K4 + k - 1)
                    for h in range(CH):
                        mm = nc.tensor.matmul(o_ps[k % 2][:, :], aT[:, h, k * P:(k + 1) * P], wp[:, h, :],
                                              start=h == 0, stop=h == CH - 1)
                    mm.then_inc(projected, 1)

            turn_q(0, 0, True)
            group(0, 0, True)
            group(0, 1, False, second=True)
            with pe.Fori(1, B - 1) as b:
                for half in range(2):
                    group(b, half, False)
            group(B - 1, 0, False)
            group(B - 1, 1, False, more=False)
            project(NG - 1)


def ffn_project(nc, tag, x_d, src_d, qk_d, V, w):
    with Phase(nc, tag + "_fp") as ph:
        sb, ps, sem = ph.sb, ph.ps, ph.sem
        x4 = sb("x4", [P, 2, K4, C])
        src = sb("src", [P, 2, K4, C])
        stats, mv = sb("stats", [P, K4, 6]), sb("mv", [P, K4, 2])
        var, rstd, nhalf = sb("var", [P, K4]), sb("rstd", [P, K4]), sb("nhalf", [P, K4])
        ident = sb("ident", [P, P])
        wq, wqs = sb("wq", [P, CH, C]), sb("wqs", [P, CH, C])
        wc = sb("wc", [P, CH, P])
        wk, wks, wv = sb("wk", [64, C]), sb("wks", [64, C]), sb("wv", [P, C])
        cos, sin = sb("cos", [P, T]), sb("sin", [P, T])
        srcT = sb("srcT", [P, 2, CH, G])
        kcvc = sb("kcvc", [P, G])
        ta, tb = sb("ta", [P, 2, G]), sb("tb", [P, 2, G])
        rot = sb("rot", [P, 2, G])
        hi, lo = sb("hi", [P, 2, G], F32R), sb("lo", [P, 2, G], F32R)
        tp = ps("tp", [P, CH, G])
        pair = [[ps(f"pair{i}{j}", [P, G]) for j in range(2)] for i in range(2)]
        kv_ps, v_ps = ps("kv", [P, G]), ps("v", [P, 2, C])

        weights_in, x_in = sem("weights_in"), [sem("x_in0"), sem("x_in1")]
        src_out = [sem("src_out0"), sem("src_out1")]
        consts = sem("consts")
        ln_chain, var_ready, rstd_ready = sem("ln_chain"), sem("var_ready"), sem("rstd_ready")
        turned, srcT_ready = sem("turned"), sem("srcT_ready")
        kv_made, kv_ready = sem("kv_made"), sem("kv_ready")
        v_made, v_ready = sem("v_made"), sem("v_ready")
        pair_made, rot_chain, rot_ready = sem("pair_made"), sem("rot_chain"), sem("rot_ready")
        hi_ready, lo_ready, parts_out = sem("hi_ready"), sem("lo_ready"), [sem("parts_out0"), sem("parts_out1")]
        NW = 10

        block = ph.ctx.enter_context(nc.Block())

        def groups(eng, body):
            with eng.Fori(0, B) as b:
                for half in range(2):
                    body(b, half)

        @block.sync
        def _(sp):
            for dst, a in ((ident, w["ident"]), (wq, w["wq"].rearrange("(h p) f -> p h f", p=P)),
                           (wqs, w["wqs"].rearrange("(h p) f -> p h f", p=P)), (wk, w["wk"]), (wks, w["wks"]),
                           (cos, w["cos"]), (sin, w["sin"])):
                sp.dma_start(dst[:], a).then_inc(weights_in, 16)
            sp.dma_start(wv[64:128, :], w["wv"]).then_inc(weights_in, 16)
            sp.dma_start(wc[:, :, 0:64], w["wkc"].rearrange("(h p) f -> p h f", p=P)).then_inc(weights_in, 16)
            sp.dma_start(wc[:, :, 64:128], w["wvc"].rearrange("(h p) f -> p h f", p=P)).then_inc(weights_in, 16)

            def load_x(b, half):
                sp.dma_start(x4[:, half], group_view(x_d, 2 * b + half)).then_inc(x_in[half], 16)

            load_x(0, 0)
            load_x(0, 1)

            def step(b, half, more):
                g = 2 * b + half
                sp.wait_ge(ln_chain, (g + 1) * LN_LINKS)
                sp.dma_start(group_view(src_d, g), src[:, half]).then_inc(src_out[half], 16)
                if more:
                    load_x(b + 1, half)
                for n in range(4):
                    rows = qk_d[:, bass.ds(b * C + (n % 2) * P, P), half * G:(half + 1) * G]
                    sp.wait_ge(hi_ready, g * 4 + n + 1)
                    sp.dma_start(rows[2 * (n // 2)], hi[:, n % 2].bitcast(F32)).then_inc(parts_out[n % 2], 16)
                    sp.wait_ge(lo_ready, g * 4 + n + 1)
                    sp.dma_start(rows[2 * (n // 2) + 1], lo[:, n % 2].bitcast(F32)).then_inc(parts_out[n % 2], 16)

            with sp.Fori(0, B - 1) as b:
                for half in range(2):
                    step(b, half, True)
            for half in range(2):
                step(B - 1, half, False)
            for s in src_out:
                sp.wait_ge(s, B * 16)
            for s in parts_out:
                sp.wait_ge(s, NG * 4 * 16)

        @block.gpsimd
        def _(pool):
            nc.gpsimd.memset(nhalf[:, :], -0.5).then_inc(consts, 1)
            pool.wait_ge(consts, 1)

            def power(g):
                pool.wait_ge(var_ready, g + 1)
                nc.gpsimd.tensor_tensor(rstd[:, :], var[:, :], nhalf[:, :], ALU.pow).then_inc(rstd_ready, 1)

            def rotated(g, n, fresh):
                i = n % 2
                pool.wait_ge(rot_chain, g * 8 + 2 * n + 2)
                if not fresh:
                    pool.wait_ge(hi_ready, g * 4 + n - 1)
                    pool.wait_ge(lo_ready, g * 4 + n - 1)
                nc.gpsimd.tensor_tensor(rot[:, i], ta[:, i], tb[:, i], ALU.add).then_inc(rot_ready, 1)

            def low(g, n, fresh):
                i = n % 2
                pool.wait_ge(rot_ready, g * 4 + n + 1)
                pool.wait_ge(hi_ready, g * 4 + n + 1)
                if not fresh:
                    pool.wait_ge(parts_out[i], g * 64 + (n // 2) * 32)
                nc.gpsimd.tensor_tensor(lo[:, i], rot[:, i], hi[:, i].bitcast(F32), ALU.subtract).then_inc(lo_ready, 1)

            def step(g, first, more):
                rotated(g, 0, first)
                if more:
                    power(g + 1)
                rotated(g, 1, first)
                low(g, 0, first)
                rotated(g, 2, False)
                low(g, 1, first)
                rotated(g, 3, False)
                low(g, 2, False)
                low(g, 3, False)

            power(0)
            step(0, True, True)
            with pool.Fori(1, NG - 1) as g:
                step(g, False, True)
            step(NG - 1, False, False)

        @block.vector
        def _(dve):
            dve.wait_ge(weights_in, NW * 16)

            def norm(b, half, first):
                g = 2 * b + half
                dve.wait_ge(x_in[half], (b + 1) * 16)
                if not first:
                    dve.wait_ge(turned, g - 1)
                    dve.wait_ge(src_out[half], b * 16)
                normalize_group(dve, nc, g, ln_chain, var_ready, rstd_ready, x4[:, half], stats, mv, var, rstd,
                                src[:, half])

            def step(b, half, first, more):
                g = 2 * b + half
                link = Chain(dve, rot_chain, g, 8)
                for n in range(4):
                    i = n % 2
                    t = slice(half * G, (half + 1) * G)
                    dve.wait_ge(pair_made, g * 4 + n + 1)
                    if not (first and n < 2):
                        dve.wait_ge(rot_ready, g * 4 + n - 1)
                    link.done(nc.vector.tensor_tensor(ta[:, i], pair[i][0][:, :], cos[:, t], ALU.mult))
                    link.done(nc.vector.tensor_tensor(tb[:, i], pair[i][1][:, :], sin[:, t], ALU.mult))
                    if n == 0 and more:
                        norm(b + half, 1 - half, first)
                link.close()

            norm(0, 0, True)
            step(0, 0, True, True)
            step(0, 1, False, True)
            with dve.Fori(1, B - 1) as b:
                for half in range(2):
                    step(b, half, False, True)
            step(B - 1, 0, False, True)
            step(B - 1, 1, False, False)

        @block.scalar
        def _(act):
            def turned_in(b, half, first):
                g = 2 * b + half
                act.wait_ge(turned, g + 1)
                if not first:
                    act.wait_ge(v_made, 2 * (g - 1))
                nc.scalar.copy(srcT[:, half], tp[:, :, :]).then_inc(srcT_ready, 1)

            def halves(b, half, n, first):
                g = 2 * b + half
                act.wait_ge(rot_ready, g * 4 + n + 1)
                if not (first and n < 2):
                    act.wait_ge(parts_out[n % 2], g * 64 + (n // 2) * 32)
                nc.scalar.copy(hi[:, n % 2], rot[:, n % 2]).then_inc(hi_ready, 1)

            def step(b, half, first, more):
                g = 2 * b + half
                act.wait_ge(kv_made, g + 1)
                if not (first and half == 0):
                    act.wait_ge(pair_made, 4 * g)
                nc.scalar.copy(kcvc[:, :], kv_ps[:, :]).then_inc(kv_ready, 1)
                halves(b, half, 0, first and half == 0)
                for r in range(2):
                    act.wait_ge(v_made, 2 * g + r + 1)
                    kt = half * K4 + 2 * r
                    nc.scalar.copy(V[:, bass.ds(b * 8, 8), kt:kt + 2, :].rearrange("p u k c -> p k u c"),
                                   v_ps[:, :, :].rearrange("p k (u c) -> p k u c", u=8)).then_inc(v_ready, 1)
                halves(b, half, 1, first and half == 0)
                if more:
                    turned_in(b + half, 1 - half, first and half == 0)
                halves(b, half, 2, False)
                halves(b, half, 3, False)

            turned_in(0, 0, True)
            step(0, 0, True, True)
            step(0, 1, False, True)
            with act.Fori(1, B - 1) as b:
                for half in range(2):
                    step(b, half, False, True)
            step(B - 1, 0, False, True)
            step(B - 1, 1, False, False)

        @block.tensor
        def _(pe):
            pe.wait_ge(weights_in, NW * 16)

            def turn(b, half, first):
                g = 2 * b + half
                pe.wait_ge(ln_chain, (g + 1) * LN_LINKS)
                if not first:
                    pe.wait_ge(srcT_ready, g)
                for k in range(K4):
                    for h in range(CH):
                        last = nc.tensor.transpose(tp[:, h, k * P:(k + 1) * P], src[:, half, k, h * P:(h + 1) * P], ident[:, :])
                last.then_inc(turned, 1)

            def project(b, half, first, more):
                g = 2 * b + half
                pe.wait_ge(srcT_ready, g + 1)
                if not first:
                    pe.wait_ge(kv_ready, g)
                for h in range(CH):
                    mm = nc.tensor.matmul(kv_ps[:, :], wc[:, h, :], srcT[:, half, h, :], start=h == 0, stop=h == CH - 1)
                mm.then_inc(kv_made, 1)
                for n in range(4):
                    if not (first and n < 2):
                        pe.wait_ge(rot_chain, g * 8 + 2 * (n - 1))
                    f = slice((n % 2) * P, (n % 2 + 1) * P)
                    if n == 2:
                        pe.wait_ge(kv_ready, g + 1)
                    for j in range(2):
                        if n < 2:
                            a = (wq, wqs)[j]
                            for h in range(CH):
                                mm = nc.tensor.matmul(pair[n % 2][j][:, :], a[:, h, f], srcT[:, half, h, :],
                                                      start=h == 0, stop=h == CH - 1)
                        else:
                            mm = nc.tensor.matmul(pair[n % 2][j][:, :], (wk, wks)[j][:, f], kcvc[0:64, :],
                                                  start=True, stop=True)
                    mm.then_inc(pair_made, 1)
                    if n == 1:
                        pe.wait_ge(kv_ready, g + 1)
                        for r in range(2):
                            if not (first and r == 0):
                                pe.wait_ge(v_ready, 2 * g + r)
                            for k in range(2):
                                mm = nc.tensor.matmul(v_ps[:, k, :], kcvc[64:128, (2 * r + k) * P:(2 * r + k + 1) * P],
                                                      wv[64:128, :], start=True, stop=True)
                            mm.then_inc(v_made, 1)
                    if n == 2 and more:
                        turn(b + half, 1 - half, False)

            turn(0, 0, True)
            project(0, 0, True, True)
            project(0, 1, False, True)
            with pe.Fori(1, B - 1) as b:
                for half in range(2):
                    project(b, half, False, True)
            project(B - 1, 0, False, True)
            project(B - 1, 1, False, False)


def ffn_attend(nc, tag, qk_d, V, heads_d, w, parts):
    U = 32
    KT = T // P
    NB = 3
    LEAD = 3
    R = 4 * DH
    SCALE = 0.25
    with Phase(nc, tag + "_fa") as ph:
        sb, ps, sem = ph.sb, ph.ps, ph.sem
        qs = [sb(f"qs{i}", [R + 2, 2, T], F32R) for i in range(NB)]
        ks = [sb(f"ks{i}", [R + 2, 2, T], F32R) for i in range(NB)]
        va = [sb(f"va{i}", [P, KT, 2, 32]) for i in range(NB)]
        probs = [sb(f"probs{i}", [P, T]) for i in range(4)]
        pm = sb("pm", [P, 2, KT, 2])
        mx = sb("mx", [P, 2 * KT])
        nhi, nlo = sb("nhi", [2 * KT, P], F32R), sb("nlo", [2 * KT, P], F32R)
        osb, ident = sb("osb", [P, G]), sb("ident", [P, P])
        rsum = sb("rsum", [P, K4 * 4])
        heads = [sb(f"heads{i}", [P, KT, 2 * DH]) for i in range(NB)]
        ring = [ps(f"ring{i}", [P, G]) for i in range(3)]
        score = [ps(f"score{i}", [P, T]) for i in range(2)]
        acc = ps("acc", [P, G])

        ident_in, ones_set, va_set = sem("ident_in"), sem("ones_set"), sem("va_set")
        loaded = [sem(f"loaded{i}") for i in range(NB)]
        rows_in = [sem(f"rows_in{i}") for i in range(NB)]
        va_ready = sem("va_ready")
        ring_made, ring_read = sem("ring_made"), sem("ring_read")
        mx_ready, nhi_ready = sem("mx_ready"), sem("nhi_ready")
        score_made, exp_done, pv_done = sem("score_made"), sem("exp_done"), sem("pv_done")
        heads_out = [sem(f"heads_out{i}") for i in range(NB)]
        osb_ready, out_chain = sem("osb_ready"), sem("out_chain")

        raw = [sb(f"raw{i}", [P, 1024]) for i in range(2)]
        raw_in, split = [sem("raw_in0"), sem("raw_in1")], sem("split")

        def flat(a):
            return a.rearrange("p a b -> p (a b)")

        pieces = [[flat(a)[:, at:at + 1024] for a in (w[name], hi, lo)] for name, (hi, lo) in parts.items()
                  for at in range(0, flat(hi).shape[1], 1024)]

        block = ph.ctx.enter_context(nc.Block())

        def steady(eng, step, first=0):
            for u in range(3 * first + 1):
                step(0, u)
            with eng.Fori(first, 9) as i:
                for c in (1, 2, 3):
                    step(i, c, True)
            for u in range(28, U + 1):
                step(0, u)

        def items(u):
            out = []
            if u == U:
                return ["out"]
            for k in range(KT):
                if u is None or u + (1 if k + LEAD < KT else 2) < U:
                    out += [("one", k, x) for x in range(4)]
                if k == 2 and u != 0:
                    out.append("out")
                if k == KT - LEAD and (u is None or u + 1 < U):
                    out.append("max")
            return out

        PER_UNIT = len(items(None))
        BEFORE = 4 * KT + 1 + 4 * LEAD
        assert PER_UNIT % 3 == 1

        def place(i, c, inner, what):
            if inner:
                n = BEFORE + len(items(0)) + (c - 1) * PER_UNIT + items(None).index(what)
                return 3 * i * PER_UNIT + n, ring[n % 3]
            n = BEFORE + sum(len(items(v)) for v in range(c)) + items(c).index(what)
            return n, ring[n % 3]

        def ready_out(i, c, inner=False):
            return place(i, c + 1, inner, "out")[0] + 1

        def ready_max(i, c, inner=False):
            return 4 * KT + 1 if not inner and c == 0 else place(i, c - 1, inner, "max")[0] + 1

        @block.sync
        def _(sp):
            sp.dma_start(ident[:, :], w["ident"]).then_inc(ident_in, 16)

            def load(i, c):
                u = 3 * i + c
                for stack, parts in ((qs, (0, 0, 1, 1)), (ks, (2, 3, 2, 3))):
                    for r, part in enumerate(parts):
                        sp.dma_start(stack[c % NB][r * DH:(r + 1) * DH].bitcast(F32),
                                     qk_d[part, bass.ds(u * 32, 32), :].rearrange("(h d) t -> d h t", h=2)
                                     ).then_inc(loaded[c % NB], 16)

            def max_rows(i, c, inner=False):
                u = 3 * i + c
                sp.wait_ge(nhi_ready, u + 1)
                sp.dma_start(qs[c % NB][R:R + 1].bitcast(F32), nhi[:, :].bitcast(F32)).then_inc(rows_in[c % NB], 16)
                sp.wait_ge(ring_read, ready_max(i, c, inner))
                sp.dma_start(qs[c % NB][R + 1:R + 2].bitcast(F32), nlo[:, :].bitcast(F32)).then_inc(rows_in[c % NB], 16)

            for u in range(NB):
                load(0, u)
            max_rows(0, 0)

            def step(i, c, inner=False):
                u = 3 * i + c
                if inner or u + 1 < U:
                    max_rows(i, c + 1, inner)
                if inner or u >= 1:
                    sp.wait_ge(ring_read, ready_out(i, c - 1, inner))
                    sp.dma_start(heads_d[:, bass.ds(u - 1, 1), :, :].rearrange("p u k c -> p (u k c)"),
                                 heads[(c - 1) % NB][:, :, :].rearrange("p k c -> p (k c)")
                                 ).then_inc(heads_out[(c - 1) % NB], 16)
                if inner or u + NB < U:
                    sp.wait_ge(score_made, (u + 1) * 2 * KT)
                    load(i, c + NB)

            steady(sp, step)
            for s in heads_out:
                sp.wait_ge(s, (U // NB) * 16)
            sp.wait_ge(heads_out[0], (U // NB + 1) * 16)
            sp.wait_ge(heads_out[1], (U // NB + 1) * 16)

        @block.gpsimd
        def _(pool):
            for i in range(NB):
                nc.gpsimd.memset(va[i][:, :, :, :], 0.0).then_inc(va_set, 1)
            pool.wait_ge(va_set, NB)
            for i in range(NB):
                nc.gpsimd.memset(va[i][:, :, :, DH:DH + 1], 1.0).then_inc(va_set, 1)
            pool.wait_ge(va_set, 2 * NB)
            for i in range(NB):
                if i:
                    pool.wait_ge(ones_set, i)
                nc.gpsimd.memset(ks[i][R:R + 2].bitcast(F32), 1.0).then_inc(ones_set, 1)
            pool.wait_ge(ones_set, NB)

            def values(i, c):
                u = 3 * i + c
                nc.gpsimd.tensor_copy(va[c % NB][:, :, :, 0:DH],
                                      V[:, bass.ds(u, 1), :, :].rearrange("p u k (h d) -> p (u k) h d", h=2)
                                      ).then_inc(va_ready, 1)

            for u in range(NB):
                values(0, u)

            def load_piece(n):
                pool.dma_start(raw[n % 2][:, :], pieces[n][0]).then_inc(raw_in[n % 2], 16)

            load_piece(0)
            load_piece(1)
            for n, (_, hi, lo) in enumerate(pieces):
                pool.wait_ge(raw_in[n % 2], (n // 2 + 1) * 16)
                nc.gpsimd.tensor_copy(hi, raw[n % 2][:, :]).then_inc(split, 1)
                pool.wait_ge(split, 2 * n + 1)
                nc.gpsimd.tensor_tensor(lo, raw[n % 2][:, :], hi.bitcast(F32), ALU.subtract).then_inc(split, 1)
                if n + 2 < len(pieces):
                    pool.wait_ge(split, 2 * n + 2)
                    load_piece(n + 2)
            pool.wait_ge(split, 2 * len(pieces))

            def step(i, c, inner=False):
                u = 3 * i + c
                if inner or u + NB < U:
                    pool.wait_ge(pv_done, (u + 1) * KT)
                    values(i, c + NB)

            steady(pool, step)

        @block.scalar
        def _(act):
            def exps(i, c, k, first_ones):
                u = 3 * i + c
                for h in range(2):
                    act.wait_ge(score_made, u * 2 * KT + 2 * k + h + 1)
                    if not first_ones:
                        act.wait_ge(pv_done, u * KT + k - 1)
                    nc.scalar.activation(probs[(2 * k + h) % 4][:, :], score[h][:, :], ACT.Exp,
                                         scale=SCALE).then_inc(exp_done, 1)

            def take_out(i, c, first_one, inner=False):
                u = 3 * i + c
                act.wait_ge(pv_done, (u + 1) * KT)
                if not first_one:
                    act.wait_ge(ring_made, ready_out(i, c - 1, inner))
                nc.scalar.copy(osb[:, :], acc[:, :]).then_inc(osb_ready, 1)

            def step(i, c, inner=False):
                u = 3 * i + c
                if not inner and u == U:
                    take_out(i, c - 1, False)
                    return
                zero = not inner and u == 0
                for k in range(KT):
                    exps(i, c, k, zero and k < 2)
                    if k == 0 and not zero:
                        take_out(i, c - 1, not inner and u == 1, inner)
            step(0, 0)
            step(0, 1)
            with act.Fori(0, 8) as i:
                for c in (2, 3, 4):
                    step(i, c, True)
            for u in range(26, U + 1):
                step(0, u)

        @block.vector
        def _(dve):
            def reduce_first(at, p):
                for x in range(4):
                    n, bank = at(x)
                    dve.wait_ge(ring_made, n + 1)
                    nc.vector.tensor_reduce(pm[:, x // 2, p, x % 2:x % 2 + 1], bank[:, :], AX.X,
                                            ALU.max).then_inc(ring_read, 1)

            def largest(i, c, n):
                u = 3 * i + c
                dve.wait_ge(ring_read, n)
                nc.vector.tensor_reduce(mx[:, :].rearrange("p (h q) -> p h q", h=2), pm[:, :, :, :], AX.X,
                                        ALU.max).then_inc(mx_ready, 1)
                dve.wait_ge(mx_ready, u + 1)

            def negatives(i, c, where, first_one):
                u = 3 * i + c
                n, bank = where
                dve.wait_ge(ring_made, n + 1)
                if not first_one:
                    dve.wait_ge(rows_in[(c - 1) % NB], (i + (c - 1) // NB + 1) * 32)
                nc.vector.tensor_scalar(nhi[:, :], bank[0:2 * KT, 0:P], -1.0, None, ALU.mult).then_inc(nhi_ready, 1)
                dve.wait_ge(nhi_ready, u + 1)
                nc.vector.scalar_tensor_tensor(out=nlo[:, :], in0=bank[0:2 * KT, 0:P], scalar=-1.0,
                                               in1=nhi[:, :].bitcast(F32), op0=ALU.mult,
                                               op1=ALU.subtract).then_inc(ring_read, 1)

            def divide(i, c, where, first_ones=False):
                u = 3 * i + c
                n, bank = where
                link = Chain(dve, out_chain, u, 2)
                dve.wait_ge(ring_made, n + 1)
                if not first_ones:
                    dve.wait_ge(ring_read, n)
                out = bank[:, :].rearrange("p (j s c) -> p j s c", j=K4, s=4)
                link(nc.vector.reciprocal(rsum[:, :].rearrange("p (j s) -> p j s", s=4), out[:, :, :, DH]))
                inv = rsum[:, :].rearrange("p (j h q) -> p j h q", j=K4, h=2)
                if not first_ones:
                    dve.wait_ge(heads_out[c % NB], (i + c // NB) * 16)
                for q in range(2):
                    dst = heads[c % NB][:, q * K4:(q + 1) * K4, :].rearrange("p k (h d) -> p k h d", h=2)
                    ins = nc.vector.tensor_tensor(dst, out[:, :, q::2, 0:DH],
                                                  inv[:, :, :, q:q + 1].broadcast_to([P, K4, 2, DH]), ALU.mult)
                    if q == 0:
                        link(ins)
                    else:
                        ins.then_inc(ring_read, 1)
                link.close()

            def step(i, c, inner=False):
                u = 3 * i + c
                for k in range(KT):
                    p = k + LEAD
                    n = 1 if p < KT else 2
                    if inner or u + n < U:
                        reduce_first(lambda x, k=k: place(i, c, inner, ("one", k, x)), p % KT)
                    if p == KT - 1 and (inner or u + 1 < U):
                        largest(i, c + 1, place(i, c, inner, ("one", k, 3))[0] + 1)
                    if p == KT and (inner or u + 1 < U):
                        negatives(i, c + 1, place(i, c, inner, "max"), False)
                    if k == 2 and (inner or u >= 1):
                        divide(i, c - 1, place(i, c, inner, "out"), not inner and u <= NB)

            for p in range(KT):
                reduce_first(lambda x, p=p: (4 * p + x, ring[(4 * p + x) % 3]), p)
            largest(0, 0, 4 * KT)
            negatives(0, 0, (4 * KT, ring[4 * KT % 3]), True)
            for p in range(LEAD):
                reduce_first(lambda x, p=p: (4 * (KT + p) + 1 + x, ring[(4 * (KT + p) + 1 + x) % 3]), p)
            steady(dve, step, 1)

        @block.tensor
        def _(pe):
            pe.wait_ge(ident_in, 16)
            pe.wait_ge(ones_set, NB)

            def free(n):
                pe.wait_ge(ring_read, n - 2)

            def first_pass(i, c, p, x, where, fresh=False):
                n, bank = where
                if p == 0 and x == 0:
                    pe.wait_ge(loaded[c % NB], (i + c // NB + 1) * 8 * 16)
                if not fresh:
                    free(n)
                h, kh = x // 2, x % 2
                nc.tensor.matmul(bank[:, :], qs[c % NB][0:R, h, p * P:(p + 1) * P],
                                 ks[c % NB][0:R, h, kh * G:(kh + 1) * G], start=True, stop=True).then_inc(ring_made, 1)

            def turn_max(i, c, where):
                n, bank = where
                pe.wait_ge(mx_ready, 3 * i + c + 1)
                free(n)
                nc.tensor.transpose(bank[0:2 * KT, 0:P], mx[:, :], ident[:, :]).then_inc(ring_made, 1)

            def second_pass(i, c, k, h, first_ones):
                u = 3 * i + c
                if k == 0 and h == 0:
                    pe.wait_ge(rows_in[c % NB], (i + c // NB + 1) * 32)
                if not first_ones:
                    pe.wait_ge(exp_done, u * 2 * KT + 2 * (k - 1) + h + 1)
                for q in range(2):
                    mm = nc.tensor.matmul(score[h][:, q * G:(q + 1) * G], ks[c % NB][:, h, k * P:(k + 1) * P],
                                          qs[c % NB][:, h, q * G:(q + 1) * G], start=True, stop=True)
                mm.then_inc(score_made, 1)

            def products(i, c, k, first_unit):
                u = 3 * i + c
                pe.wait_ge(exp_done, u * 2 * KT + 2 * k + 2)
                if k == 0:
                    pe.wait_ge(va_ready, u + 1)
                    if not first_unit:
                        pe.wait_ge(osb_ready, u)
                for s in range(4):
                    h, q = s // 2, s % 2
                    mm = nc.tensor.matmul(acc[32 * s:32 * s + 32, :], va[c % NB][:, k, h, :],
                                          probs[(2 * k + h) % 4][:, q * G:(q + 1) * G],
                                          start=k == 0, stop=k == KT - 1)
                mm.then_inc(pv_done, 1)

            def turn_out(i, c, where):
                n, bank = where
                pe.wait_ge(osb_ready, 3 * i + c + 1)
                free(n)
                for j in range(K4):
                    mm = nc.tensor.transpose(bank[:, j * P:(j + 1) * P], osb[:, j * P:(j + 1) * P], ident[:, :])
                mm.then_inc(ring_made, 1)

            def step(i, c, inner=False):
                u = 3 * i + c
                zero = not inner and u == 0
                if not inner and u == U:
                    products(i, c - 1, KT - 1, False)
                    turn_out(i, c - 1, place(i, c, False, "out"))
                    return
                for k in range(KT):
                    p = k + LEAD
                    n = 1 if p < KT else 2
                    ahead = inner or u + n < U

                    def one(x):
                        if ahead:
                            first_pass(i, c + n, p % KT, x, place(i, c, inner, ("one", k, x)))
                    one(0)
                    second_pass(i, c, k, 0, zero and k == 0)
                    one(1)
                    second_pass(i, c, k, 1, zero and k == 0)
                    one(2)
                    if k > 0:
                        products(i, c, k - 1, zero)
                    elif not zero:
                        products(i, c - 1, KT - 1, False)
                    one(3)
                    if k == 2 and not zero:
                        turn_out(i, c - 1, place(i, c, inner, "out"))
                    if p == KT and (inner or u + 1 < U):
                        turn_max(i, c + 1, place(i, c, inner, "max"))

            for p in range(KT):
                for x in range(4):
                    first_pass(0, 0, p, x, (4 * p + x, ring[(4 * p + x) % 3]), 4 * p + x < 3)
            turn_max(0, 0, (4 * KT, ring[4 * KT % 3]))
            for p in range(LEAD):
                for x in range(4):
                    n = 4 * (KT + p) + 1 + x
                    first_pass(0, 1, p, x, (n, ring[n % 3]))
            for _ in range(4):
                nc.tensor.matmul(acc[:, :], ident[:, :], V[:, 0:2].rearrange("p u k c -> p (u k c)"), start=True, stop=True)
            steady(pe, step)


E_, HID = 8, 512
RMS_EPS = 1e-6


def ffn_experts(nc, tag, x_d, src_d, heads_d, out_d, w, res):
    NP = 2 * HID // P
    IT = E_ // 2 + 1
    with Phase(nc, tag + "_fx") as ph:
        sb, ps, sem = ph.sb, ph.ps, ph.sem
        (w2h, w2l), (w1h, w1l), (wsoh, wsol) = res["w2"], res["w1"], res["wso"]
        wsh, wsl = sb("wsh", [P, CH, 2 * HID], F32R), sb("wsl", [P, CH, 2 * HID], F32R)
        gwh, gwl = sb("gwh", [P, CH, 10], F32R), sb("gwl", [P, CH, 10], F32R)
        graw = sb("graw", [P, CH, 10])
        wo, ident = sb("wo", [P, CH, C]), sb("ident", [P, P])
        n1w, n2w = sb("n1w", [P, C]), sb("n2w", [P, C])
        gbias, lower = sb("gbias", [P, 10]), sb("lower", [P, 64])
        hh, hl = sb("hh", [P, NP, G], F32R), sb("hl", [P, NP, G], F32R)
        xh, xl = sb("xh", [P, CH, G], F32R), sb("xl", [P, CH, G], F32R)
        sa = sb("sa", [P, K4, C])
        saT, src4 = sb("saT", [P, CH, G]), sb("src4", [P, K4, C])
        y4, x1, acc = sb("y4", [P, K4, C]), sb("x1", [P, K4, C]), sb("acc", [P, K4, C])
        x4 = sb("x4", [P, K4, C])
        linear = sb("linear", [P, 2, G])
        th, tt, v = sb("th", [P, 2, G]), sb("tt", [P, G]), sb("v", [P, 2, G])
        sq = sb("sq", [P, C])
        ss1, ms1, r1 = sb("ss1", [P, K4]), sb("ms1", [P, K4]), sb("r1", [P, K4])
        ss2, ms2, r2 = sb("ss2", [P, K4]), sb("ms2", [P, K4]), sb("r2", [P, K4])
        nhalf = sb("nhalf", [P, K4])
        lg = sb("lg", [P, K4, 10])
        g1 = sb("g1", [P, K4])
        gd, eg, mask, pen = sb("gd", [P, K4, 2]), sb("eg", [P, K4, 2]), sb("mask", [P, K4, 2]), sb("pen", [P, K4, 2])
        gprob = sb("gprob", [P, K4])
        el, pe_ = sb("el", [P, K4, E_]), sb("pe", [P, K4, E_])
        beat, tie = sb("beat", [P, K4, 64]), sb("tie", [P, K4, 64])
        wt = sb("wt", [P, K4, E_])
        tp = ps("tp", [P, CH, G])
        hp = [ps(f"hp{i}", [P, 2, G]) for i in range(2)]
        ex = [ps(f"ex{i}", [P, G]) for i in range(2)]

        weights_in, raw_in, consts = sem("weights_in"), sem("raw_in"), sem("consts")
        ws_hi, ws_lo = sem("ws_hi"), sem("ws_lo")
        sa_in, src_in, x_in, out_done = sem("sa_in"), sem("src_in"), sem("x_in"), sem("out_done")
        sa_turned, saT_ready, wo_made, y_ready = sem("sa_turned"), sem("saT_ready"), sem("wo_made"), sem("y_ready")
        ss1_ready, ms1_ready, r1_ready, x1_ready = sem("ss1_ready"), sem("ms1_ready"), sem("r1_ready"), sem("x1_ready")
        x1_turned, xh_ready, xl_ready = sem("x1_turned"), sem("xh_ready"), sem("xl_ready")
        gate_made, gate_chain, gexp = sem("gate_made"), sem("gate_chain"), sem("gexp")
        pair_made, tanh_ready, pair_chain = sem("pair_made"), sem("tanh_ready"), sem("pair_chain")
        out_added, linear_ready = sem("out_added"), sem("linear_ready")
        hh_ready, hl_ready = sem("hh_ready"), sem("hl_ready")
        acc_set, ex_made, ex_chain = sem("acc_set"), sem("ex_made"), sem("ex_chain")
        ss2_ready, ms2_ready, r2_ready, out_chain = sem("ss2_ready"), sem("ms2_ready"), sem("r2_ready"), sem("out_chain")
        NWD = 7
        GATE = 24
        EXC = K4 * (1 + E_)

        block = ph.ctx.enter_context(nc.Block())

        def steps(eng, step):
            step(0, True, False)
            with eng.Fori(1, NG) as s:
                step(s, False, False)
            step(NG, False, True)

        @block.sync
        def _(sp):
            sp.dma_start(x4[:, :, :].rearrange("p a b -> p (a b)"),
                         w["wsi"][:, 0:1, :].rearrange("p a b -> p (a b)")).then_inc(raw_in, 16)
            sp.dma_start(y4[:, :, :].rearrange("p a b -> p (a b)"),
                         w["wsi"][:, 1:2, :].rearrange("p a b -> p (a b)")).then_inc(raw_in, 16)
            sp.dma_start(graw[:, :, :], w["wgate"]).then_inc(raw_in, 16)
            for dst, a in ((ident, w["ident"]), (wo, w["wo"].rearrange("(h p) f -> p h f", p=P)),
                           (n1w, w["n1w"].broadcast_to([P, C])), (n2w, w["n2w"].broadcast_to([P, C])),
                           (gbias[:, 0:2], w["gbias"].broadcast_to([P, 2])),
                           (gbias[:, 2:10], w["ebias"].broadcast_to([P, 8])),
                           (lower, w["lower"].broadcast_to([P, 64]))):
                sp.dma_start(dst[:], a).then_inc(weights_in, 16)

            def load_front(b, half, first):
                g = 2 * b + half
                if not first:
                    sp.wait_ge(sa_turned, g)
                for k in range(K4):
                    sp.dma_start(sa[:, k].rearrange("p (u c) -> p u c", u=8),
                                 heads_d[:, bass.ds(b * 8, 8), half * K4 + k, :]).then_inc(sa_in, 16)
                if not first:
                    sp.wait_ge(y_ready, 2 * g)
                sp.dma_start(src4[:, :, :], group_view(src_d, g)).then_inc(src_in, 16)

            def load_x(g, first):
                if first:
                    sp.wait_ge(ws_lo, CH)
                else:
                    sp.wait_ge(out_done, g * 16)
                sp.dma_start(x4[:, :, :], group_view(x_d, g)).then_inc(x_in, 16)

            def store(g):
                sp.wait_ge(out_added, g + 1)
                sp.dma_start(group_view(out_d, g), x4[:, :, :]).then_inc(out_done, 16)

            load_front(0, 0, True)
            load_x(0, True)
            load_front(0, 1, False)
            with sp.Fori(1, B) as b:
                load_front(b, 0, False)
                store(2 * b - 2)
                load_x(2 * b - 1, False)
                load_front(b, 1, False)
                store(2 * b - 1)
                load_x(2 * b, False)
            store(NG - 2)
            load_x(NG - 1, False)
            store(NG - 1)
            sp.wait_ge(out_done, NG * 16)

        @block.gpsimd
        def _(pool):
            nc.gpsimd.memset(nhalf[:, :], -0.5).then_inc(consts, 1)
            pool.wait_ge(consts, 1)

            def hidden_lo(s, n):
                pool.wait_ge(hh_ready, s * NP + n + 1)
                nc.gpsimd.tensor_tensor(hl[:, n], v[:, n % 2], hh[:, n].bitcast(F32), ALU.subtract).then_inc(hl_ready, 1)

            def residual(g):
                pool.wait_ge(x_in, (g + 1) * 16)
                pool.wait_ge(out_chain, (g + 1) * K4)
                nc.gpsimd.tensor_tensor(x4[:, :, :], x4[:, :, :], acc[:, :, :], ALU.add).then_inc(out_added, 1)

            def step(s, first, last):
                if not last:
                    pool.wait_ge(ms1_ready, s + 1)
                    nc.gpsimd.tensor_tensor(r1[:, :], ms1[:, :], nhalf[:, :], ALU.pow).then_inc(r1_ready, 1)
                if not first:
                    pool.wait_ge(ms2_ready, s)
                    nc.gpsimd.tensor_tensor(r2[:, :], ms2[:, :], nhalf[:, :], ALU.pow).then_inc(r2_ready, 1)
                if not last:
                    for n in range(NP):
                        hidden_lo(s, n)
                        if n == 4 and not first:
                            residual(s - 1)
                else:
                    residual(s - 1)

            steps(pool, step)

        @block.scalar
        def _(act):
            act.wait_ge(raw_in, 48)
            nc.scalar.copy(wsh[:, 0], x4[:, :, :].rearrange("p a b -> p (a b)")).then_inc(ws_hi, 1)
            nc.scalar.copy(wsh[:, 1], y4[:, :, :].rearrange("p a b -> p (a b)")).then_inc(ws_hi, 1)
            nc.scalar.copy(gwh[:, :, :], graw[:, :, :]).then_inc(ws_hi, 1)

            def pair(s, n):
                act.wait_ge(pair_made, NP * s + n + 1)
                nc.scalar.activation(th[:, n % 2], hp[(n + 1) % 2][:, 0], ACT.Tanh, scale=0.5).then_inc(tanh_ready, 1)
                nc.scalar.copy(linear[:, n % 2], hp[(n + 1) % 2][:, 1]).then_inc(linear_ready, 1)

            def hidden_hi(s, n, first):
                act.wait_ge(pair_chain, (s * NP + n + 1) * 2)
                if n == 0 and not first:
                    act.wait_ge(ex_made, s * K4 * IT)
                nc.scalar.copy(hh[:, n], v[:, n % 2]).then_inc(hh_ready, 1)

            def squares(src, ss, ready, wait, tiles=range(K4)):
                for k in tiles:
                    wait(k)
                    if k:
                        act.wait_ge(ready[0], ready[1] + k)
                    nc.scalar.activation(sq[:, :], src[:, k], ACT.Square, accum_out=ss[:, k:k + 1]).then_inc(ready[0], 1)

            def step(s, first, last):
                if not last:
                    act.wait_ge(sa_turned, s + 1)
                    if not first:
                        act.wait_ge(wo_made, s)
                    nc.scalar.copy(saT[:, :, :], tp[:, :, :]).then_inc(saT_ready, 1)
                    squares(y4, ss1, (ss1_ready, s * K4), lambda k: act.wait_ge(y_ready, 2 * s + k // 2 + 1))
                    act.wait_ge(ss1_ready, (s + 1) * K4)
                def summed(k):
                    act.wait_ge(ex_chain, (s - 1) * EXC + (k + 1) * (1 + E_))

                if not first:
                    if not last:
                        squares(acc, ss2, (ss2_ready, (s - 1) * K4), summed, range(K4 - 1))
                        act.wait_ge(ss2_ready, s * K4 - 1)
                    else:
                        squares(acc, ss2, (ss2_ready, (s - 1) * K4), summed)
                        return
                act.wait_ge(x1_turned, s + 1)
                if not first:
                    act.wait_ge(pair_made, NP * s)
                nc.scalar.copy(xh[:, :, :], tp[:, :, :]).then_inc(xh_ready, 1)
                if not first:
                    squares(acc, ss2, (ss2_ready, (s - 1) * K4), summed, (K4 - 1,))
                    act.wait_ge(ss2_ready, s * K4)
                for n in range(NP):
                    pair(s, n)
                    if n:
                        hidden_hi(s, n - 1, first)
                    if n == 1:
                        act.wait_ge(gate_chain, s * GATE + 3)
                        nc.scalar.activation(eg[:, :, :], gd[:, :, :], ACT.Exp).then_inc(gexp, 1)
                    if n == 3:
                        act.wait_ge(gate_chain, s * GATE + 14)
                        nc.scalar.activation(pe_[:, :, :], el[:, :, :], ACT.Exp).then_inc(gexp, 1)
                hidden_hi(s, NP - 1, first)

            steps(act, step)

        @block.vector
        def _(dve):
            for i, (hi, lo, raw) in enumerate(((wsh[:, 0], wsl[:, 0], x4), (wsh[:, 1], wsl[:, 1], y4))):
                dve.wait_ge(ws_hi, i + 1)
                nc.vector.tensor_tensor(lo, raw[:, :, :].rearrange("p a b -> p (a b)"), hi.bitcast(F32),
                                        ALU.subtract).then_inc(ws_lo, 1)
            dve.wait_ge(ws_hi, 3)
            nc.vector.tensor_tensor(gwl[:, :, :], graw[:, :, :], gwh[:, :, :].bitcast(F32), ALU.subtract).then_inc(ws_lo, 1)
            dve.wait_ge(ws_lo, 3)
            dve.wait_ge(weights_in, NWD * 16)

            def accumulate(link, k, g, items):
                for i in items:
                    n = k * IT + i
                    dve.wait_ge(ex_made, g * K4 * IT + n + 1)
                    bank = ex[n % 2]
                    if i == 0 and k == 0:
                        dve.wait_ge(acc_set, g + 1)
                    if i == IT - 1:
                        link(nc.vector.tensor_tensor(acc[:, k], bank[:, 0:C], acc[:, k], ALU.add))
                    else:
                        for j in range(2):
                            e = 2 * i + j
                            link(nc.vector.scalar_tensor_tensor(
                                out=acc[:, k], in0=bank[:, j * C:(j + 1) * C], scalar=wt[:, k, e:e + 1],
                                in1=acc[:, k], op0=ALU.mult, op1=ALU.add))

            def mean_square(ss, ms, ready):
                nc.vector.tensor_scalar(ms[:, :], ss[:, :], 1.0 / C, RMS_EPS, ALU.mult, ALU.add).then_inc(ready, 1)

            def bcast(a, n):
                return a.rearrange("p (k o) -> p k o", o=1).broadcast_to([P, K4, n])

            def gate(s):
                link = Chain(dve, gate_chain, s, GATE)
                dve.wait_ge(gate_made, s + 1)
                link(nc.vector.tensor_tensor(lg[:, :, :], tp[:, 0, 0:40].rearrange("p (k n) -> p k n", k=K4),
                                             gbias[:, :].rearrange("p (o n) -> p o n", o=1).broadcast_to([P, K4, 10]), ALU.add))
                link(nc.vector.tensor_reduce(g1[:, :], lg[:, :, 0:2], AX.X, ALU.max))
                link(nc.vector.tensor_tensor(gd[:, :, :], lg[:, :, 0:2], bcast(g1[:, :], 2), ALU.subtract))
                yield
                dve.wait_ge(gexp, 2 * s + 1)
                link(nc.vector.tensor_reduce(g1[:, :], eg[:, :, :], AX.X, ALU.add))
                link(nc.vector.reciprocal(g1[:, :], g1[:, :]))
                link(nc.vector.tensor_tensor(eg[:, :, :], eg[:, :, :], bcast(g1[:, :], 2), ALU.mult))
                link(nc.vector.tensor_reduce(gprob[:, :], eg[:, :, :], AX.X, ALU.max))
                link(nc.vector.tensor_tensor(mask[:, :, 0], eg[:, :, 0], eg[:, :, 1], ALU.is_ge))
                yield
                link(nc.vector.tensor_scalar(mask[:, :, 1], mask[:, :, 0], -1.0, 1.0, ALU.mult, ALU.add))
                link(nc.vector.tensor_scalar(pen[:, :, :], mask[:, :, :], -1.0, 1e30, ALU.add, ALU.mult))
                el4 = el[:, :, :].rearrange("p k (g e) -> p k g e", g=2)
                wide = [P, K4, 2, E_ // 2]
                m4, p4 = (a[:, :, :].rearrange("p k (g o) -> p k g o", o=1).broadcast_to(wide) for a in (mask, pen))
                link(nc.vector.tensor_tensor(el4, lg[:, :, 2:10].rearrange("p k (g e) -> p k g e", g=2), m4, ALU.mult))
                link(nc.vector.tensor_tensor(el4, el4, p4, ALU.add))
                link(nc.vector.tensor_reduce(g1[:, :], el[:, :, :], AX.X, ALU.max))
                link(nc.vector.tensor_tensor(el[:, :, :], el[:, :, :], bcast(g1[:, :], E_), ALU.subtract))
                yield
                dve.wait_ge(gexp, 2 * s + 2)
                link(nc.vector.tensor_reduce(g1[:, :], pe_[:, :, :], AX.X, ALU.add))
                link(nc.vector.reciprocal(g1[:, :], g1[:, :]))
                link(nc.vector.tensor_tensor(g1[:, :], g1[:, :], gprob[:, :], ALU.mult))
                link(nc.vector.tensor_tensor(pe_[:, :, :], pe_[:, :, :], bcast(g1[:, :], E_), ALU.mult))
                yield
                mine = pe_[:, :, :].rearrange("p k (e o) -> p k e o", o=1).broadcast_to([P, K4, E_, E_])
                other = pe_[:, :, :].rearrange("p k (o e) -> p k o e", o=1).broadcast_to([P, K4, E_, E_])
                b4, t4 = (a[:, :, :].rearrange("p k (e f) -> p k e f", e=E_) for a in (beat, tie))
                link.done(nc.vector.tensor_tensor(b4, other, mine, ALU.is_gt))
                link(nc.vector.tensor_tensor(t4, other, mine, ALU.is_equal))
                link(nc.vector.tensor_tensor(tie[:, :, :], tie[:, :, :],
                                             lower[:, :].rearrange("p (o n) -> p o n", o=1).broadcast_to([P, K4, 64]), ALU.mult))
                yield
                link(nc.vector.tensor_tensor(beat[:, :, :], beat[:, :, :], tie[:, :, :], ALU.add))
                link(nc.vector.tensor_reduce(wt[:, :, :], b4, AX.X, ALU.add))
                link(nc.vector.scalar_tensor_tensor(out=wt[:, :, :], in0=wt[:, :, :], scalar=2.0, in1=pe_[:, :, :],
                                                    op0=ALU.is_lt, op1=ALU.mult))
                link.close()
                yield

            def pair(s, n, first):
                link = Chain(dve, pair_chain, s * NP + n, 2)
                bank = hp[(n + 1) % 2]
                dve.wait_ge(tanh_ready, s * NP + n + 1)
                link(nc.vector.scalar_tensor_tensor(out=tt[:, :], in0=th[:, n % 2], scalar=1.0, in1=bank[:, 0],
                                                    op0=ALU.add, op1=ALU.mult))
                dve.wait_ge(linear_ready, s * NP + n + 1)
                if not (first and n < 2):
                    dve.wait_ge(hl_ready, s * NP + n - 1)
                link(nc.vector.scalar_tensor_tensor(out=v[:, n % 2], in0=tt[:, :], scalar=0.5, in1=linear[:, n % 2],
                                                    op0=ALU.mult, op1=ALU.mult))

            def output(g):
                link = Chain(dve, out_chain, g, K4)
                dve.wait_ge(r2_ready, g + 1)
                for k in range(K4):
                    link.done(nc.vector.scalar_tensor_tensor(out=acc[:, k], in0=acc[:, k], scalar=r2[:, k:k + 1],
                                                             in1=n2w[:, :], op0=ALU.mult, op1=ALU.mult))
                link.close()

            def step(s, first, last):
                ex_link = None if first else Chain(dve, ex_chain, s - 1, EXC)
                everything = range(IT)

                def experts(k, items=everything):
                    if not first:
                        accumulate(ex_link, k, s - 1, items)

                experts(0)
                experts(1)
                if not last:
                    dve.wait_ge(wo_made, s + 1)
                    dve.wait_ge(src_in, (s + 1) * 16)
                    for j in range(2):
                        nc.vector.tensor_tensor(y4[:, 2 * j:2 * j + 2].rearrange("p k c -> p (k c)"), hp[0][:, j],
                                                src4[:, 2 * j:2 * j + 2].rearrange("p k c -> p (k c)"), ALU.add
                                                ).then_inc(y_ready, 1)
                experts(2, range(0, 2))
                if not last:
                    dve.wait_ge(ss1_ready, (s + 1) * K4)
                    mean_square(ss1, ms1, ms1_ready)
                experts(2, range(2, IT))
                if not last:
                    dve.wait_ge(r1_ready, s + 1)
                    for k in range(K4):
                        nc.vector.scalar_tensor_tensor(out=x1[:, k], in0=y4[:, k], scalar=r1[:, k:k + 1],
                                                       in1=n1w[:, :], op0=ALU.mult, op1=ALU.mult).then_inc(x1_ready, 1)
                experts(3, range(0, 3))
                if not last:
                    dve.wait_ge(xh_ready, s + 1)
                    nc.vector.tensor_tensor(xl[:, :, :], tp[:, :, :], xh[:, :, :].bitcast(F32), ALU.subtract).then_inc(xl_ready, 1)
                experts(3, range(3, IT))
                if not first:
                    dve.wait_ge(ss2_ready, s * K4)
                    mean_square(ss2, ms2, ms2_ready)
                if last:
                    output(s - 1)
                    return
                parts = gate(s)
                for n in range(NP):
                    pair(s, n, first)
                    if n != 3:
                        next(parts, None)
                    elif not first:
                        output(s - 1)
                    if n == 6:
                        if not first:
                            dve.wait_ge(out_added, s)
                        nc.vector.tensor_copy(acc[:, :, :], x1[:, :, :]).then_inc(acc_set, 1)

            steps(dve, step)

        @block.tensor
        def _(pe):
            pe.wait_ge(weights_in, NWD * 16)

            def experts(g, k, items=range(IT)):
                t = slice(k * P, (k + 1) * P)
                for i in items:
                    n = k * IT + i
                    if n >= 2:
                        m = n - 2
                        pe.wait_ge(ex_chain, g * EXC + (m // IT) * (1 + E_) + min(2 * (m % IT + 1), 1 + E_))
                    if i == IT - 1 and k == 0:
                        pe.wait_ge(hl_ready, (g + 1) * NP)
                    out = ex[n % 2][:, 0:C] if i == IT - 1 else ex[n % 2][:, :]
                    for kc in range(HID // P):
                        if i == IT - 1:
                            c, wh, wl = kc + HID // P, wsoh[:, kc], wsol[:, kc]
                        else:
                            c, wh, wl = kc, w2h[:, kc, i * G:(i + 1) * G], w2l[:, kc, i * G:(i + 1) * G]
                        for j, (a, r) in enumerate(((hh, wh), (hh, wl), (hl, wh))):
                            mm = nc.tensor.matmul(out, a[:, c, t], r, start=kc == 0 and j == 0,
                                                  stop=kc == HID // P - 1 and j == 2)
                    mm.then_inc(ex_made, 1)

            def turn_sa(s, first):
                pe.wait_ge(sa_in, (s + 1) * K4 * 16)
                if not first:
                    pe.wait_ge(gate_chain, (s - 1) * GATE + 1)
                for k in range(K4):
                    for h in range(CH):
                        mm = nc.tensor.transpose(tp[:, h, k * P:(k + 1) * P],
                                                 sa[:, k, h * P:(h + 1) * P], ident[:, :])
                mm.then_inc(sa_turned, 1)

            def project(s, first):
                pe.wait_ge(saT_ready, s + 1)
                if not first:
                    pe.wait_ge(pair_chain, s * NP * 2)
                for k in range(K4):
                    for h in range(CH):
                        mm = nc.tensor.matmul(hp[0][:, k // 2, (k % 2) * C:(k % 2 + 1) * C], saT[:, h, k * P:(k + 1) * P],
                                              wo[:, h, :], start=h == 0, stop=h == CH - 1)
                mm.then_inc(wo_made, 1)

            def turn_x1(s):
                pe.wait_ge(x1_ready, (s + 1) * K4)
                for k in range(K4):
                    for h in range(CH):
                        mm = nc.tensor.transpose(tp[:, h, k * P:(k + 1) * P], x1[:, k, h * P:(h + 1) * P], ident[:, :])
                mm.then_inc(x1_turned, 1)

            def gate(s):
                pe.wait_ge(xl_ready, s + 1)
                for k in range(K4):
                    t = slice(k * P, (k + 1) * P)
                    for h in range(CH):
                        for j, (a, r) in enumerate(((xh, gwh), (xh, gwl), (xl, gwh), (xl, gwl))):
                            mm = nc.tensor.matmul(tp[:, 0, k * 10:(k + 1) * 10], a[:, h, t], r[:, h, :],
                                                  start=h == 0 and j == 0, stop=h == CH - 1 and j == 3)
                mm.then_inc(gate_made, 1)

            def pair(s, n, first):
                if n == 1:
                    pe.wait_ge(y_ready, 2 * (s + 1))
                elif n > 1 or not first:
                    pe.wait_ge(linear_ready, s * NP + n - 1)
                    pe.wait_ge(pair_chain, (s * NP + n - 2) * 2 + 1)
                wh, wl = (w1h, w1l) if n < NP // 2 else (wsh, wsl)
                m = n % (NP // 2)
                for j in range(2):
                    f = slice(j * HID + m * P, j * HID + (m + 1) * P)
                    for h in range(CH):
                        for i, (a, x) in enumerate(((wh, xh), (wh, xl), (wl, xh))):
                            mm = nc.tensor.matmul(hp[(n + 1) % 2][:, j], a[:, h, f], x[:, h], start=h == 0 and i == 0,
                                                  stop=h == CH - 1 and i == 2)
                mm.then_inc(pair_made, 1)

            def step(s, first, last):
                if not last:
                    turn_sa(s, first)
                if not first:
                    pe.wait_ge(hl_ready, s * NP - NP // 2)
                    experts(s - 1, 0)
                if not first:
                    experts(s - 1, 1)
                if not last:
                    project(s, first)
                if not first:
                    experts(s - 1, 2)
                    experts(s - 1, 3, range(0, 3))
                if not last:
                    turn_x1(s)
                if not first:
                    experts(s - 1, 3, range(3, IT))
                if last:
                    return
                if first:
                    pe.wait_ge(ws_lo, 3)
                gate(s)
                for n in range(NP):
                    pair(s, n, first)

            steps(pe, step)


def relative_attention(nc, x_d, out_d, w):
    H, FE = 8, 128
    NJ = T // P
    FW = H * FE
    PAIRS = [(i, k) for k in range(B) for i in range(k + 1)]
    NPROD = 5
    SCALE = 1.0 / C ** 0.5
    with Phase(nc, "ra") as ph:
        sb, ps, sem = ph.sb, ph.ps, ph.sem
        x4, xf = sb("x4", [P, B, C]), sb("xf", [P, B, C])
        stats, mv = sb("stats", [P, K4, 6]), sb("mv", [P, K4, 2])
        var, rstd, nhalf = sb("var", [P, K4]), sb("rstd", [P, K4]), sb("nhalf", [P, K4])
        h0, h1, h = sb("h0", [P, B, C]), sb("h1", [P, B, C]), sb("h", [P, B, C])
        ident, gamma, beta, bout = sb("ident", [P, P]), sb("gamma", [P, C]), sb("beta", [P, C]), sb("bout", [P, C])
        wqh, wql = sb("wqh", [P, CH, FW], F32R), sb("wql", [P, CH, FW], F32R)
        wvh, wvl = sb("wvh", [P, CH, FW], F32R), sb("wvl", [P, CH, FW], F32R)
        woh, wol = sb("woh", [P, H, C], F32R), sb("wol", [P, H, C], F32R)
        w5, w5h, w5l = sb("w5", [P, CH, H * 5]), sb("w5h", [P, CH, H * 5], F32R), sb("w5l", [P, CH, H * 5], F32R)
        pe_t, r5, ub, vb = sb("pe_t", [P, CH, B]), sb("r5", [P, H, 5]), sb("ub", [P, H]), sb("vb", [P, H])
        vr, ones, vrow = sb("vr", [P, H, B]), sb("ones", [P, P]), sb("vrow", [P, H, 5])
        tril = sb("tril", [P, NJ, H])
        hTh, hTl = sb("hTh", [P, CH, G], F32R), sb("hTl", [P, CH, G], F32R)
        q, o = sb("q", [P, B, FW]), sb("o", [P, B, FW])
        v = [sb(f"v{i}", [P, B, FW]) for i in range(2)]
        second = sb("second", [P, FW])
        prod = [sb(f"prod{i}", [P, FW]) for i in range(NPROD)]
        posq = sb("posq", [P, B, H, 5])
        pad = sb("pad", [P, 5 * B, H])
        dots, sc = sb("dots", [P, B * B, H]), sb("sc", [P, B * B, H])
        mx = sb("mx", [P, B, H])
        oTh = [sb(f"oTh{i}", [P, H, P], F32R) for i in range(2)]
        oTl = [sb(f"oTl{i}", [P, H, P], F32R) for i in range(2)]
        tp = ps("tp", [P, 1024])
        ring = [ps(f"ring{i}", [P, FW]) for i in range(2)]
        pos_ps, out_ps = ps("pos", [P, B, H * 5]), ps("out", [P, C])

        weights_in, consts = sem("weights_in"), sem("consts")
        raw_in = [sem(f"raw_in{n}") for n in range(5)]
        split_hi, split_lo = sem("split_hi"), sem("split_lo")
        prep_pe, prep = sem("prep_pe"), sem("prep")
        x_in, xf_in, stored = sem("x_in"), sem("xf_in"), sem("stored")
        ln1_chain, ln2_chain, var_ready, rstd_ready = sem("ln1_chain"), sem("ln2_chain"), sem("var_ready"), sem("rstd_ready")
        var2_ready, rstd2_ready = sem("var2_ready"), sem("rstd2_ready")
        h_ready, turned, hTh_ready, hTl_ready = sem("h_ready"), sem("turned"), sem("hTh_ready"), sem("hTl_ready")
        q_made, q_ready, v_made, v_ready, pos_made = sem("q_made"), sem("q_ready"), sem("v_made"), sem("v_ready"), sem("pos_made")
        prod_ready, dot_ready, soft_chain, exp_ready = sem("prod_ready"), sem("dot_ready"), sem("soft_chain"), sem("exp_ready")
        o_begun, o_joined = sem("o_begun"), sem("o_joined")
        o_chain, o_turned, oTh_ready, oTl_ready = sem("o_chain"), sem("o_turned"), sem("oTh_ready"), sem("oTl_ready")
        out_made, final_chain = sem("out_made"), sem("final_chain")
        ND = len(PAIRS)
        SOFT = 15
        AT_EXP = 12
        OC = ((B - 1) + (B - 1) * (B - 2)) * H

        block = ph.ctx.enter_context(nc.Block())

        def rows(dram, j):
            return dram.rearrange("(b t) c -> t b c", b=B)[bass.ds(j * P, P)]

        def flat(a):
            return a.rearrange("p a b -> p (a b)")

        def steps(eng, step):
            step(0, 0, True, True, True)
            step(1, 1, False, True, True)
            with eng.Fori(1, NJ // 2 - 1) as half:
                for i in range(2):
                    step(2 * half + i, i, False, True, True)
            step(NJ - 2, 0, False, True, False)
            step(NJ - 1, 1, False, False, False)

        raws = [(w["b_wq"], wqh, wql, q), (w["b_wv"], wvh, wvl, v[0]), (w["b_wout"], woh, wol, o)]

        @block.sync
        def _(sp):
            def load(j):
                sp.dma_start(x4[:, :, :], rows(x_d, j)).then_inc(x_in, 16)

            load(0)
            for dst, a in ((ident, w["ident"]), (gamma, w["gamma"].broadcast_to([P, C])),
                           (beta, w["beta"].broadcast_to([P, C])), (bout, w["bout"].broadcast_to([P, C])),
                           (pe_t, w["pe_t"]), (ub, w["u_t"]), (vb, w["v_t"]), (tril, w["tril"])):
                sp.dma_start(dst[:], a).then_inc(weights_in, 16)
            for n, (src, dst) in ((0, (w["b_wq"], q[:, 0:2, :])), (3, (w["b_wr"], v[1][:, 0:2, :])),
                                  (4, (w["b_wqt"], v[1][:, 2:4, :])), (1, (w["b_wv"], v[0][:, 0:2, :])),
                                  (2, (w["b_wout"], o[:, 0:2, :]))):
                sp.dma_start(flat(dst), flat(src)).then_inc(raw_in[n], 16)
            sp.wait_ge(ln1_chain, LN_LINKS)
            load(1)

            def step(j, par, first, more, more2):
                if not first:
                    sp.wait_ge(stored, j * 16)
                sp.dma_start(xf[:, :, :], rows(x_d, j)).then_inc(xf_in, 16)
                if more2:
                    sp.wait_ge(ln1_chain, (j + 2) * LN_LINKS)
                    load(j + 2)
                sp.wait_ge(final_chain, (j + 1) * (B + 1))
                sp.dma_start(rows(out_d, j), xf[:, :, :]).then_inc(stored, 16)

            steps(sp, step)
            sp.wait_ge(stored, NJ * 16)

        @block.gpsimd
        def _(pool):
            nc.gpsimd.memset(nhalf[:, :], -0.5).then_inc(consts, 1)
            nc.gpsimd.memset(ones[:, :], 1.0).then_inc(consts, 1)
            pool.wait_ge(consts, 2)
            nc.gpsimd.memset(pad[:, :, :], 0.0).then_inc(consts, 1)
            pool.wait_ge(weights_in, 8 * 16)

            def powers(j):
                pool.wait_ge(var_ready, j + 1)
                nc.gpsimd.tensor_tensor(rstd[:, :], var[:, :], nhalf[:, :], ALU.pow).then_inc(rstd_ready, 1)
                pool.wait_ge(var2_ready, j + 1)
                nc.gpsimd.tensor_tensor(rstd[:, :], var[:, :], nhalf[:, :], ALU.pow).then_inc(rstd2_ready, 1)

            def scale(j, first):
                pool.wait_ge(ln2_chain, (j + 1) * LN_LINKS)
                if not first:
                    pool.wait_ge(turned, j)
                for n, (par, op) in enumerate(((gamma, ALU.mult), (beta, ALU.add))):
                    nc.gpsimd.tensor_tensor(h[:, :, :], h1[:, :, :] if n == 0 else h[:, :, :],
                                            par[:, :].rearrange("p (o c) -> p o c", o=1).broadcast_to([P, B, C]),
                                            op).then_inc(h_ready, 1)
                    pool.wait_ge(h_ready, 2 * j + n + 1)

            def products(j, first, items=range(ND)):
                for n in items:
                    i, k = PAIRS[n]
                    if i == 0:
                        pool.wait_ge(q_ready, j * B + k + 1)
                    if not (first and n < NPROD):
                        pool.wait_ge(dot_ready, j * ND + n - NPROD + 1)
                    nc.gpsimd.tensor_tensor(prod[n % NPROD][:, :], q[:, i], q[:, k], ALU.mult).then_inc(prod_ready, 1)

            def join(j, i):
                pool.wait_ge(o_begun, j * B + i + 1)
                nc.gpsimd.tensor_tensor(o[:, i], o[:, i], second[:, :], ALU.add).then_inc(o_joined, 1)

            powers(0)
            scale(0, True)
            powers(1)
            scale(1, False)
            products(0, True)

            def step(j, par, first, more, more2):
                if more2:
                    powers(j + 2)
                for i in range(1, B):
                    join(j, i)
                    if more:
                        products(j + 1, False, ((0, 1), (2, 3), (4,))[i - 1])
                if more2:
                    scale(j + 2, False)
                if more:
                    products(j + 1, False, range(NPROD, ND))

            steps(pool, step)

        @block.scalar
        def _(act):
            def high(n):
                _, hi, _, stage = raws[n]
                act.wait_ge(raw_in[n], 16)
                nc.scalar.copy(flat(hi[:, :, :]), flat(stage[:, 0:2, :])).then_inc(split_hi, 1)

            def turned_in(j, first):
                act.wait_ge(turned, j + 1)
                if not first:
                    act.wait_ge(v_made, j * B)
                nc.scalar.copy(flat(hTh[:, :, :]), tp[:, :]).then_inc(hTh_ready, 1)

            def take(j, made, ready, dst, free, batches=range(B)):
                for b in batches:
                    act.wait_ge(made, j * B + b + 1)
                    if b == 0 and free:
                        act.wait_ge(*free)
                    nc.scalar.copy(dst[:, b], ring[b % 2][:, :]).then_inc(ready, 1)

            def begin(j, par, i, first):
                if i == 0:
                    act.wait_ge(soft_chain, (j + 1) * SOFT)
                    act.wait_ge(v_ready, (j + 1) * B)
                if not first:
                    act.wait_ge(o_turned, (j - 1) * B + i + 1)
                if i > 1:
                    act.wait_ge(o_joined, j * (B - 1) + i - 1)
                elif i == 1 and not first:
                    act.wait_ge(o_joined, j * (B - 1))
                for k in range(2 if i else 1):
                    for n in range(H):
                        f = slice(n * FE, (n + 1) * FE)
                        ins = nc.scalar.activation(second[:, f] if k else o[:, i, f], v[par][:, k, f], ACT.Copy,
                                                   scale=sc[:, i * B + k, n:n + 1])
                ins.then_inc(o_begun, 1)

            high(0)
            turned_in(0, True)
            high(1)
            act.wait_ge(split_lo, 1)
            take(0, q_made, q_ready, q, None)
            act.wait_ge(prep, 6)
            nc.scalar.copy(flat(w5h[:, :, :]), flat(w5[:, :, :])).then_inc(split_hi, 1)
            high(2)
            act.wait_ge(split_lo, 2)
            take(0, v_made, v_ready, v[0], None)

            def step(j, par, first, more, more2):
                if more:
                    turned_in(j + 1, False)
                act.wait_ge(soft_chain, j * SOFT + AT_EXP)
                nc.scalar.activation(sc[:, :, :], sc[:, :, :], ACT.Exp, scale=SCALE).then_inc(exp_ready, 1)
                for i in range(B - 1):
                    begin(j, par, i, first)
                    if more and i < 2:
                        take(j + 1, q_made, q_ready, q, (prod_ready, (j + 1) * ND), (2 * i, 2 * i + 1))
                for b in range(B):
                    act.wait_ge(o_turned, j * B + b + 1)
                    if not (first and b < 2):
                        act.wait_ge(out_made, j * B + b - 1)
                    nc.scalar.copy(flat(oTh[b % 2][:, :, :]), tp[:, :]).then_inc(oTh_ready, 1)
                    if more:
                        take(j + 1, v_made, v_ready, v[1 - par], None if first else (o_chain, j * OC), (b,))
                    if b == 0:
                        begin(j, par, B - 1, first)

            steps(act, step)

        @block.vector
        def _(dve):
            def norms(j, first):
                dve.wait_ge(x_in, (j + 1) * 16)
                normalize_group(dve, nc, j, ln1_chain, var_ready, rstd_ready, x4, stats, mv, var, rstd, h0)
                if not first:
                    dve.wait_ge(h_ready, 2 * j)
                normalize_group(dve, nc, j, ln2_chain, var2_ready, rstd2_ready, h0, stats, mv, var, rstd, h1)

            norms(0, True)

            dve.wait_ge(weights_in, 8 * 16)
            def turned_lo(j):
                dve.wait_ge(hTh_ready, j + 1)
                nc.vector.tensor_tensor(flat(hTl[:, :, :]), tp[:, :], flat(hTh[:, :, :]).bitcast(F32),
                                        ALU.subtract).then_inc(hTl_ready, 1)

            def dot(j, items):
                for n in items:
                    i, k = PAIRS[n]
                    dve.wait_ge(prod_ready, j * ND + n + 1)
                    nc.vector.tensor_reduce(dots[:, i * B + k], prod[n % NPROD][:, :].rearrange("p (h f) -> p h f", h=H),
                                            AX.X, ALU.add).then_inc(dot_ready, 1)

            def scores(j):
                link = Chain(dve, soft_chain, j, SOFT)
                dve.wait_ge(dot_ready, (j + 1) * ND)
                for dst, src in ((slice(4, 13, 4), slice(1, 4)), (slice(9, 14, 4), slice(6, 8)), (slice(14, 15), slice(11, 12))):
                    link.done(nc.vector.tensor_copy(dots[:, dst], dots[:, src]))
                dve.wait_ge(pos_made, j + 1)
                link(nc.vector.tensor_tensor(posq[:, :, :, :].rearrange("p b h e -> p b (h e)"), pos_ps[:, :, :],
                                             vrow[:, :, :].rearrange("p (o h) e -> p o (h e)", o=1).broadcast_to([P, B, H * 5]), ALU.add))
                pad4 = pad[:, :, :].rearrange("p (i j) h -> p i j h", i=B)
                mask = tril[:, bass.ds(j, 1), :].broadcast_to([P, B, H])
                for i in range(B):
                    ins = nc.vector.tensor_tensor(pad4[:, i, 1:5], posq[:, i, :, 0:4].rearrange("p h e -> p e h"), mask, ALU.mult)
                    link.done(ins) if i < B - 1 else link(ins)
                link(nc.vector.tensor_tensor(sc[:, :, :], dots[:, :, :], pad[:, 4:20, :], ALU.add))
                return link

            def step(j, par, first, more, more2):
                link = scores(j)
                sc4 = sc[:, :, :].rearrange("p (i k) h -> p i k h", i=B)
                over_k = sc[:, :, :].rearrange("p (i k) h -> p i h k", i=B)
                uq = posq[:, :, :, 4].rearrange("p (o k) h -> p o k h", o=1).broadcast_to([P, B, B, H])
                mxb = mx[:, :, :].rearrange("p i (o h) -> p i o h", o=1).broadcast_to([P, B, B, H])
                link(nc.vector.tensor_tensor(sc4, sc4, uq, ALU.add))
                link(nc.vector.tensor_reduce(mx[:, :, :], over_k, AX.X, ALU.max))
                link(nc.vector.tensor_tensor(sc4, sc4, mxb, ALU.subtract))
                if more:
                    turned_lo(j + 1)
                dve.wait_ge(exp_ready, j + 1)
                link(nc.vector.tensor_reduce(mx[:, :, :], over_k, AX.X, ALU.add))
                link(nc.vector.reciprocal(mx[:, :, :], mx[:, :, :]))
                link(nc.vector.tensor_tensor(sc4, sc4, mxb, ALU.mult))
                link.close()
                dve.wait_ge(v_ready, (j + 1) * B)
                dve.wait_ge(xf_in, (j + 1) * 16)
                fin = Chain(dve, final_chain, j, B + 1)
                fin(nc.vector.tensor_tensor(xf[:, :, :], xf[:, :, :],
                                            bout[:, :].rearrange("p (o c) -> p o c", o=1).broadcast_to([P, B, C]), ALU.add))
                ol = Chain(dve, o_chain, j, OC)
                for i in range(B):
                    if i == 1 and more2:
                        norms(j + 2, False)
                    if i == 0:
                        dve.wait_ge(o_begun, j * B + 1)
                    else:
                        dve.wait_ge(o_joined, j * (B - 1) + i)
                    for k in range(2 if i else 1, B):
                        for n in range(H):
                            f = slice(n * FE, (n + 1) * FE)
                            p1 = sc[:, i * B + k, n:n + 1]
                            ol.done(nc.vector.scalar_tensor_tensor(out=o[:, i, f], in0=v[par][:, k, f], scalar=p1,
                                                                   in1=o[:, i, f], op0=ALU.mult, op1=ALU.add))
                        ol.wait()
                        if more:
                            at = (i - 1) * 2 + k - 2
                            if 0 <= at < 5 and i:
                                dot(j + 1, (at,))
                    if i >= 1:
                        lo_part(j, i - 1, first)
                    if i >= 2:
                        final(j, i - 2, fin)
                ol.close()
                if more:
                    dot(j + 1, range(5, 7))
                lo_part(j, 3, first)
                final(j, 2, fin)
                if more:
                    dot(j + 1, range(7, ND))
                final(j, 3, fin)

            def lo_part(j, i, first):
                dve.wait_ge(oTh_ready, j * B + i + 1)
                nc.vector.tensor_tensor(flat(oTl[i % 2][:, :, :]), tp[:, :], flat(oTh[i % 2][:, :, :]).bitcast(F32),
                                        ALU.subtract).then_inc(oTl_ready, 1)

            def final(j, i, fin):
                dve.wait_ge(out_made, j * B + i + 1)
                fin(nc.vector.tensor_tensor(xf[:, i], xf[:, i], out_ps[:, :], ALU.add))

            link = Chain(dve, prep, 0, 8)

            def low(n, count):
                _, hi, lo, stage = raws[n]
                dve.wait_ge(split_hi, count)
                nc.vector.tensor_tensor(flat(lo[:, :, :]), flat(stage[:, 0:2, :]), flat(hi[:, :, :]).bitcast(F32),
                                        ALU.subtract).then_inc(split_lo, 1)

            low(0, 1)
            dve.wait_ge(prep_pe, 1)
            link.done(nc.vector.tensor_copy(r5[:, :, 0:4], pos_ps[:, 0, 0:32].rearrange("p (h j) -> p h j", h=H)))
            link(nc.vector.tensor_copy(r5[:, :, 4], ub[:, :]))
            link(nc.vector.tensor_tensor(vr[:, :, :], r5[:, :, 0:4],
                                         vb[:, :].rearrange("p (h o) -> p h o", o=1).broadcast_to([P, H, B]), ALU.mult))
            link(nc.vector.memset(vrow[:, :, :], 0.0))
            turned_lo(0)
            norms(1, False)
            dve.wait_ge(prep_pe, 2)
            link(nc.vector.tensor_copy(vrow[:, :, 0:4], out_ps[:, 0:32].rearrange("p (h j) -> p h j", h=H)))
            low(1, 2)
            dve.wait_ge(prep_pe, 3)
            link(nc.vector.tensor_copy(flat(w5[:, :, :]), flat(pos_ps[:, 0:CH, :])))
            dve.wait_ge(split_hi, 3)
            nc.vector.tensor_tensor(flat(w5l[:, :, :]), flat(w5[:, :, :]), flat(w5h[:, :, :]).bitcast(F32),
                                    ALU.subtract).then_inc(split_lo, 1)
            low(2, 4)
            dve.wait_ge(consts, 3)
            dot(0, range(ND))
            steps(dve, step)

        @block.tensor
        def _(pe):
            pe.wait_ge(raw_in[3], 16)
            pe.wait_ge(raw_in[4], 16)
            pe.wait_ge(weights_in, 8 * 16)
            wr, wqt = v[1][:, 0:2, :], v[1][:, 2:4, :].rearrange("p a (n c) -> p (a n) c", c=C)
            for n in range(H):
                for hf in range(CH):
                    mm = nc.tensor.matmul(pos_ps[:, 0, n * 4:(n + 1) * 4], wr[:, hf, n * FE:(n + 1) * FE], pe_t[:, hf, :],
                                          start=hf == 0, stop=hf == CH - 1)
            mm.then_inc(prep_pe, 1)
            def turn(j, free):
                pe.wait_ge(h_ready, 2 * (j + 1))
                if free:
                    pe.wait_ge(*free)
                for k in range(B):
                    for hf in range(CH):
                        mm = nc.tensor.transpose(tp[:, hf * G + k * P:hf * G + (k + 1) * P], h[:, k, hf * P:(hf + 1) * P], ident[:, :])
                mm.then_inc(turned, 1)

            def three(out, lhs, rhs, first, last):
                (lh, ll), (rh, rl) = lhs, rhs
                for n, (a, r) in enumerate(((lh, rh), (lh, rl), (ll, rh))):
                    mm = nc.tensor.matmul(out, a, r, start=first and n == 0, stop=last and n == 2)
                return mm

            def project(j, wh, wl, made, free, batches=range(B)):
                for b in batches:
                    t = slice(b * P, (b + 1) * P)
                    free(b)
                    for cc in range(2):
                        f = slice(cc * G, (cc + 1) * G)
                        for hf in range(CH):
                            mm = three(ring[b % 2][:, f], (hTh[:, hf, t], hTl[:, hf, t]), (wh[:, hf, f], wl[:, hf, f]),
                                       hf == 0, hf == CH - 1)
                    mm.then_inc(made, 1)

            def queries(j, first):
                pe.wait_ge(hTl_ready, j + 1)

                def free(b):
                    if b >= 2:
                        pe.wait_ge(q_ready, j * B + b - 1)
                    elif not first:
                        pe.wait_ge(v_ready, (j - 1) * B + b + 3)
                project(j, wqh, wql, q_made, free)

            def positions(j, first):
                if not first:
                    pe.wait_ge(soft_chain, (j - 1) * SOFT + 4)
                for b in range(B):
                    t = slice(b * P, (b + 1) * P)
                    for hf in range(CH):
                        for n, (a, r) in enumerate(((hTh, w5h), (hTh, w5l), (hTl, w5h), (hTl, w5l))):
                            mm = nc.tensor.matmul(pos_ps[:, b, :], a[:, hf, t], r[:, hf, :], start=hf == 0 and n == 0,
                                                  stop=hf == CH - 1 and n == 3)
                mm.then_inc(pos_made, 1)

            def values(j, batches=range(B)):
                def free(b):
                    if b >= 2:
                        pe.wait_ge(v_ready, j * B + b - 1)
                    else:
                        pe.wait_ge(q_ready, j * B + b + 3)
                project(j, wvh, wvl, v_made, free, batches)

            def output(j, first, more):
                for i in range(B):
                    pe.wait_ge(o_chain, j * OC + ((B - 1) + (B - 2) * i) * H)
                    if i == 0:
                        if more:
                            pe.wait_ge(hTl_ready, j + 2)
                        elif not first:
                            pe.wait_ge(oTl_ready, j * B)
                    else:
                        pe.wait_ge(oTl_ready, j * B + i)
                    for n in range(H):
                        mm = nc.tensor.transpose(tp[:, n * P:(n + 1) * P], o[:, i, n * FE:(n + 1) * FE], ident[:, :])
                    mm.then_inc(o_turned, 1)
                    if more:
                        values(j + 1, (i,))
                    if i > 0:
                        product(j, i - 1, first)
                product(j, B - 1, first)

            def product(j, i, first):
                pe.wait_ge(oTl_ready, j * B + i + 1)
                if not (first and i == 0):
                    pe.wait_ge(final_chain, j * (B + 1) + i + (0 if i == 0 else 1))
                for n in range(H):
                    mm = three(out_ps[:, :], (oTh[i % 2][:, n], oTl[i % 2][:, n]), (woh[:, n], wol[:, n]), n == 0, n == H - 1)
                mm.then_inc(out_made, 1)

            turn(0, None)
            pe.wait_ge(consts, 2)
            pe.wait_ge(prep, 3)
            nc.tensor.matmul(out_ps[:, 0:32], ones[:, :], vr[:, :, :].rearrange("p h j -> p (h j)"), start=True,
                             stop=True).then_inc(prep_pe, 1)
            pe.wait_ge(split_lo, 1)
            queries(0, True)
            for hf in range(CH):
                for n in range(H):
                    mm = nc.tensor.matmul(pos_ps[:, hf, n * 5:(n + 1) * 5], wqt[:, n, hf * P:(hf + 1) * P], r5[:, n, :],
                                          start=True, stop=True)
            mm.then_inc(prep_pe, 1)
            pe.wait_ge(split_lo, 3)
            positions(0, True)
            values(0)
            pe.wait_ge(split_lo, 4)

            def step(j, par, first, more, more2):
                if more:
                    turn(j + 1, (hTl_ready, 1) if first else (oTl_ready, j * B))
                    queries(j + 1, False)
                    positions(j + 1, False)
                output(j, first, more)

            steps(pe, step)


def transformer(nc, x_d, out_d, w):
    def scratch(name, shape):
        return nc.dram_tensor(name, shape, F32, kind="Internal").ap()

    q_d, ctx_d = scratch("lin_q", [N, C]), scratch("lin_sums", [P, B * CH, P + 8])
    src_d, qk_d, heads_d = scratch("ffn_src", [N, C]), scratch("ffn_qk", [4, N // (T // C), T]), scratch("ffn_heads", [P, 32, 8, 32])
    xa_d, xb_d, xc_d = (scratch(n, [N, C]) for n in ("after_linear", "after_ffn", "after_relative"))

    linear_keys(nc, x_d, q_d, ctx_d, w)
    linear_mix(nc, x_d, q_d, ctx_d, xa_d, w)
    feed_forward(nc, "f1", xa_d, xb_d, src_d, qk_d, heads_d, w)
    relative_attention(nc, xb_d, xc_d, w)
    feed_forward(nc, "f2", xc_d, out_d, src_d, qk_d, heads_d, w)


def feed_forward(nc, tag, x_d, out_d, src_d, qk_d, heads_d, w):
    with ExitStack() as ctx:
        parts = {name: [ctx.enter_context(nc.sbuf_tensor(f"{tag}_{name}_{half}", shape, F32R))[:, :, :] for half in ("hi", "lo")]
                 for name, shape in (("wso", [P, 4, C]), ("w1", [P, CH, 1024]), ("w2", [P, 4, 8 * C]))}
        with nc.sbuf_tensor(f"{tag}_values", [P, 32, 8, 32], F32) as V:
            ffn_project(nc, tag, x_d, src_d, qk_d, V, w)
            ffn_attend(nc, tag, qk_d, V, heads_d, w, parts)
        ffn_experts(nc, tag, x_d, src_d, heads_d, out_d, w, parts)


def lay_out(inputs):
    a = {name[3:]: np.asarray(v) for name, v in inputs.items()}

    def rows(m):
        return m.reshape(-1, P, m.shape[-1]).transpose(1, 0, 2)

    head = np.arange(P) // DH
    inv_freq = (1.0 / 10000.0 ** (np.arange(0, DH, 2, dtype=np.float32) / np.float32(DH))).astype(np.float32)
    angle = (np.arange(T, dtype=np.float32)[:, None] * inv_freq[None]).T[(np.arange(P) % DH) // 2]
    sign = np.where(np.arange(P) % 2 == 0, -1, 1)[:, None]
    partner = np.arange(C) ^ 1
    pos = np.arange(B, dtype=np.float32)[::-1, None]
    div = np.exp(np.arange(0, C, 2, dtype=np.float32) * np.float32(-math.log(10000.0) / C))
    pe = np.stack([np.sin(pos * div), np.cos(pos * div)], -1).reshape(B, C)
    token = np.arange(T).reshape(T // P, P).T
    f, g, h = "ffn_", "attn_b_", "attn_a_"
    out = dict(
        x=a["attn_a_x"].reshape(N, C), ident=np.eye(P),
        qkv=np.stack([a[h + n].T for n in ("Wq", "Wk", "Wv")]),
        qkv_bias=np.concatenate([a[h + n] for n in ("bq", "bk", "bv")])[None],
        block_mask=head[:, None] == head[None], head_mask=head[:, None] == np.arange(8)[None],
        wpt=a[h + "Wp"].T, bp=a[h + "bp"][None],
        cos=np.cos(angle), sin=np.sin(angle) * sign,
        wq=a[f + "Wq"], wqs=a[f + "Wq"][:, partner], wkc=a[f + "Wk_c"], wvc=a[f + "Wv_c"],
        wk=a[f + "Wk"], wks=a[f + "Wk"][:, partner], wv=a[f + "Wv"], wo=a[f + "Wo"],
        w2=rows(a[f + "W2_experts"].transpose(1, 0, 2).reshape(4 * P, 8 * C)),
        w1=rows(a[f + "W1_shared"]), wso=rows(a[f + "W_shared_out"]), wsi=rows(a[f + "W_shared_in"]),
        wgate=rows(np.concatenate([a[f + "Wg_gate"], a[f + "We_gate"]], 1)),
        n1w=a[f + "norm1_w"][None], n2w=a[f + "norm2_w"][None],
        gbias=a[f + "group_bias"][None], ebias=a[f + "expert_bias"][None],
        lower=np.tril(np.ones((8, 8)), -1).reshape(1, 64),
        b_wq=rows(a[g + "Wq"]), b_wv=rows(a[g + "Wv"]), b_wr=rows(a[g + "Wr"]), b_wout=rows(a[g + "Wout"]),
        b_wqt=rows(a[g + "Wq"].T), gamma=a[g + "gamma"][None], beta=a[g + "beta"][None], bout=a[g + "bout"][None],
        u_t=a[g + "u_bias"].T, v_t=a[g + "v_bias"].T, pe_t=rows(pe.T),
        tril=np.arange(8)[None, None] <= token[:, :, None],
    )
    constants = ("ident", "block_mask", "head_mask", "cos", "sin", "lower", "pe_t", "tril")
    return {n: np.ascontiguousarray(v.astype(np.float32) if n in constants else v) for n, v in out.items()}


def kernel(**inputs):
    import concourse.bacc as bacc
    from concourse.bass_utils import run_bass_kernel_spmd

    nc = bacc.Bacc("TRN2", target_bir_lowering=False, num_devices=1)
    arrays = lay_out(inputs)
    aps = {n: nc.dram_tensor(n, v.shape, mybir.dt.from_np(v.dtype), kind="ExternalInput").ap() for n, v in arrays.items()}
    out = nc.dram_tensor("out", [N, C], F32, kind="ExternalOutput").ap()
    transformer(nc, aps.pop("x"), out, aps)
    r = run_bass_kernel_spmd(nc, [arrays], core_ids=[0])
    return r.results[0]["out"].reshape(B, T, C)
```
